# Optimizing a Trainium2 kernel written in Bass

```python
import numpy as np
import jax
import jax.numpy as jnp

def _softmax(x, axis=-1):
    return jax.nn.softmax(x, axis=axis)

def _gelu(x):
    return jax.nn.gelu(x, approximate=True)

def _silu(x):
    return jax.nn.silu(x)

def _sigmoid(x):
    return jax.nn.sigmoid(x)

def _layernorm(x, axis=-1, eps=1e-05):
    m = jnp.mean(x, axis=axis, keepdims=True)
    v = jnp.var(x, axis=axis, keepdims=True)
    return (x - m) / jnp.sqrt(v + eps)

def _scatter_add(tgt, idx, src, axis=0):
    return tgt.at[idx].add(src)

def _segment_sum(src, seg, n):
    return jax.ops.segment_sum(src, seg, n)
kernel_name = 'mk_decoder_preln_d2_seqx_r8_a3bf8c'

def setup_inputs(seed: int=0):
    np.random.seed(seed)
    _w = jnp.asarray

    def _rec_inputs():
        import jax
        import jax.numpy as jnp
        _rk = jax.random.key(seed)
        x = -0.0005146 + 1 * jax.random.normal(jax.random.fold_in(_rk, 1), (2, 512, 128), jnp.float32)
        _lenS = 512 - jax.random.randint(jax.random.fold_in(_rk, 7), (2,), 0, max(1, 512 // 4) + 1, jnp.int32)
        _lenS2 = 77 - jax.random.randint(jax.random.fold_in(_rk, 8), (2,), 0, max(1, 77 // 4) + 1, jnp.int32)
        _ctx_1024P = jax.random.normal(jax.random.fold_in(_rk, 11), (2, 16, 128), jnp.float32)
        _ctx_1024c = jax.random.dirichlet(jax.random.fold_in(_rk, 511), 0.3 * jnp.ones((16,), jnp.float32), (2, 77))
        _ctx_1024t = jnp.einsum('bsk,bkd->bsd', _ctx_1024c, _ctx_1024P)
        _ctx_1024t = _ctx_1024t * jax.lax.rsqrt(jnp.mean(jnp.square(_ctx_1024t)) + 1e-12) * 0.953939
        ctx_1024 = -0.000392918 + 0.999932 * (_ctx_1024t + 0.3 * jax.random.normal(jax.random.fold_in(_rk, 611), (2, 77, 128), jnp.float32))
        return (x, ctx_1024)
    x, ctx_1024 = _rec_inputs()

    def _L0_attn_setup():
        import jax, jax.numpy as jnp
        import numpy as np
        BATCH, L, H, P = (4, 1024, 128, 32)
        EPS = 1e-06

        def _reference_tuple_inner(hidden_states, norm_weight, Lambda_re, Lambda_im, log_step, B_re, B_im, C_re, C_im, D):
            ms = jnp.mean(hidden_states * hidden_states, axis=-1, keepdims=True)
            u = hidden_states * jax.lax.rsqrt(ms + EPS) * norm_weight
            Lam = Lambda_re + 1j * Lambda_im
            dt = jnp.exp(log_step)
            Lam_bar = jnp.exp(Lam * dt)
            B_bar = ((Lam_bar - 1.0) / Lam)[:, None] * (B_re + 1j * B_im)
            Bu = jnp.einsum('blh,ph->blp', u, jnp.real(B_bar)) + 1j * jnp.einsum('blh,ph->blp', u, jnp.imag(B_bar))
            As = jnp.broadcast_to(Lam_bar.astype(Bu.dtype), Bu.shape)

            def op(e1, e2):
                a1, b1 = e1
                a2, b2 = e2
                return (a2 * a1, a2 * b1 + b2)
            _, xs = jax.lax.associative_scan(op, (As, Bu), axis=1)
            y = 2.0 * (jnp.einsum('blp,hp->blh', jnp.real(xs), C_re) - jnp.einsum('blp,hp->blh', jnp.imag(xs), C_im)) + D * u
            out = hidden_states + y
            final_state = xs[:, -1]
            return (out, final_state)
        key = jax.random.key(seed)
        ks = jax.random.split(key, 8)
        hidden_states = jax.random.normal(ks[0], (BATCH, L, H), jnp.float32)
        norm_weight = jnp.ones((H,), jnp.float32)
        Lambda_re = -0.5 * jnp.ones((P,), jnp.float32)
        Lambda_im = jnp.pi * jnp.arange(P, dtype=jnp.float32)
        log_step = jax.random.uniform(ks[1], (P,), jnp.float32) * (np.log(0.1) - np.log(0.001)) + np.log(0.001)
        B_re = jax.random.normal(ks[2], (P, H), jnp.float32) / np.sqrt(H)
        B_im = jax.random.normal(ks[3], (P, H), jnp.float32) / np.sqrt(H)
        C_re = jax.random.normal(ks[4], (H, P), jnp.float32) / np.sqrt(P)
        C_im = jax.random.normal(ks[5], (H, P), jnp.float32) / np.sqrt(P)
        D = jax.random.normal(ks[6], (H,), jnp.float32)
        return {'hidden_states': hidden_states, 'norm_weight': norm_weight, 'Lambda_re': Lambda_re, 'Lambda_im': Lambda_im, 'log_step': log_step, 'B_re': B_re, 'B_im': B_im, 'C_re': C_re, 'C_im': C_im, 'D': D}
    _L0_attn_all = _L0_attn_setup()
    _L0_attn_in = {k: v for k, v in _L0_attn_all.items() if k in ('norm_weight', 'Lambda_re', 'Lambda_im', 'log_step', 'B_re', 'B_im', 'C_re', 'C_im', 'D')}
    del _L0_attn_all

    def _L0_xattn_setup():
        import jax, jax.numpy as jnp
        import numpy as np
        DIM = 128
        DIM_HEAD = 64
        HEADS = 16
        INNER = DIM_HEAD * HEADS
        EPS = 1e-05

        def layer_norm(x, g, b):
            m = jnp.mean(x, axis=-1, keepdims=True)
            v = jnp.mean(jnp.square(x - m), axis=-1, keepdims=True)
            return (x - m) * jax.lax.rsqrt(v + EPS) * g + b
        key = jax.random.key(seed)
        ks = jax.random.split(key, 8)
        B, N_IMG, N_LAT = (4, 512, 64)
        std = 1.0 / np.sqrt(DIM)
        return {'image_embeds': jax.random.normal(ks[0], (B, N_IMG, DIM), dtype=jnp.float32), 'latents': jax.random.normal(ks[1], (B, N_LAT, DIM), dtype=jnp.float32), 'ln1_g': jnp.ones((DIM,), jnp.float32), 'ln1_b': jnp.zeros((DIM,), jnp.float32), 'ln2_g': jnp.ones((DIM,), jnp.float32), 'ln2_b': jnp.zeros((DIM,), jnp.float32), 'Wq': jax.random.normal(ks[2], (DIM, INNER), dtype=jnp.float32) * std, 'Wkv': jax.random.normal(ks[3], (DIM, 2 * INNER), dtype=jnp.float32) * std, 'Wo': jax.random.normal(ks[4], (INNER, DIM), dtype=jnp.float32) * std}
    _L0_xattn_all = _L0_xattn_setup()
    _L0_xattn_in = {k: v for k, v in _L0_xattn_all.items() if k in ('ln1_g', 'ln1_b', 'ln2_g', 'ln2_b', 'Wq', 'Wkv', 'Wo')}
    del _L0_xattn_all

    def _L0_ffn_setup():
        import jax, jax.numpy as jnp
        import numpy as np
        B, S, D_MODEL, D_HIDDEN = (4, 256, 128, 512)

        def act_quant(x):
            scale = 127.0 / jnp.clip(jnp.max(jnp.abs(x), axis=-1, keepdims=True), 1e-05)
            return jnp.clip(jnp.round(x * scale), -128, 127) / scale

        def weight_quant(w):
            scale = 1.0 / jnp.clip(jnp.mean(jnp.abs(w)), 1e-05)
            return jnp.clip(jnp.round(w * scale), -1, 1) / scale

        def bit_linear(x, w):
            xq = x + jax.lax.stop_gradient(act_quant(x) - x)
            wq = w + jax.lax.stop_gradient(weight_quant(w) - w)
            return jnp.einsum('bsd,hd->bsh', xq, wq)

        def depthwise_conv1d(x_bcl, w, b):
            y = jax.lax.conv_general_dilated(x_bcl, w, window_strides=(1,), padding=[(1, 1)], dimension_numbers=('NCH', 'OIH', 'NCH'), feature_group_count=x_bcl.shape[1])
            return y + b[None, :, None]
        key = jax.random.key(seed)
        ks = jax.random.split(key, 5)
        lim1 = 1.0 / np.sqrt(D_MODEL)
        lim2 = 1.0 / np.sqrt(D_HIDDEN)
        limc = 1.0 / np.sqrt(3.0)
        return {'x': jax.random.normal(ks[0], (B, S, D_MODEL), dtype=jnp.float32), 'w1': jax.random.uniform(ks[1], (D_HIDDEN, D_MODEL), jnp.float32, -lim1, lim1), 'conv_w': jax.random.uniform(ks[2], (D_HIDDEN, 1, 3), jnp.float32, -limc, limc), 'conv_b': jax.random.uniform(ks[3], (D_HIDDEN,), jnp.float32, -limc, limc), 'w2': jax.random.uniform(ks[4], (D_MODEL, D_HIDDEN), jnp.float32, -lim2, lim2)}
    _L0_ffn_all = _L0_ffn_setup()
    _L0_ffn_in = {k: v for k, v in _L0_ffn_all.items() if k in ('w1', 'conv_w', 'conv_b', 'w2')}
    del _L0_ffn_all

    def _L1_attn_setup():
        import jax, jax.numpy as jnp
        import numpy as np
        HIDDEN = 128
        NHEADS = 16
        HEAD_DIM = HIDDEN // NHEADS
        CONV_K = 4
        EPS = 1e-06

        def _short_conv(x, w):
            K = w.shape[-1]
            L = x.shape[1]
            xp = jnp.pad(x, ((0, 0), (K - 1, 0), (0, 0)))
            y = jnp.zeros_like(x)
            for k in range(K):
                y = y + xp[:, k:k + L, :] * w[:, k]
            return y

        def _l2norm(x):
            n = jnp.sqrt(jnp.sum(x * x, axis=-1, keepdims=True))
            return x / jnp.maximum(n, EPS)

        def _delta_rule(q, k, v, beta):
            b, h, l, dk = q.shape
            dv = v.shape[-1]
            q = q * dk ** (-0.5)
            S0 = jnp.zeros((b, h, dk, dv), dtype=v.dtype)

            def step(S, inp):
                q_t, k_t, v_t, b_t = inp
                v_new = (v_t - jnp.einsum('bhd,bhdm->bhm', k_t, S)) * b_t[..., None]
                S = S + jnp.einsum('bhd,bhm->bhdm', k_t, v_new)
                o_t = jnp.einsum('bhd,bhdm->bhm', q_t, S)
                return (S, o_t)
            ql, kl, vl = (t.transpose(2, 0, 1, 3) for t in (q, k, v))
            bl = beta.transpose(2, 0, 1)
            S, o = jax.lax.scan(step, S0, (ql, kl, vl, bl))
            return (o.transpose(1, 2, 0, 3), S)

        def _reference_tuple_inner(x, Wq, Wk, Wv, Wb, Wo, conv_q, conv_k, conv_v, o_norm_w):
            b, l, _ = x.shape
            q = x @ Wq.T
            k = x @ Wk.T
            v = x @ Wv.T
            beta = jax.nn.sigmoid(x @ Wb.T)
            q = jax.nn.silu(_short_conv(q, conv_q))
            k = jax.nn.silu(_short_conv(k, conv_k))
            v = jax.nn.silu(_short_conv(v, conv_v))

            def to_heads(t):
                return t.reshape(b, l, NHEADS, HEAD_DIM).transpose(0, 2, 1, 3)
            q, k, v = (to_heads(q), to_heads(k), to_heads(v))
            beta = beta.transpose(0, 2, 1)
            q = _l2norm(q)
            k = _l2norm(k)
            o, S = _delta_rule(q, k, v, beta)
            o = o * jax.lax.rsqrt(jnp.mean(o * o, axis=-1, keepdims=True) + EPS) * o_norm_w
            out = o.transpose(0, 2, 1, 3).reshape(b, l, HIDDEN) @ Wo.T
            return (out, S)
        key = jax.random.key(seed)
        ks = jax.random.split(key, 10)
        b, l = (4, 128)
        init = 0.02
        return {'x': jax.random.normal(ks[0], (b, l, HIDDEN), dtype=jnp.float32), 'Wq': jax.random.normal(ks[1], (HIDDEN, HIDDEN), dtype=jnp.float32) * init, 'Wk': jax.random.normal(ks[2], (HIDDEN, HIDDEN), dtype=jnp.float32) * init, 'Wv': jax.random.normal(ks[3], (HIDDEN, HIDDEN), dtype=jnp.float32) * init, 'Wb': jax.random.normal(ks[4], (NHEADS, HIDDEN), dtype=jnp.float32) * init, 'Wo': jax.random.normal(ks[5], (HIDDEN, HIDDEN), dtype=jnp.float32) * init, 'conv_q': jax.random.normal(ks[6], (HIDDEN, CONV_K), dtype=jnp.float32) * 0.3, 'conv_k': jax.random.normal(ks[7], (HIDDEN, CONV_K), dtype=jnp.float32) * 0.3, 'conv_v': jax.random.normal(ks[8], (HIDDEN, CONV_K), dtype=jnp.float32) * 0.3, 'o_norm_w': jnp.ones((HEAD_DIM,), dtype=jnp.float32)}
    _L1_attn_all = _L1_attn_setup()
    _L1_attn_in = {k: v for k, v in _L1_attn_all.items() if k in ('Wq', 'Wk', 'Wv', 'Wb', 'Wo', 'conv_q', 'conv_k', 'conv_v', 'o_norm_w')}
    del _L1_attn_all

    def _L1_xattn_setup():
        import jax, jax.numpy as jnp
        import numpy as np
        B, S, C = (8, 256, 128)
        key = jax.random.key(seed)
        ks = jax.random.split(key, 9)
        scale = 1.0 / np.sqrt(C)
        return {'x1': jax.random.normal(ks[0], (B, S, C), jnp.float32), 'x2': jax.random.normal(ks[1], (B, S, C), jnp.float32), 'x3': jax.random.normal(ks[2], (B, S, C), jnp.float32), 'Wq': jax.random.normal(ks[3], (C, C), jnp.float32) * scale, 'bq': jax.random.normal(ks[4], (C,), jnp.float32) * scale, 'Wk': jax.random.normal(ks[5], (C, C), jnp.float32) * scale, 'bk': jax.random.normal(ks[6], (C,), jnp.float32) * scale, 'Wv': jax.random.normal(ks[7], (C, C), jnp.float32) * scale, 'bv': jax.random.normal(ks[8], (C,), jnp.float32) * scale}
    _L1_xattn_all = _L1_xattn_setup()
    _L1_xattn_in = {k: v for k, v in _L1_xattn_all.items() if k in ('Wq', 'bq', 'Wk', 'bk', 'Wv', 'bv')}
    del _L1_xattn_all

    def _L1_ffn_setup():
        import jax, jax.numpy as jnp
        import numpy as np
        H = 128
        I = 256
        E = 8
        B, S = (2, 128)

        def _swiglu(x, wg, wu, wd):
            return jax.nn.silu(x @ wg) * (x @ wu) @ wd
        key = jax.random.key(seed)
        ks = jax.random.split(key, 8)
        sc_h = 1.0 / np.sqrt(H)
        sc_i = 1.0 / np.sqrt(I)
        return {'hidden_states': jax.random.normal(ks[0], (B, S, H), jnp.float32), 'gate_w': jax.random.normal(ks[1], (H, E), jnp.float32) * sc_h, 'sh_gate': jax.random.normal(ks[2], (H, I), jnp.float32) * sc_h, 'sh_up': jax.random.normal(ks[3], (H, I), jnp.float32) * sc_h, 'sh_down': jax.random.normal(ks[4], (I, H), jnp.float32) * sc_i, 'rt_gate': jax.random.normal(ks[5], (E, H, I), jnp.float32) * sc_h, 'rt_up': jax.random.normal(ks[6], (E, H, I), jnp.float32) * sc_h, 'rt_down': jax.random.normal(ks[7], (E, I, H), jnp.float32) * sc_i}
    _L1_ffn_all = _L1_ffn_setup()
    _L1_ffn_in = {k: v for k, v in _L1_ffn_all.items() if k in ('gate_w', 'sh_gate', 'sh_up', 'sh_down', 'rt_gate', 'rt_up', 'rt_down')}
    del _L1_ffn_all
    return {'x': x, 'ctx_1024': ctx_1024, 'L0_attn_norm_weight': _L0_attn_in['norm_weight'], 'L0_attn_Lambda_re': _L0_attn_in['Lambda_re'], 'L0_attn_Lambda_im': _L0_attn_in['Lambda_im'], 'L0_attn_log_step': _L0_attn_in['log_step'], 'L0_attn_B_re': _L0_attn_in['B_re'], 'L0_attn_B_im': _L0_attn_in['B_im'], 'L0_attn_C_re': _L0_attn_in['C_re'], 'L0_attn_C_im': _L0_attn_in['C_im'], 'L0_attn_D': _L0_attn_in['D'], 'L0_xattn_ln1_g': _L0_xattn_in['ln1_g'], 'L0_xattn_ln1_b': _L0_xattn_in['ln1_b'], 'L0_xattn_ln2_g': _L0_xattn_in['ln2_g'], 'L0_xattn_ln2_b': _L0_xattn_in['ln2_b'], 'L0_xattn_Wq': _L0_xattn_in['Wq'], 'L0_xattn_Wkv': _L0_xattn_in['Wkv'], 'L0_xattn_Wo': _L0_xattn_in['Wo'], 'L0_ffn_w1': _L0_ffn_in['w1'], 'L0_ffn_conv_w': _L0_ffn_in['conv_w'], 'L0_ffn_conv_b': _L0_ffn_in['conv_b'], 'L0_ffn_w2': _L0_ffn_in['w2'], 'L1_attn_Wq': _L1_attn_in['Wq'], 'L1_attn_Wk': _L1_attn_in['Wk'], 'L1_attn_Wv': _L1_attn_in['Wv'], 'L1_attn_Wb': _L1_attn_in['Wb'], 'L1_attn_Wo': _L1_attn_in['Wo'], 'L1_attn_conv_q': _L1_attn_in['conv_q'], 'L1_attn_conv_k': _L1_attn_in['conv_k'], 'L1_attn_conv_v': _L1_attn_in['conv_v'], 'L1_attn_o_norm_w': _L1_attn_in['o_norm_w'], 'L1_xattn_Wq': _L1_xattn_in['Wq'], 'L1_xattn_bq': _L1_xattn_in['bq'], 'L1_xattn_Wk': _L1_xattn_in['Wk'], 'L1_xattn_bk': _L1_xattn_in['bk'], 'L1_xattn_Wv': _L1_xattn_in['Wv'], 'L1_xattn_bv': _L1_xattn_in['bv'], 'L1_ffn_gate_w': _L1_ffn_in['gate_w'], 'L1_ffn_sh_gate': _L1_ffn_in['sh_gate'], 'L1_ffn_sh_up': _L1_ffn_in['sh_up'], 'L1_ffn_sh_down': _L1_ffn_in['sh_down'], 'L1_ffn_rt_gate': _L1_ffn_in['rt_gate'], 'L1_ffn_rt_up': _L1_ffn_in['rt_up'], 'L1_ffn_rt_down': _L1_ffn_in['rt_down']}

def reference(x, ctx_1024, L0_attn_norm_weight, L0_attn_Lambda_re, L0_attn_Lambda_im, L0_attn_log_step, L0_attn_B_re, L0_attn_B_im, L0_attn_C_re, L0_attn_C_im, L0_attn_D, L0_xattn_ln1_g, L0_xattn_ln1_b, L0_xattn_ln2_g, L0_xattn_ln2_b, L0_xattn_Wq, L0_xattn_Wkv, L0_xattn_Wo, L0_ffn_w1, L0_ffn_conv_w, L0_ffn_conv_b, L0_ffn_w2, L1_attn_Wq, L1_attn_Wk, L1_attn_Wv, L1_attn_Wb, L1_attn_Wo, L1_attn_conv_q, L1_attn_conv_k, L1_attn_conv_v, L1_attn_o_norm_w, L1_xattn_Wq, L1_xattn_bq, L1_xattn_Wk, L1_xattn_bk, L1_xattn_Wv, L1_xattn_bv, L1_ffn_gate_w, L1_ffn_sh_gate, L1_ffn_sh_up, L1_ffn_sh_down, L1_ffn_rt_gate, L1_ffn_rt_up, L1_ffn_rt_down):
    import jax
    import jax.numpy as jnp

    def _L0_attn_ref(hidden_states, norm_weight, Lambda_re, Lambda_im, log_step, B_re, B_im, C_re, C_im, D):
        import jax, jax.numpy as jnp
        import numpy as np
        BATCH, L, H, P = (4, 1024, 128, 32)
        EPS = 1e-06

        def _reference_tuple_inner(hidden_states, norm_weight, Lambda_re, Lambda_im, log_step, B_re, B_im, C_re, C_im, D):
            ms = jnp.mean(hidden_states * hidden_states, axis=-1, keepdims=True)
            u = hidden_states * jax.lax.rsqrt(ms + EPS) * norm_weight
            Lam = Lambda_re + 1j * Lambda_im
            dt = jnp.exp(log_step)
            Lam_bar = jnp.exp(Lam * dt)
            B_bar = ((Lam_bar - 1.0) / Lam)[:, None] * (B_re + 1j * B_im)
            Bu = jnp.einsum('blh,ph->blp', u, jnp.real(B_bar)) + 1j * jnp.einsum('blh,ph->blp', u, jnp.imag(B_bar))
            As = jnp.broadcast_to(Lam_bar.astype(Bu.dtype), Bu.shape)

            def op(e1, e2):
                a1, b1 = e1
                a2, b2 = e2
                return (a2 * a1, a2 * b1 + b2)
            _, xs = jax.lax.associative_scan(op, (As, Bu), axis=1)
            y = 2.0 * (jnp.einsum('blp,hp->blh', jnp.real(xs), C_re) - jnp.einsum('blp,hp->blh', jnp.imag(xs), C_im)) + D * u
            out = hidden_states + y
            final_state = xs[:, -1]
            return (out, final_state)
        return _reference_tuple_inner(hidden_states, norm_weight, Lambda_re, Lambda_im, log_step, B_re, B_im, C_re, C_im, D)[0]

    def _L0_xattn_ref(image_embeds, latents, ln1_g, ln1_b, ln2_g, ln2_b, Wq, Wkv, Wo):
        import jax, jax.numpy as jnp
        import numpy as np
        DIM = 128
        DIM_HEAD = 64
        HEADS = 16
        INNER = DIM_HEAD * HEADS
        EPS = 1e-05

        def layer_norm(x, g, b):
            m = jnp.mean(x, axis=-1, keepdims=True)
            v = jnp.mean(jnp.square(x - m), axis=-1, keepdims=True)
            return (x - m) * jax.lax.rsqrt(v + EPS) * g + b
        B, S_lat, _ = latents.shape
        x = layer_norm(image_embeds, ln1_g, ln1_b)
        l = layer_norm(latents, ln2_g, ln2_b)
        q = l @ Wq
        kv_in = jnp.concatenate([x, l], axis=1)
        kv = kv_in @ Wkv
        k, v = jnp.split(kv, 2, axis=-1)

        def to_heads(t):
            return t.reshape(t.shape[0], t.shape[1], HEADS, DIM_HEAD).transpose(0, 2, 1, 3)
        q, k, v = (to_heads(q), to_heads(k), to_heads(v))
        scale = 1.0 / np.sqrt(np.sqrt(DIM_HEAD))
        w = jnp.einsum('bhqd,bhkd->bhqk', q * scale, k * scale)
        w = jax.nn.softmax(w.astype(jnp.float32), axis=-1).astype(q.dtype)
        out = jnp.einsum('bhqk,bhkd->bhqd', w, v)
        out = out.transpose(0, 2, 1, 3).reshape(B, S_lat, INNER)
        return out @ Wo

    def _L0_ffn_ref(x, w1, conv_w, conv_b, w2):
        import jax, jax.numpy as jnp
        import numpy as np
        B, S, D_MODEL, D_HIDDEN = (4, 256, 128, 512)

        def act_quant(x):
            scale = 127.0 / jnp.clip(jnp.max(jnp.abs(x), axis=-1, keepdims=True), 1e-05)
            return jnp.clip(jnp.round(x * scale), -128, 127) / scale

        def weight_quant(w):
            scale = 1.0 / jnp.clip(jnp.mean(jnp.abs(w)), 1e-05)
            return jnp.clip(jnp.round(w * scale), -1, 1) / scale

        def bit_linear(x, w):
            xq = x + jax.lax.stop_gradient(act_quant(x) - x)
            wq = w + jax.lax.stop_gradient(weight_quant(w) - w)
            return jnp.einsum('bsd,hd->bsh', xq, wq)

        def depthwise_conv1d(x_bcl, w, b):
            y = jax.lax.conv_general_dilated(x_bcl, w, window_strides=(1,), padding=[(1, 1)], dimension_numbers=('NCH', 'OIH', 'NCH'), feature_group_count=x_bcl.shape[1])
            return y + b[None, :, None]
        h = bit_linear(x, w1)
        h = depthwise_conv1d(h.transpose(0, 2, 1), conv_w, conv_b)
        h = h.transpose(0, 2, 1)
        h = jax.nn.silu(h)
        return bit_linear(h, w2)

    def _L1_attn_ref(x, Wq, Wk, Wv, Wb, Wo, conv_q, conv_k, conv_v, o_norm_w):
        import jax, jax.numpy as jnp
        import numpy as np
        HIDDEN = 128
        NHEADS = 16
        HEAD_DIM = HIDDEN // NHEADS
        CONV_K = 4
        EPS = 1e-06

        def _short_conv(x, w):
            K = w.shape[-1]
            L = x.shape[1]
            xp = jnp.pad(x, ((0, 0), (K - 1, 0), (0, 0)))
            y = jnp.zeros_like(x)
            for k in range(K):
                y = y + xp[:, k:k + L, :] * w[:, k]
            return y

        def _l2norm(x):
            n = jnp.sqrt(jnp.sum(x * x, axis=-1, keepdims=True))
            return x / jnp.maximum(n, EPS)

        def _delta_rule(q, k, v, beta):
            b, h, l, dk = q.shape
            dv = v.shape[-1]
            q = q * dk ** (-0.5)
            S0 = jnp.zeros((b, h, dk, dv), dtype=v.dtype)

            def step(S, inp):
                q_t, k_t, v_t, b_t = inp
                v_new = (v_t - jnp.einsum('bhd,bhdm->bhm', k_t, S)) * b_t[..., None]
                S = S + jnp.einsum('bhd,bhm->bhdm', k_t, v_new)
                o_t = jnp.einsum('bhd,bhdm->bhm', q_t, S)
                return (S, o_t)
            ql, kl, vl = (t.transpose(2, 0, 1, 3) for t in (q, k, v))
            bl = beta.transpose(2, 0, 1)
            S, o = jax.lax.scan(step, S0, (ql, kl, vl, bl))
            return (o.transpose(1, 2, 0, 3), S)

        def _reference_tuple_inner(x, Wq, Wk, Wv, Wb, Wo, conv_q, conv_k, conv_v, o_norm_w):
            b, l, _ = x.shape
            q = x @ Wq.T
            k = x @ Wk.T
            v = x @ Wv.T
            beta = jax.nn.sigmoid(x @ Wb.T)
            q = jax.nn.silu(_short_conv(q, conv_q))
            k = jax.nn.silu(_short_conv(k, conv_k))
            v = jax.nn.silu(_short_conv(v, conv_v))

            def to_heads(t):
                return t.reshape(b, l, NHEADS, HEAD_DIM).transpose(0, 2, 1, 3)
            q, k, v = (to_heads(q), to_heads(k), to_heads(v))
            beta = beta.transpose(0, 2, 1)
            q = _l2norm(q)
            k = _l2norm(k)
            o, S = _delta_rule(q, k, v, beta)
            o = o * jax.lax.rsqrt(jnp.mean(o * o, axis=-1, keepdims=True) + EPS) * o_norm_w
            out = o.transpose(0, 2, 1, 3).reshape(b, l, HIDDEN) @ Wo.T
            return (out, S)
        return _reference_tuple_inner(x, Wq, Wk, Wv, Wb, Wo, conv_q, conv_k, conv_v, o_norm_w)[0]

    def _L1_xattn_ref(x1, x2, x3, Wq, bq, Wk, bk, Wv, bv):
        import jax, jax.numpy as jnp
        import numpy as np
        B, S, C = (8, 256, 128)
        q = jnp.einsum('bsc,dc->bsd', x1, Wq) + bq
        k = jnp.einsum('bsc,dc->bsd', x2, Wk) + bk
        v = jnp.einsum('bsc,dc->bsd', x3, Wv) + bv
        scores = jnp.einsum('bqd,bkd->bqk', q, k)
        attn = jax.nn.softmax(scores, axis=-1)
        return jnp.einsum('bqk,bkd->bqd', attn, v)

    def _L1_ffn_ref(hidden_states, gate_w, sh_gate, sh_up, sh_down, rt_gate, rt_up, rt_down):
        import jax, jax.numpy as jnp
        import numpy as np
        H = 128
        I = 256
        E = 8
        B, S = (2, 128)

        def _swiglu(x, wg, wu, wd):
            return jax.nn.silu(x @ wg) * (x @ wu) @ wd
        b, s, h = hidden_states.shape
        x = hidden_states.reshape(-1, h)
        logits = x @ gate_w
        top_val = jnp.max(logits, axis=-1, keepdims=True)
        top_id = jnp.argmax(logits, axis=-1)
        score = jax.nn.sigmoid(top_val)
        xs = x * score
        g = jnp.einsum('th,ehi->eti', xs, rt_gate)
        u = jnp.einsum('th,ehi->eti', xs, rt_up)
        act = jax.nn.silu(g) * u
        y = jnp.einsum('eti,eih->eth', act, rt_down)
        onehot = jax.nn.one_hot(top_id, E, dtype=x.dtype)
        routed = jnp.einsum('eth,te->th', y, onehot)
        shared = _swiglu(x, sh_gate, sh_up, sh_down)
        return (shared + routed).reshape(b, s, h)
    x = x + _L0_attn_ref(_layernorm(x, axis=-1), L0_attn_norm_weight, L0_attn_Lambda_re, L0_attn_Lambda_im, L0_attn_log_step, L0_attn_B_re, L0_attn_B_im, L0_attn_C_re, L0_attn_C_im, L0_attn_D)
    x = x + _L0_xattn_ref(ctx_1024, _layernorm(x, axis=-1), L0_xattn_ln1_g, L0_xattn_ln1_b, L0_xattn_ln2_g, L0_xattn_ln2_b, L0_xattn_Wq, L0_xattn_Wkv, L0_xattn_Wo)
    x = x + _L0_ffn_ref(_layernorm(x, axis=-1), L0_ffn_w1, L0_ffn_conv_w, L0_ffn_conv_b, L0_ffn_w2)
    x = x + _L1_attn_ref(_layernorm(x, axis=-1), L1_attn_Wq, L1_attn_Wk, L1_attn_Wv, L1_attn_Wb, L1_attn_Wo, L1_attn_conv_q, L1_attn_conv_k, L1_attn_conv_v, L1_attn_o_norm_w)
    x = x + _L1_xattn_ref(_layernorm(x, axis=-1), ctx_1024, ctx_1024, L1_xattn_Wq, L1_xattn_bq, L1_xattn_Wk, L1_xattn_bk, L1_xattn_Wv, L1_xattn_bv)
    x = x + _L1_ffn_ref(_layernorm(x, axis=-1), L1_ffn_gate_w, L1_ffn_sh_gate, L1_ffn_sh_up, L1_ffn_sh_down, L1_ffn_rt_gate, L1_ffn_rt_up, L1_ffn_rt_down)
    return x

_drawn_inputs = setup_inputs


def setup_inputs(seed=0):
    import zlib

    import numpy as np

    out = dict(_drawn_inputs(seed))
    spreads = {'L0_attn_norm_weight': (1.0, 0.2),
     'L0_attn_Lambda_re': (-0.5, 0.597),
     'L0_xattn_ln1_g': (1.0, 0.2),
     'L0_xattn_ln1_b': (0.0, 0.1),
     'L0_xattn_ln2_g': (1.0, 0.2),
     'L0_xattn_ln2_b': (0.0, 0.1),
     'L1_attn_o_norm_w': (1.0, 0.2)}
    factors = {'L1_xattn_bk': 8.0}
    for name, (base, spread) in spreads.items():
        noise = np.random.default_rng([zlib.crc32(name.encode()), seed]).standard_normal(out[name].shape)
        drawn = base * np.exp(spread * noise) if base else spread * noise
        out[name] = jnp.asarray(drawn.astype(out[name].dtype))
    for name, factor in factors.items():
        out[name] = (out[name] * factor).astype(out[name].dtype)
    return out
```

```python
from contextlib import ExitStack

import numpy as np
import concourse.bass as bass
from concourse import mybir

F32 = mybir.dt.float32
BF16 = mybir.dt.bfloat16
F32R = mybir.dt.float32r
I32 = mybir.dt.int32
ALU = mybir.AluOpType
ACT = mybir.ActivationFunctionType
AX = mybir.AxisListType

P = 128
BATCH, SEQ, CTX = 2, 512, 77
TOK = BATCH * SEQ
TILES = TOK // P
KEYS = SEQ + CTX
STATES = 32
HEADS0, DH0 = 16, 64
LN_EPS, RMS_EPS = 1e-5, 1e-6
ROUND = 12582912.0


class Chain:

    def __init__(self, engine, semaphore):
        self.engine, self.semaphore, self.count = engine, semaphore, 0

    def __call__(self, instruction):
        self.count += 1
        instruction.then_inc(self.semaphore, 1)
        self.engine.wait_ge(self.semaphore, self.count)


class Shared:

    def __init__(self, nc, ctx):
        self.nc, self.ctx, self.semaphores = nc, ctx, {}
        self.ln_count = self.uncentered = self.xn_count = 0
        self.dve = Chain(nc.vector, self.sem("vector_step"))
        self.act = Chain(nc.scalar, self.sem("scalar_step"))
        self.pool = Chain(nc.gpsimd, self.sem("gpsimd_step"))

    def sem(self, name):
        if name not in self.semaphores:
            self.semaphores[name] = self.nc.alloc_semaphore(name=name)
        return self.semaphores[name]

    def end_stage(self):
        own = [name for name in self.semaphores if not name.startswith(("ln_", "xn_ready", "vector_step",
                                                                        "scalar_step", "gpsimd_step"))]
        self.nc.clear_and_free_semaphores([self.semaphores.pop(name) for name in own])
        self.nc.all_engine_barrier()



def norm_mean(s, pe, k, source):
    n = source.shape[-1]
    s.nc.tensor.matmul(s.bank[:, k % 2, 0:n], s.mean_weights[:, :], source,
                       start=True, stop=True).then_inc(s.sem("ln_mean"), 1)


def norm_center(s, dve, k, source):
    n = source.shape[-1]
    dve.wait_ge(s.sem("ln_mean"), k - s.uncentered + 1)
    s.nc.vector.tensor_tensor(s.centered[:, k % 2, 0:n], source, s.bank[:, k % 2, 0:n],
                              ALU.subtract).then_inc(s.sem("ln_centered"), 1)


def norm_square(s, act, k, n):
    act.wait_ge(s.sem("ln_centered"), k - s.uncentered + 1)
    s.nc.scalar.activation(s.squared[:, k % 2, 0:n], s.centered[:, k % 2, 0:n],
                           ACT.Square).then_inc(s.sem("ln_squared"), 1)


def norm_variance(s, pe, k, n):
    pe.wait_ge(s.sem("ln_squared"), k + 1)
    s.nc.tensor.matmul(s.bank[:, 2 + k % 2, 0:n], s.mean_weights[:, :], s.squared[:, k % 2, 0:n],
                       start=True, stop=True).then_inc(s.sem("ln_variance"), 1)


def norm_deviation(s, act, k, n, eps):
    act.wait_ge(s.sem("ln_variance"), k + 1)
    s.nc.scalar.activation(s.deviation[:, k % 2, 0:n], s.bank[:, 2 + k % 2, 0:n], ACT.Sqrt,
                           bias=eps).then_inc(s.sem("ln_deviation"), 1)


def norm_apply(s, dve, k, n, target, gain=None, source=None):
    dve.wait_ge(s.sem("ln_deviation"), k + 1)
    s.dve(s.nc.vector.reciprocal(s.deviation[:, k % 2, 0:n], s.deviation[:, k % 2, 0:n]))
    source = s.centered[:, k % 2, 0:n] if source is None else source
    if gain is None:
        return s.nc.vector.tensor_tensor(target, source, s.deviation[:, k % 2, 0:n], ALU.mult)
    return s.nc.vector.scalar_tensor_tensor(target, source, gain, s.deviation[:, k % 2, 0:n],
                                            ALU.mult, ALU.mult)



def constants(s, block):
    nc = s.nc

    @block.gpsimd
    def _(pool):
        s.pool(nc.gpsimd.memset(s.identity[:, :], 0.0))
        s.pool(nc.gpsimd.affine_select(out=s.identity[:, :], in_=s.identity[:, :],
                                       compare_op=ALU.not_equal, fill=1.0, base=0,
                                       pattern=[[-1, P]], channel_multiplier=1))
        s.pool(nc.gpsimd.tensor_copy(s.identity16[:, :], s.identity[:, :]))
        s.pool(nc.gpsimd.memset(s.mean_weights[:, :], 1.0 / P))
        s.pool(nc.gpsimd.memset(s.ln_eps[:, :], LN_EPS))
        s.pool(nc.gpsimd.memset(s.rms_eps[:, :], RMS_EPS))



def stage_recurrence(s, i):
    nc = s.nc
    RI = 2 * STATES
    with ExitStack() as ctx:
        def sb(name, shape, dt=F32):
            return ctx.enter_context(nc.sbuf_tensor(name, shape, dt))

        x_rows = sb("x_rows", [P, TILES, P])
        b_first = sb("b_first", [P, P])
        b_second = sb("b_second", [P, P])
        b_bar = sb("b_bar", [P, P])
        b_bar_t = sb("b_bar_t", [P, P])
        c_raw = sb("c_raw", [P, 2, STATES])
        c_cos = sb("c_cos", [P, P])
        c_sin = sb("c_sin", [P, P])
        c_cos_t = sb("c_cos_t", [P, P])
        c_sin_t = sb("c_sin_t", [P, P])
        small = sb("ssm_small", [P, 48])
        power_bits = sb("power_bits", [P, 1], I32)
        series = sb("series", [P, 12, 2])
        cos_table = sb("cos_table", [P, SEQ])
        sin_table = sb("sin_table", [P, SEQ])
        turned = sb("turned", [P, SEQ])
        turned2 = sb("turned2", [P, SEQ])
        radius = sb("radius", [P, SEQ])
        state = sb("ssm_state", [P, SEQ])
        h = sb("h", [P, BATCH, SEQ])
        u = sb("u", [P, BATCH, SEQ])
        columns = {}

        def col(name):
            j = columns.setdefault(name, len(columns))
            assert j < 48
            return small[:, j:j + 1]

        loaded, params = s.sem("x_loaded"), s.sem("ssm_loaded")
        n_params = 0
        with nc.Block() as block:
            constants(s, block)

            @block.sync
            def _(sp):
                sp.dma_start(x_rows[:, :, :],
                             i["x"].rearrange("b (n p) d -> p (b n) d", p=P)).then_inc(loaded, 16)
                for part in range(4):
                    rows = slice(part * STATES, (part + 1) * STATES)
                    for name in ("Lambda_re", "Lambda_im", "log_step"):
                        sp.dma_start(col(name)[rows, :], i["L0_attn_" + name].rearrange("(p o) -> p o", o=1)
                                     ).then_inc(params, 16)
                for name in ("norm_weight", "D"):
                    sp.dma_start(col(name), i["L0_attn_" + name].rearrange("(p o) -> p o", o=1)
                                 ).then_inc(params, 16)

            @block.scalar
            def _(act):
                order = (("B_re", "B_im", "B_im", "B_re"), ("B_im", "B_re", "B_re", "B_im"))
                for target, names in zip((b_first, b_second), order):
                    for part, name in enumerate(names):
                        act.dma_start(target[part * STATES:(part + 1) * STATES, :],
                                      i["L0_attn_" + name]).then_inc(params, 16)
                for part, name in enumerate(("C_re", "C_im")):
                    act.dma_start(c_raw[:, part, :], i["L0_attn_" + name]).then_inc(params, 16)
                for b in range(BATCH):
                    for half in range(2):
                        act.wait_ge(s.sem("x_transposed"), 2 * b + half + 1)
                        nc.scalar.activation(s.x[:, b, half * 256:half * 256 + 256],
                                             s.bank[:, 4 + 2 * b + half, 0:256], ACT.Copy
                                             ).then_inc(s.sem("x_ready"), 1)
                for b in range(BATCH):
                    norm_square(s, act, b, SEQ)
                act.wait_ge(s.sem("gpsimd_step"), 6)
                for b in range(BATCH):
                    norm_deviation(s, act, b, SEQ, s.ln_eps[:, :])
                for b in range(BATCH):
                    act.wait_ge(s.sem("h_ready"), b + 1)
                    nc.scalar.activation(s.squared[:, b, :], h[:, b, :], ACT.Square
                                         ).then_inc(s.sem("ln_squared"), 1)
                for b in range(BATCH):
                    norm_deviation(s, act, 2 + b, SEQ, s.rms_eps[:, :])
                act.wait_ge(s.sem("ssm_transposed"), 3)
                for source, target in ((1, b_bar_t), (2, c_cos_t), (3, c_sin_t)):
                    ins = nc.scalar.activation(target[:, :], s.bank[:, 4 + source, 0:P], ACT.Copy)
                ins.then_inc(s.sem("ssm_weights"), 1)

            @block.vector
            def _(dve):
                v, step = nc.vector, s.dve
                for j in range(12):
                    for c in range(2):
                        fact = float(np.prod(np.arange(1.0, 2 * j + 2 - c)))
                        v.memset(series[:, j, c:c + 1], (-1.0) ** j / fact)
                sign_first, sign_second = col("sign_first"), col("sign_second")
                step(v.memset(sign_first, 1.0))
                step(v.memset(sign_second, 1.0))
                step(v.memset(sign_first[96:128, :], -1.0))
                step(v.memset(sign_second[0:32, :], -1.0))
                dve.wait_ge(params, 16 * (4 * 3 + 2 + 8 + 2))

                def exponential(out, source):
                    n, r, q = col("exp_n"), col("exp_r"), col("exp_q")
                    step(v.tensor_scalar(n, source, float(np.log2(np.e)), ROUND, ALU.mult, ALU.add))
                    step(v.tensor_scalar(n, n, ROUND, -126.0, ALU.subtract, ALU.max))
                    step(v.tensor_scalar(n, n, 127.0, None, ALU.min))
                    step(v.scalar_tensor_tensor(r, n, -0.693359375, source, ALU.mult, ALU.add))
                    step(v.scalar_tensor_tensor(r, n, 2.12194440e-4, r, ALU.mult, ALU.add))
                    fact = [float(np.prod(np.arange(1.0, j + 1))) for j in range(8)]
                    step(v.tensor_scalar(q, r, 1 / fact[7], 1 / fact[6], ALU.mult, ALU.add))
                    for j in range(5, -1, -1):
                        step(v.tensor_scalar(q, q, r, 1 / fact[j], ALU.mult, ALU.add))
                    step(v.tensor_scalar(power_bits[:, :], n, 127.0, float(2 ** 23), ALU.add, ALU.mult))
                    step(v.tensor_tensor(out, q, power_bits[:, :].bitcast(F32), ALU.mult))

                dt, decay, angle, rad = col("dt"), col("decay"), col("angle"), col("rad")
                exponential(dt, col("log_step"))
                step(v.tensor_tensor(decay, col("Lambda_re"), dt, ALU.mult))
                step(v.tensor_tensor(angle, col("Lambda_im"), dt, ALU.mult))
                exponential(rad, decay)
                turns, a, a2 = col("turns"), col("a"), col("a2")
                step(v.tensor_scalar(turns, angle, float(1 / (2 * np.pi)), ROUND, ALU.mult, ALU.add))
                step(v.tensor_scalar(turns, turns, ROUND, None, ALU.subtract))
                two_pi = 2 * np.pi
                first = 6.28125
                second = float(np.float32(np.round((two_pi - first) * 2 ** 20) / 2 ** 20))
                third = two_pi - first - second
                step(v.scalar_tensor_tensor(a, turns, -first, angle, ALU.mult, ALU.add))
                step(v.scalar_tensor_tensor(a, turns, -second, a, ALU.mult, ALU.add))
                step(v.scalar_tensor_tensor(a, turns, -third, a, ALU.mult, ALU.add))
                step(v.tensor_tensor(a2, a, a, ALU.mult))
                col("sine"), col("cosine")
                j = columns["sine"]
                both = small[:, j:j + 2]
                step(v.scalar_tensor_tensor(both, series[:, 11, :], a2, series[:, 10, :], ALU.mult, ALU.add))
                for j in range(9, -1, -1):
                    step(v.scalar_tensor_tensor(both, both, a2, series[:, j, :], ALU.mult, ALU.add))
                sine, cosine = col("sine"), col("cosine")
                step(v.tensor_tensor(sine, sine, a, ALU.mult))
                re, im = col("Lambda_re"), col("Lambda_im")
                lre, lim, norm, coef_re, coef_im, t = (
                    col(n) for n in ("lre", "lim", "norm", "coef_re", "coef_im", "t"))
                v.tensor_tensor(lim, rad, sine, ALU.mult)
                v.tensor_tensor(norm, im, im, ALU.mult)
                step(v.tensor_tensor(lre, rad, cosine, ALU.mult))
                step(v.tensor_scalar(lre, lre, 1.0, None, ALU.subtract))
                step(v.scalar_tensor_tensor(norm, re, re, norm, ALU.mult, ALU.add))
                step(v.reciprocal(norm, norm))
                step(v.tensor_tensor(t, lim, im, ALU.mult))
                step(v.scalar_tensor_tensor(coef_re, lre, re, t, ALU.mult, ALU.add))
                step(v.tensor_tensor(t, lre, im, ALU.mult))
                step(v.scalar_tensor_tensor(coef_im, lim, re, t, ALU.mult, ALU.subtract))
                step(v.tensor_scalar(coef_re, coef_re, norm, sign_first, ALU.mult, ALU.mult))
                step(v.tensor_scalar(coef_im, coef_im, norm, sign_second, ALU.mult, ALU.mult))
                step(v.tensor_scalar(b_bar[:, :], b_first[:, :], coef_re, None, ALU.mult))
                v.scalar_tensor_tensor(b_bar[:, :], b_second[:, :], coef_im, b_bar[:, :],
                                       ALU.mult, ALU.add).then_inc(s.sem("ssm_rows"), 1)
                for part, (c, cs, ss) in enumerate(((0, 2.0, -2.0), (1, -2.0, -2.0))):
                    for b in range(BATCH):
                        at = slice(b * RI + part * STATES, b * RI + (part + 1) * STATES)
                        v.tensor_scalar(c_cos[:, at], c_raw[:, c, :], cs, None, ALU.mult
                                        ).then_inc(s.sem("ssm_rows"), 1)
                        v.tensor_scalar(c_sin[:, at], c_raw[:, 1 - c, :], ss, None, ALU.mult
                                        ).then_inc(s.sem("ssm_rows"), 1)
                for b in range(BATCH):
                    dve.wait_ge(s.sem("x_ready"), 2 * b + 2)
                    norm_center(s, dve, b, s.x[:, b, :])
                ck, sk, t = cosine, sine, col("t2")
                step(v.memset(cos_table[:, 0:1], 1.0))
                step(v.memset(sin_table[:, 0:1], 0.0))
                v.memset(radius[:, :], 1.0)
                k = 1
                while k < SEQ:
                    old, new = slice(0, k), slice(k, 2 * k)
                    v.tensor_scalar(turned[:, old], sin_table[:, old], sk, None, ALU.mult)
                    step(v.tensor_scalar(turned2[:, old], cos_table[:, old], sk, None, ALU.mult))
                    v.scalar_tensor_tensor(cos_table[:, new], cos_table[:, old], ck, turned[:, old],
                                           ALU.mult, ALU.subtract)
                    step(v.scalar_tensor_tensor(sin_table[:, new], sin_table[:, old], ck, turned2[:, old],
                                                ALU.mult, ALU.add))
                    k *= 2
                    if k < SEQ:
                        step(v.tensor_tensor(t, sk, sk, ALU.mult))
                        step(v.tensor_tensor(sk, sk, ck, ALU.mult))
                        step(v.scalar_tensor_tensor(ck, ck, ck, t, ALU.mult, ALU.subtract))
                        step(v.tensor_scalar(sk, sk, 2.0, None, ALU.mult))
                step(v.tensor_scalar(radius[:, :], radius[:, :], rad, None, ALU.mult))
                for b in range(BATCH):
                    norm_apply(s, dve, b, SEQ, h[:, b, :]).then_inc(s.sem("h_ready"), 1)
                for b in range(BATCH):
                    dve.wait_ge(s.sem("h_ready"), b + 1)
                    norm_apply(s, dve, 2 + b, SEQ, u[:, b, :], gain=col("norm_weight"),
                               source=h[:, b, :]).then_inc(s.sem("u_ready"), 1)
                dve.wait_ge(s.sem("bu_ready"), 2)
                v.tensor_tensor(turned[:, :], cos_table[:, :], s.bank[:, 4, :], ALU.mult)
                step(v.tensor_tensor(turned2[:, :], sin_table[:, :], s.bank[:, 5, :], ALU.mult))
                step(v.tensor_tensor(turned[:, :], turned[:, :], turned2[:, :], ALU.add))
                step(v.tensor_tensor_scan(state[:, :], radius[:, :], turned[:, :], 0.0, ALU.mult, ALU.add))
                v.tensor_tensor(turned[:, :], cos_table[:, :], state[:, :], ALU.mult
                                ).then_inc(s.sem("state_turned"), 1)
                v.tensor_tensor(turned2[:, :], sin_table[:, :], state[:, :], ALU.mult
                                ).then_inc(s.sem("state_turned"), 1)
                for b in range(BATCH):
                    step(v.scalar_tensor_tensor(h[:, b, :], u[:, b, :], col("D"), h[:, b, :],
                                                ALU.mult, ALU.add))
                for b in range(BATCH):
                    step(v.tensor_tensor(h[:, b, :], h[:, b, :], s.x[:, b, :], ALU.add))
                for b in range(BATCH):
                    dve.wait_ge(s.sem("y_ready"), b + 1)
                    step(v.tensor_tensor(s.x[:, b, :], h[:, b, :], s.bank[:, 6 + b, :], ALU.add))

            @block.tensor
            def _(pe):
                pe.wait_ge(loaded, 16)
                pe.wait_ge(s.sem("gpsimd_step"), 6)
                for n in range(TILES):
                    ins = nc.tensor.transpose(s.bank[:, 4 + n // 2, (n % 2) * P:(n % 2 + 1) * P],
                                              x_rows[:, n, :], s.identity[:, :])
                    if n % 2:
                        ins.then_inc(s.sem("x_transposed"), 1)
                for b in range(BATCH):
                    pe.wait_ge(s.sem("x_ready"), 2 * b + 2)
                    norm_mean(s, pe, b, s.x[:, b, :])
                for b in range(BATCH):
                    norm_variance(s, pe, b, SEQ)
                pe.wait_ge(s.sem("ssm_rows"), 9)
                for slot, source in ((5, b_bar), (6, c_cos), (7, c_sin)):
                    nc.tensor.transpose(s.bank[:, slot, 0:P], source[:, :], s.identity[:, :]
                                        ).then_inc(s.sem("ssm_transposed"), 1)
                for b in range(BATCH):
                    norm_variance(s, pe, 2 + b, SEQ)
                pe.wait_ge(s.sem("ssm_weights"), 1)
                for b in range(BATCH):
                    pe.wait_ge(s.sem("u_ready"), b + 1)
                    at = slice(b * RI, (b + 1) * RI)
                    nc.tensor.matmul(s.bank[at, 4, :], b_bar_t[:, 0:RI], u[:, b, :], start=True, stop=True)
                    nc.tensor.matmul(s.bank[at, 5, :], b_bar_t[:, RI:P], u[:, b, :], start=True, stop=True
                                     ).then_inc(s.sem("bu_ready"), 1)
                pe.wait_ge(s.sem("state_turned"), 2)
                for b in range(BATCH):
                    at = slice(b * RI, (b + 1) * RI)
                    nc.tensor.matmul(s.bank[:, 6 + b, :], c_cos_t[at, :], turned[at, :], start=True, stop=False)
                    nc.tensor.matmul(s.bank[:, 6 + b, :], c_sin_t[at, :], turned2[at, :], start=False, stop=True
                                     ).then_inc(s.sem("y_ready"), 1)
        s.ln_count = 4
        s.uncentered = 2



def stage_cross_attention0(s, i):
    nc = s.nc
    PAIRS = HEADS0 // 2
    QT = SEQ // P
    KT = -(-KEYS // P)
    widths = [min(P, KEYS - kt * P) for kt in range(KT)]
    TAIL = widths[-1]
    SCALE = float(1.0 / np.sqrt(np.sqrt(DH0)))
    A, B, MAX, SCORE, OUT, ROW = 0, 1, 2, 4, 6, 7
    with ExitStack() as ctx:
        def sb(name, shape, dt=F32):
            return ctx.enter_context(nc.sbuf_tensor(name, shape, dt))

        ctx_rows = sb("ctx_rows", [CTX, BATCH, P])
        gains = sb("x0_gains", [P, 4])
        h = sb("x0_h", [P, BATCH, SEQ])
        kv = sb("kv_in", [P, BATCH, KEYS])
        wq, wk, wv = (sb(n, [P, P]) for n in ("wq_slot", "wk_slot", "wv_slot"))
        wo = sb("wo0", [P, PAIRS, P])
        q_high2 = sb("q_high2", [P, BATCH, 2, SEQ], F32R)
        q_low = sb("q_low", [DH0 + 1, BATCH, 2, SEQ], F32R)
        k_both = sb("k_both", [P, BATCH, 2, KEYS], F32R)
        k_high = sb("k_high", [DH0 + 1, BATCH, 2, KEYS], F32R)
        queries16 = sb("queries16", [DH0, BATCH, 2, SEQ], BF16)
        keys16 = sb("keys16", [DH0, BATCH, 2, KEYS], BF16)
        values = sb("values", [P, BATCH, KT, 2, DH0 + 1])
        probs = sb("probs", [P, 2, KT, SEQ])
        zero = sb("zero", [DH0, 1])
        shift = sb("shift", [P, 2, QT], BF16)
        inverse = sb("inverse", [P, QT, 1])
        attended = sb("attended", [P, BATCH, QT, P])
        attended_t = sb("attended_t", [P, PAIRS, BATCH, SEQ])
        bank, sem = s.bank, s.sem
        maxima = bank[:, MAX:MAX + 2, :].rearrange("p k n -> p (k n)")[:, 0:KEYS]
        weighted = bank[:, OUT, 0:QT * (DH0 + 1)].rearrange("p (q d) -> p q d", d=DH0 + 1)
        k0 = s.ln_count
        s.ln_count += 5

        def split(u):
            return u // 2, u // 2 % 2, u % 2

        with nc.Block() as block:
            @block.sync
            def _(sp):
                sp.dma_start(ctx_rows[:, :, :], i["ctx_1024"].rearrange("b p d -> p b d")
                             ).then_inc(sem("ctx_loaded"), 16)
                for j, name in enumerate(("ln2_g", "ln2_b", "ln1_g", "ln1_b")):
                    sp.dma_start(gains[:, j:j + 1], i["L0_xattn_" + name].rearrange("(p o) -> p o", o=1)
                                 ).then_inc(sem("gains_loaded"), 16)
                sp.dma_start(wo[:, :, :], i["L0_xattn_Wo"].rearrange("(j p) n -> p j n", p=P)
                             ).then_inc(sem("wo0_loaded"), 16)

                def load(pair):
                    cols = bass.ds(pair * P, P)
                    vcols = bass.ds(pair * P + HEADS0 * DH0, P)
                    sp.dma_start(wq[:, :], i["L0_xattn_Wq"][:, cols]).then_inc(sem("pair_loaded"), 16)
                    sp.dma_start(wk[:, :], i["L0_xattn_Wkv"][:, cols]).then_inc(sem("pair_loaded"), 16)
                    sp.dma_start(wv[:, :], i["L0_xattn_Wkv"][:, vcols]).then_inc(sem("pair_loaded"), 16)

                load(0)
                with sp.Fori(1, PAIRS) as pair:
                    sp.wait_ge(sem("v_projected"), 2 * pair)
                    load(pair)

            @block.scalar
            def _(act):
                for b in range(BATCH):
                    norm_square(s, act, k0 + b, SEQ)
                for b in range(BATCH):
                    norm_deviation(s, act, k0 + b, SEQ, s.ln_eps[:, :])
                for b in range(BATCH):
                    norm_square(s, act, k0 + 2 + b, SEQ)
                for b in range(BATCH):
                    norm_deviation(s, act, k0 + 2 + b, SEQ, s.ln_eps[:, :])
                norm_square(s, act, k0 + 4, BATCH * CTX)
                norm_deviation(s, act, k0 + 4, BATCH * CTX, s.ln_eps[:, :])

                def high_parts(semaphore, hh, targets, source):
                    for target in targets:
                        nc.scalar.activation(target, source[hh * DH0:(hh + 1) * DH0, :],
                                             ACT.Copy, scale=SCALE).then_inc(sem(semaphore), 1)

                def evacuate_q(g, b):
                    act.wait_ge(sem("q_projected"), g + 1)
                    for hh in range(2):
                        high_parts("q_ready", hh, (q_high2[0:DH0, b, hh, :], q_high2[DH0:P, b, hh, :]),
                                   bank[:, A, :])

                def evacuate_k(g, b):
                    act.wait_ge(sem("k_projected"), g + 1)
                    for hh in range(2):
                        high_parts("k_ready", hh, (k_both[0:DH0, b, hh, 0:SEQ], k_high[0:DH0, b, hh, 0:SEQ]),
                                   bank[:, B, :])

                def evacuate_tail(g, b):
                    act.wait_ge(sem("tail_projected"), g + 1)
                    for hh in range(2):
                        high_parts("k_tail_ready", hh, (k_both[0:DH0, b, hh, SEQ:KEYS],
                                                        k_high[0:DH0, b, hh, SEQ:KEYS]), bank[:, A, 0:CTX])

                def row(w, b, hh):
                    act.wait_ge(sem("shift_turned"), w + 1)
                    nc.scalar.activation(q_low[DH0:DH0 + 1, b, hh, :], bank[DH0:DH0 + 1, ROW, :],
                                         ACT.Copy).then_inc(sem("shift_ready"), 1)

                def unit(pair, u, first, last):
                    w = 4 * pair + u
                    gg, b, hh = split(u)
                    g = 2 * pair + gg
                    next_group = hh == 0 and not (last and b == 1)
                    if not (first and u < 2):
                        act.wait_ge(sem("pv_done"), w - 1)
                    for kt in range(KT):
                        act.wait_ge(sem("scored"), KT * w + kt + 1)
                        nc.scalar.activation(probs[0:widths[kt], hh, kt, :],
                                             bank[0:widths[kt], SCORE + kt % 2, :], ACT.Exp
                                             ).then_inc(sem("probs_ready"), 1)
                        if next_group and kt == 1:
                            evacuate_q(g + 1, 1 - b)
                        if next_group and kt == 2:
                            evacuate_k(g + 1, 1 - b)
                        if next_group and kt == 3:
                            evacuate_tail(g + 1, 1 - b)
                    if not (last and u == 3):
                        row(w + 1, (u + 1) // 2 % 2, 1 - hh)

                evacuate_q(0, 0)
                evacuate_k(0, 0)
                evacuate_tail(0, 0)
                row(0, 0, 0)
                for u in range(4):
                    unit(0, u, True, False)
                with act.Fori(1, PAIRS - 1) as pair:
                    for u in range(4):
                        unit(pair, u, False, False)
                for u in range(4):
                    unit(PAIRS - 1, u, False, True)

            @block.gpsimd
            def _(pool):
                s.pool(nc.gpsimd.memset(zero[:, :], 0.0))
                nc.gpsimd.memset(k_high[DH0:DH0 + 1, :, :, :].bitcast(F32), 1.0).then_inc(sem("x0_ones"), 1)
                pool.wait_ge(sem("x0_ones"), 1)
                nc.gpsimd.memset(values[:, :, :, :, DH0:DH0 + 1], 1.0).then_inc(sem("x0_ones"), 1)

                def narrow(target, source, n):
                    nc.gpsimd.tensor_tensor(target, source.bitcast(F32),
                                            zero[:, :, None].to_broadcast([DH0, 2, n]), ALU.add
                                            ).then_inc(sem("narrowed"), 1)

                def narrow_group(g, b):
                    pool.wait_ge(sem("q_ready"), 4 * g + 4)
                    narrow(queries16[:, b, :, :], q_high2[0:DH0, b, :, :], SEQ)
                    pool.wait_ge(sem("k_ready"), 4 * g + 4)
                    narrow(keys16[:, b, :, 0:SEQ], k_both[0:DH0, b, :, 0:SEQ], SEQ)
                    pool.wait_ge(sem("k_tail_ready"), 4 * g + 4)
                    narrow(keys16[:, b, :, SEQ:KEYS], k_both[0:DH0, b, :, SEQ:KEYS], CTX)

                with pool.Fori(0, PAIRS) as pair:
                    for b in range(BATCH):
                        narrow_group(2 * pair + b, b)

            @block.vector
            def _(dve):
                v, step = nc.vector, s.dve
                for b in range(BATCH):
                    norm_center(s, dve, k0 + b, s.x[:, b, :])
                for b in range(BATCH):
                    norm_apply(s, dve, k0 + b, SEQ, h[:, b, :]).then_inc(sem("x0_h"), 1)
                for b in range(BATCH):
                    norm_center(s, dve, k0 + 2 + b, h[:, b, :])
                dve.wait_ge(sem("gains_loaded"), 64)
                for b in range(BATCH):
                    step(norm_apply(s, dve, k0 + 2 + b, SEQ, kv[:, b, 0:SEQ]))
                    v.tensor_scalar(kv[:, b, 0:SEQ], kv[:, b, 0:SEQ], gains[:, 0:1], gains[:, 1:2],
                                    ALU.mult, ALU.add).then_inc(sem("kv_in_ready"), 1)
                dve.wait_ge(sem("ctx_turned"), 2)
                v.tensor_copy(s.ctx_t[:, :], bank[:, B, 0:BATCH * CTX]).then_inc(sem("ctx_ready"), 1)
                dve.wait_ge(sem("ctx_ready"), 1)
                norm_center(s, dve, k0 + 4, s.ctx_t[:, :])
                tail = kv[:, :, SEQ:KEYS]
                step(norm_apply(s, dve, k0 + 4, BATCH * CTX, h[:, 0, 0:BATCH * CTX]))
                v.tensor_scalar(tail, h[:, 0, 0:BATCH * CTX].rearrange("p (b n) -> p b n", b=BATCH),
                                gains[:, 2:3], gains[:, 3:4], ALU.mult, ALU.add
                                ).then_inc(sem("kv_in_ready"), 1)
                dve.wait_ge(sem("x0_ones"), 2)

                def maximum(w, hh, qt):
                    dve.wait_ge(sem("max_scored"), QT * w + qt + 1)
                    v.tensor_reduce(shift[:, hh, qt:qt + 1], maxima, AX.X, ALU.max, negate=True
                                    ).then_inc(sem("max_taken"), 1)

                def normalize(w, b, hh):
                    dve.wait_ge(sem("pv_done"), w + 1)
                    v.reciprocal(inverse[:, :, :], weighted[:, :, DH0:DH0 + 1]).then_inc(sem("inverse_ready"), 1)
                    dve.wait_ge(sem("inverse_ready"), w + 1)
                    v.tensor_tensor(attended[:, b, :, hh * DH0:(hh + 1) * DH0], weighted[:, :, 0:DH0],
                                    inverse[:, :, :].to_broadcast([P, QT, DH0]), ALU.mult
                                    ).then_inc(sem("normalized"), 1)

                def low_part(semaphore, target, high, source):
                    v.scalar_tensor_tensor(target, source, SCALE, high.bitcast(F32), ALU.mult, ALU.subtract
                                           ).then_inc(sem(semaphore), 1)

                def q_lows(g, b):
                    dve.wait_ge(sem("q_ready"), 4 * g + 4)
                    for hh in range(2):
                        low_part("q_low_ready", q_low[0:DH0, b, hh, :], q_high2[0:DH0, b, hh, :],
                                 bank[hh * DH0:(hh + 1) * DH0, A, :])

                def k_lows(g, b):
                    dve.wait_ge(sem("k_ready"), 4 * g + 4)
                    for hh in range(2):
                        low_part("k_low_ready", k_both[DH0:P, b, hh, 0:SEQ], k_both[0:DH0, b, hh, 0:SEQ],
                                 bank[hh * DH0:(hh + 1) * DH0, B, :])

                def tail_lows(g, b):
                    dve.wait_ge(sem("k_tail_ready"), 4 * g + 4)
                    for hh in range(2):
                        low_part("k_low_ready", k_both[DH0:P, b, hh, SEQ:KEYS], k_both[0:DH0, b, hh, SEQ:KEYS],
                                 bank[hh * DH0:(hh + 1) * DH0, A, 0:CTX])

                def value_tail(b):
                    v.tensor_copy(values[0:TAIL, b, KT - 1, :, 0:DH0],
                                  bank[0:TAIL, A, P:2 * P].rearrange("p (h d) -> p h d", h=2)
                                  ).then_inc(sem("v_tail_ready"), 1)

                def value(g, b):
                    dve.wait_ge(sem("v_projected"), g + 1)
                    v.tensor_copy(values[:, b, 0:KT - 1, :, 0:DH0].rearrange("p k h d -> p (k h) d"),
                                  bank[:, A, :].rearrange("p (k d) -> p k d", d=DH0)
                                  ).then_inc(sem("v_ready"), 1)

                def keep_turned(g, pair, b):
                    dve.wait_ge(sem("attended_turned"), g + 1)
                    v.tensor_copy(attended_t[:, pair, b, :], bank[:, B, :]).then_inc(sem("attended_kept"), 1)

                def unit(pair, u, first, last):
                    w = 4 * pair + u
                    gg, b, hh = split(u)
                    g = 2 * pair + gg
                    next_group = not (last and b == 1)
                    if not (first and u < 2):
                        normalize(w - 2, (u - 2) // 2 % 2, hh)
                    if hh == 1 and next_group:
                        value_tail(1 - b)
                    for qt in range(QT):
                        if not (last and u == 3):
                            maximum(w + 1, 1 - hh, qt)
                        if hh == 0 and qt == 0 and next_group:
                            q_lows(g + 1, 1 - b)
                        if hh == 1 and qt == 1 and not (first and b == 0):
                            keep_turned(g - 1, pair if b else pair - 1, 1 - b)
                        if hh == 1 and qt == 2 and next_group:
                            value(g + 1, 1 - b)
                    if hh == 0 and next_group:
                        k_lows(g + 1, 1 - b)
                        tail_lows(g + 1, 1 - b)

                q_lows(0, 0)
                k_lows(0, 0)
                tail_lows(0, 0)
                value_tail(0)
                value(0, 0)
                for qt in range(QT):
                    maximum(0, 0, qt)
                for u in range(4):
                    unit(0, u, True, False)
                with dve.Fori(1, PAIRS - 1) as pair:
                    for u in range(4):
                        unit(pair, u, False, False)
                for u in range(4):
                    unit(PAIRS - 1, u, False, True)
                normalize(4 * PAIRS - 2, 1, 0)
                normalize(4 * PAIRS - 1, 1, 1)
                keep_turned(2 * PAIRS - 1, PAIRS - 1, 1)
                for b in range(BATCH):
                    dve.wait_ge(sem("x0_projected"), b + 1)
                    step(v.tensor_tensor(s.x[:, b, :], s.x[:, b, :], bank[:, SCORE + b, :], ALU.add))

            @block.tensor
            def _(pe):
                mm = nc.tensor.matmul
                for b in range(BATCH):
                    norm_mean(s, pe, k0 + b, s.x[:, b, :])
                for b in range(BATCH):
                    norm_variance(s, pe, k0 + b, SEQ)
                pe.wait_ge(sem("x0_h"), 2)
                for b in range(BATCH):
                    norm_mean(s, pe, k0 + 2 + b, h[:, b, :])
                for b in range(BATCH):
                    norm_variance(s, pe, k0 + 2 + b, SEQ)
                pe.wait_ge(sem("ctx_loaded"), 16)
                pe.wait_ge(sem("kv_in_ready"), 1)
                for b in range(BATCH):
                    nc.tensor.transpose(bank[:, B, b * CTX:(b + 1) * CTX], ctx_rows[:, b, :],
                                        s.identity[0:CTX, 0:CTX]).then_inc(sem("ctx_turned"), 1)
                pe.wait_ge(sem("ctx_ready"), 1)
                norm_mean(s, pe, k0 + 4, s.ctx_t[:, :])
                norm_variance(s, pe, k0 + 4, BATCH * CTX)
                pe.wait_ge(sem("kv_in_ready"), 3)

                def project_q(pair, g, b):
                    pe.wait_ge(sem("pair_loaded"), 48 * pair + 48)
                    if not (isinstance(g, int) and g == 0):
                        pe.wait_ge(sem("v_ready"), g)
                    mm(bank[:, A, :], wq[:, :], kv[:, b, 0:SEQ], start=True, stop=True
                       ).then_inc(sem("q_projected"), 1)

                def project_k(g, b):
                    if not (isinstance(g, int) and g < 3):
                        pe.wait_ge(sem("attended_kept"), g - 2)
                    elif g:
                        pe.wait_ge(sem("k_low_ready"), 4 * g)
                    mm(bank[:, B, :], wk[:, :], kv[:, b, 0:SEQ], start=True, stop=True
                       ).then_inc(sem("k_projected"), 1)

                def project_tail(g, b):
                    pe.wait_ge(sem("q_low_ready"), 2 * g + 2)
                    mm(bank[:, A, 0:CTX], wk[:, :], kv[:, b, SEQ:KEYS], start=True, stop=True)
                    mm(bank[0:TAIL, A, P:2 * P], kv[:, b, KEYS - TAIL:KEYS], wv[:, :], start=True, stop=True
                       ).then_inc(sem("tail_projected"), 1)

                def project_v(g, b):
                    pe.wait_ge(sem("v_tail_ready"), g + 1)
                    for kt in range(KT - 1):
                        ins = mm(bank[:, A, kt * P:(kt + 1) * P], kv[:, b, kt * P:(kt + 1) * P], wv[:, :],
                                 start=True, stop=True)
                    ins.then_inc(sem("v_projected"), 1)

                def turn_attended(g, b, keys_between):
                    pe.wait_ge(sem("normalized"), 2 * g + 2)
                    if keys_between:
                        pe.wait_ge(sem("k_low_ready"), 4 * g + 12)
                    else:
                        pe.wait_ge(sem("attended_kept"), g)
                    for qt in range(QT):
                        ins = nc.tensor.transpose(bank[:, B, qt * P:(qt + 1) * P], attended[:, b, qt, :],
                                                  s.identity[:, :])
                    ins.then_inc(sem("attended_turned"), 1)

                def score_high(w, g, b, hh, kt, first):
                    if kt == 0:
                        pe.wait_ge(sem("k_low_ready"), 4 * g + 4)
                        pe.wait_ge(sem("q_low_ready"), 2 * g + 2)
                    if not (first and kt < 2):
                        pe.wait_ge(sem("probs_ready"), KT * w + kt - 1 if kt >= 2 else KT * w - kt)
                    mm(bank[0:widths[kt], SCORE + kt % 2, :], k_both[:, b, hh, kt * P:kt * P + widths[kt]],
                       q_high2[:, b, hh, :], start=True, stop=False)

                def score_low(w, b, hh, kt):
                    if kt == 0:
                        pe.wait_ge(sem("shift_ready"), w + 1)
                    mm(bank[0:widths[kt], SCORE + kt % 2, :], k_high[:, b, hh, kt * P:kt * P + widths[kt]],
                       q_low[:, b, hh, :], start=False, stop=True).then_inc(sem("scored"), 1)

                def weigh(w, g, b, hh, qt, first):
                    if qt == 0:
                        pe.wait_ge(sem("probs_ready"), KT * w + KT)
                        pe.wait_ge(sem("v_ready"), g + 1)
                        if not first:
                            pe.wait_ge(sem("normalized"), w)
                    for kt in range(KT):
                        n = widths[kt]
                        ins = mm(weighted[:, qt, :], probs[0:n, hh, kt, qt * P:(qt + 1) * P],
                                 values[0:n, b, kt, hh, :], start=kt == 0, stop=kt == KT - 1)
                    if qt == QT - 1:
                        ins.then_inc(sem("pv_done"), 1)

                def score_max(w, g, b, hh, qt, first):
                    if qt == 0:
                        pe.wait_ge(sem("narrowed"), 3 * g + 3)
                    if not (first and qt == 0):
                        pe.wait_ge(sem("max_taken"), QT * w + qt)
                    lhs = queries16[:, b, hh, qt * P:(qt + 1) * P]
                    mm(maxima[:, 0:SEQ], lhs, keys16[:, b, hh, 0:SEQ], start=True, stop=True)
                    mm(maxima[:, SEQ:KEYS], lhs, keys16[:, b, hh, SEQ:KEYS], start=True, stop=True
                       ).then_inc(sem("max_scored"), 1)

                def turn_shift(w, hh):
                    pe.wait_ge(sem("max_taken"), QT * w + QT)
                    for qt in range(QT):
                        ins = mm(bank[DH0:DH0 + 1, ROW, qt * P:(qt + 1) * P], shift[:, hh, qt:qt + 1],
                                 s.identity16[:, :], start=True, stop=True)
                    ins.then_inc(sem("shift_turned"), 1)

                def unit(pair, u, first, last):
                    w = 4 * pair + u
                    gg, b, hh = split(u)
                    g = 2 * pair + gg
                    before, after = (u - 1) // 2, (u + 1) // 2
                    start, ends = first and u == 0, last and u == 3
                    next_group = not (last and b == 1)

                    def weigh_before(qt):
                        if not start:
                            weigh(w - 1, 2 * pair + before, before % 2, 1 - hh, qt, first and u == 1)

                    def max_after(qt):
                        if not ends:
                            score_max(w + 1, 2 * pair + after, after % 2, 1 - hh, qt, False)

                    def score(kt):
                        score_high(w, g, b, hh, kt, start)
                        score_low(w, b, hh, kt)

                    score_high(w, g, b, hh, 0, start)
                    score_high(w, g, b, hh, 1, start)
                    score_low(w, b, hh, 0)
                    score_low(w, b, hh, 1)
                    if hh == 0 and next_group:
                        project_q(pair + b, g + 1, 1 - b)
                    weigh_before(0)
                    max_after(0)
                    score(2)
                    if hh == 0 and next_group:
                        project_k(g + 1, 1 - b)
                    if hh == 1 and not (first and b == 0):
                        turn_attended(g - 1, 1 - b, next_group)
                    weigh_before(1)
                    max_after(1)
                    score(3)
                    if hh == 0 and next_group:
                        project_tail(g + 1, 1 - b)
                    if hh == 1 and next_group:
                        project_v(g + 1, 1 - b)
                    max_after(2)
                    weigh_before(2)
                    max_after(3)
                    score(4)
                    weigh_before(3)
                    if not ends:
                        turn_shift(w + 1, 1 - hh)

                project_q(0, 0, 0)
                project_k(0, 0)
                project_tail(0, 0)
                project_v(0, 0)
                for qt in range(QT):
                    score_max(0, 0, 0, 0, qt, True)
                turn_shift(0, 0)
                for u in range(4):
                    unit(0, u, True, False)
                with pe.Fori(1, PAIRS - 1) as pair:
                    for u in range(4):
                        unit(pair, u, False, False)
                for u in range(4):
                    unit(PAIRS - 1, u, False, True)
                for qt in range(QT):
                    weigh(4 * PAIRS - 1, 2 * PAIRS - 1, 1, 1, qt, False)
                turn_attended(2 * PAIRS - 1, 1, False)
                pe.wait_ge(sem("wo0_loaded"), 16)
                pe.wait_ge(sem("probs_ready"), KT * 4 * PAIRS)
                pe.wait_ge(sem("attended_kept"), 2 * PAIRS)
                for b in range(BATCH):
                    for j in range(PAIRS):
                        ins = mm(bank[:, SCORE + b, :], wo[:, j, :], attended_t[:, j, b, :],
                                 start=j == 0, stop=j == PAIRS - 1)
                    ins.then_inc(sem("x0_projected"), 1)



def norm_all_pe(s, pe, k):
    for b in range(BATCH):
        norm_mean(s, pe, k + b, s.x[:, b, :])
    for b in range(BATCH):
        norm_variance(s, pe, k + b, SEQ)


def norm_all_act(s, act, k):
    for b in range(BATCH):
        norm_square(s, act, k + b, SEQ)
    for b in range(BATCH):
        norm_deviation(s, act, k + b, SEQ, s.ln_eps[:, :])


def norm_all_dve(s, dve, k, target):
    for b in range(BATCH):
        norm_center(s, dve, k + b, s.x[:, b, :])
    for b in range(BATCH):
        norm_apply(s, dve, k + b, SEQ, target[:, b, :]).then_inc(s.sem("xn_ready"), 1)



def stage_ternary_ffn(s, i):
    nc = s.nc
    HIDDEN = 512
    J = HIDDEN // P
    WEIGHTS = HIDDEN * P
    with ExitStack() as ctx:
        def sb(name, shape, dt=F32):
            return ctx.enter_context(nc.sbuf_tensor(name, shape, dt))

        w1 = sb("ffn_w1", [P, J, P])
        w2 = sb("ffn_w2", [P, HIDDEN])
        w1_t16 = sb("w1_t16", [P, J, P], BF16)
        w2_t16 = sb("w2_t16", [P, J, P], BF16)
        ternary = sb("ternary", [P, 2, HIDDEN], BF16)
        rounded = sb("w_rounded", [P, HIDDEN])
        mass = sb("mass", [P, 2])
        share = sb("share", [P, P])
        wscale = sb("wscale", [P, 4])
        taps = sb("taps", [P, J, 3])
        tap_bias = sb("tap_bias", [P, J])
        xn = sb("ffn_xn", [P, BATCH, SEQ])
        peak = sb("peak", [P, 3, TILES])
        scale = sb("token_scale", [P, BATCH, SEQ])
        unscale = sb("token_unscale", [P, BATCH, SEQ])
        q1 = sb("q1", [P, BATCH, SEQ], BF16)
        hidden = sb("hidden", [P, J, BATCH, SEQ + 2])
        conv = sb("conv", [P, J, BATCH, SEQ])
        tanh = sb("tanh", [P, J, BATCH, SEQ])
        q2 = sb("q2", [P, J, BATCH, SEQ], BF16)
        bank, sem = s.bank, s.sem
        k0 = s.ln_count
        s.ln_count += 2
        xn0 = s.xn_count
        s.xn_count += 2
        with nc.Block() as block:
            @block.sync
            def _(sp):
                sp.dma_start(w1[:, :, :], i["L0_ffn_w1"].rearrange("(j p) d -> p j d", p=P)
                             ).then_inc(sem("ffn_loaded"), 16)
                sp.dma_start(w2[:, :], i["L0_ffn_w2"]).then_inc(sem("ffn_loaded"), 16)
                sp.dma_start(taps[:, :, :], i["L0_ffn_conv_w"].rearrange("(j p) o k -> p j (o k)", p=P)
                             ).then_inc(sem("ffn_loaded"), 16)
                sp.dma_start(tap_bias[:, :], i["L0_ffn_conv_b"].rearrange("(j p) -> p j", p=P),
                             allow_slow_non_contiguous=True).then_inc(sem("ffn_loaded"), 16)

            @block.gpsimd
            def _(pool):
                nc.gpsimd.memset(share[:, :], 1.0 / WEIGHTS).then_inc(sem("ffn_constants"), 1)
                nc.gpsimd.memset(hidden[:, :, :, 0:1], 0.0).then_inc(sem("ffn_constants"), 1)
                nc.gpsimd.memset(hidden[:, :, :, SEQ + 1:SEQ + 2], 0.0).then_inc(sem("ffn_constants"), 1)

            @block.scalar
            def _(act):
                norm_all_act(s, act, k0)
                for b in range(BATCH):
                    act.wait_ge(sem("unscale_rows"), b + 1)
                    nc.scalar.activation(unscale[:, b, :], bank[:, 6 + b, :], ACT.Copy,
                                         ).then_inc(sem("unscale_ready"), 1)
                for j in range(J):
                    act.wait_ge(sem("hidden_ready"), 2 * j + 2)
                    nc.scalar.activation(conv[:, j, :, :], hidden[:, j, :, 1:SEQ + 1], ACT.Identity,
                                         scale=taps[:, j, 1:2], bias=tap_bias[:, j:j + 1]
                                         ).then_inc(sem("middle_tap"), 1)
                for j in range(J):
                    act.wait_ge(sem("convolved"), j + 1)
                    nc.scalar.activation(tanh[:, j, :, :], conv[:, j, :, :], ACT.Tanh, scale=0.5
                                         ).then_inc(sem("tanh_ready"), 1)
                for j in range(J):
                    act.wait_ge(sem("silu_ready"), j + 1)
                    nc.scalar.activation(tanh[:, j, :, :], conv[:, j, :, :], ACT.Abs
                                         ).then_inc(sem("silu_absolute"), 1)
                for b in range(BATCH):
                    act.wait_ge(sem("unscale_rows"), 2 + b + 1)
                    nc.scalar.activation(unscale[:, b, :], bank[:, 6 + b, :], ACT.Copy,
                                         ).then_inc(sem("unscale_ready"), 1)

            @block.vector
            def _(dve):
                v, step = nc.vector, s.dve
                dve.wait_ge(sem("ffn_loaded"), 64)
                w1_flat = w1[:, :, :].rearrange("p j d -> p (j d)")
                v.tensor_reduce(mass[:, 0:1], w1_flat, AX.X, ALU.add, apply_absolute_value=True
                                ).then_inc(sem("mass_ready"), 1)
                v.tensor_reduce(mass[:, 1:2], w2[:, :], AX.X, ALU.add, apply_absolute_value=True
                                ).then_inc(sem("mass_ready"), 1)
                norm_center(s, dve, k0, s.x[:, 0, :])
                norm_center(s, dve, k0 + 1, s.x[:, 1, :])
                dve.wait_ge(sem("mass_shared"), 1)
                step(v.tensor_scalar(wscale[:, 0:2], bank[:, 4, 0:2], 1e-5, None, ALU.max))
                step(v.reciprocal(wscale[:, 2:4], wscale[:, 0:2]))
                for n, w in enumerate((w1_flat, w2[:, :])):
                    step(v.tensor_scalar(rounded[:, :], w, wscale[:, 2 + n:3 + n], ROUND, ALU.mult, ALU.add))
                    step(v.tensor_scalar(rounded[:, :], rounded[:, :], ROUND, 1.0, ALU.subtract, ALU.min))
                    v.tensor_scalar(ternary[:, n, :], rounded[:, :], -1.0, None, ALU.max
                                    ).then_inc(sem("ternary_rows"), 1)
                    dve.wait_ge(sem("ternary_rows"), n + 1)
                step(v.tensor_scalar(wscale[:, 0:1], wscale[:, 0:1], 1 / 127.0, None, ALU.mult))
                step(v.tensor_scalar(wscale[:, 1:2], wscale[:, 1:2], 0.5 / 127.0, None, ALU.mult))
                dve.wait_ge(sem("w_turned"), 2)
                step(v.tensor_copy(w1_t16[:, :, :].rearrange("p j d -> p (j d)"),
                                   bank[:, 4, 0:256].bitcast(BF16)))
                v.tensor_copy(w2_t16[:, :, :].rearrange("p j d -> p (j d)"),
                              bank[:, 5, 0:256].bitcast(BF16)).then_inc(sem("ternary_ready"), 1)
                for b in range(BATCH):
                    norm_apply(s, dve, k0 + b, SEQ, xn[:, b, :]).then_inc(sem("xn_ready"), 1)

                def token_scales(n, floor):
                    for b in range(BATCH):
                        dve.wait_ge(sem("peak_turned"), 2 * n + b + 1)
                        step(v.tensor_reduce(peak[:, 0, 4 * b:4 * b + 4],
                                             bank[:, 4 + b, :].rearrange("p (n d) -> p n d", d=P),
                                             AX.X, ALU.max, apply_absolute_value=True))
                    step(v.tensor_scalar(peak[:, 0, :], peak[:, 0, :], floor, None, ALU.max))
                    step(v.reciprocal(peak[:, 1, :], peak[:, 0, :]))
                    v.tensor_scalar(peak[:, 2, :], peak[:, 0, :], wscale[:, n:n + 1], None, ALU.mult
                                    ).then_inc(sem("token_scales"), 1)
                    v.tensor_scalar(peak[:, 1, :], peak[:, 1, :], 127.0, None, ALU.mult
                                    ).then_inc(sem("token_scales"), 1)

                token_scales(0, 1e-5)
                for b in range(BATCH):
                    dve.wait_ge(sem("scale_rows"), b + 1)
                    step(v.tensor_tensor(xn[:, b, :], xn[:, b, :], bank[:, 4 + b, :], ALU.mult))
                    step(v.tensor_scalar(xn[:, b, :], xn[:, b, :], ROUND, ROUND + 127.0, ALU.add, ALU.min))
                    v.tensor_scalar(q1[:, b, :], xn[:, b, :], ROUND - 128.0, ROUND, ALU.max, ALU.subtract
                                    ).then_inc(sem("q1_ready"), 1)
                dve.wait_ge(sem("ffn_constants"), 3)
                dve.wait_ge(sem("unscale_ready"), 2)
                for j in range(J):
                    for b in range(BATCH):
                        dve.wait_ge(sem("up_projected"), 2 * j + b + 1)
                        v.tensor_tensor(hidden[:, j, b, 1:SEQ + 1], bank[:, (2 * j + b) % 4, :],
                                        unscale[:, b, :], ALU.mult).then_inc(sem("hidden_ready"), 1)
                for j in range(J):
                    dve.wait_ge(sem("middle_tap"), j + 1)
                    for tap, at in ((0, 0), (2, 2)):
                        ins = v.scalar_tensor_tensor(conv[:, j, :, :], hidden[:, j, :, at:at + SEQ],
                                                     taps[:, j, tap:tap + 1], conv[:, j, :, :],
                                                     ALU.mult, ALU.add)
                        if tap == 0:
                            step(ins)
                    ins.then_inc(sem("convolved"), 1)
                for j in range(J):
                    dve.wait_ge(sem("tanh_ready"), j + 1)
                    v.scalar_tensor_tensor(conv[:, j, :, :], tanh[:, j, :, :], 1.0, conv[:, j, :, :],
                                           ALU.add, ALU.mult).then_inc(sem("silu_ready"), 1)
                largest = tanh[:, 0, :, :]
                for j in range(1, J):
                    dve.wait_ge(sem("silu_absolute"), j + 1)
                    v.tensor_tensor(largest, largest, tanh[:, j, :, :], ALU.max).then_inc(sem("largest"), 1)
                    dve.wait_ge(sem("largest"), j)
                token_scales(1, 2e-5)
                for b in range(BATCH):
                    dve.wait_ge(sem("scale_rows"), 2 + b + 1)
                    step(v.tensor_copy(scale[:, b, :], bank[:, 4 + b, :]))
                for j in range(J):
                    step(v.tensor_tensor(conv[:, j, :, :], conv[:, j, :, :], scale[:, :, :], ALU.mult))
                    step(v.tensor_scalar(conv[:, j, :, :], conv[:, j, :, :], ROUND, ROUND + 127.0, ALU.add, ALU.min))
                    v.tensor_scalar(q2[:, j, :, :], conv[:, j, :, :], ROUND - 128.0, ROUND, ALU.max, ALU.subtract
                                    ).then_inc(sem("q2_ready"), 1)
                for b in range(BATCH):
                    dve.wait_ge(sem("down_projected"), b + 1)
                    dve.wait_ge(sem("unscale_ready"), 2 + b + 1)
                    step(v.tensor_tensor(unscale[:, b, :], unscale[:, b, :], bank[:, b, :], ALU.mult))
                    step(v.tensor_tensor(s.x[:, b, :], s.x[:, b, :], unscale[:, b, :], ALU.add))

            @block.tensor
            def _(pe):
                mm = nc.tensor.matmul
                norm_mean(s, pe, k0, s.x[:, 0, :])
                norm_mean(s, pe, k0 + 1, s.x[:, 1, :])
                pe.wait_ge(sem("ffn_constants"), 1)
                pe.wait_ge(sem("mass_ready"), 2)
                mm(bank[:, 4, 0:2], share[:, :], mass[:, :], start=True, stop=True
                   ).then_inc(sem("mass_shared"), 1)
                for b in range(BATCH):
                    norm_variance(s, pe, k0 + b, SEQ)
                pe.wait_ge(sem("ternary_rows"), 2)
                for n, slot in enumerate((4, 5)):
                    for j in range(J):
                        ins = nc.tensor.transpose(bank[:, slot, j * 64:j * 64 + 64].bitcast(BF16),
                                                  ternary[:, n, j * P:(j + 1) * P], s.identity16[:, :])
                    ins.then_inc(sem("w_turned"), 1)
                pe.wait_ge(sem("ternary_ready"), 1)

                def peaks(n, source):
                    for b in range(BATCH):
                        for q in range(4):
                            ins = nc.tensor.transpose(bank[:, 4 + b, q * P:(q + 1) * P],
                                                      source[:, b, q * P:(q + 1) * P], s.identity[:, :])
                        ins.then_inc(sem("peak_turned"), 1)

                def rows(n):
                    pe.wait_ge(sem("token_scales"), 2 * n + 2)
                    for kind, slot, name in ((1, 4, "scale_rows"), (2, 6, "unscale_rows")):
                        for b in range(BATCH):
                            for q in range(4):
                                column = peak[:, kind, 4 * b + q:4 * b + q + 1]
                                ins = mm(bank[:, slot + b, q * P:(q + 1) * P], column.to_broadcast([P, P]),
                                         s.identity[:, :], start=True, stop=True)
                            ins.then_inc(sem(name), 1)

                pe.wait_ge(sem("xn_ready"), xn0 + 2)
                peaks(0, xn)
                rows(0)
                for j in range(J):
                    for b in range(BATCH):
                        if j == 0:
                            pe.wait_ge(sem("q1_ready"), b + 1)
                        if j >= 2:
                            pe.wait_ge(sem("hidden_ready"), 2 * j + b - 3)
                        mm(bank[:, (2 * j + b) % 4, :], w1_t16[:, j, :], q1[:, b, :], start=True, stop=True
                           ).then_inc(sem("up_projected"), 1)
                pe.wait_ge(sem("largest"), J - 1)
                peaks(1, tanh[:, 0, :, :])
                rows(1)
                pe.wait_ge(sem("q2_ready"), J)
                for b in range(BATCH):
                    for j in range(J):
                        ins = mm(bank[:, b, :], w2_t16[:, j, :], q2[:, j, b, :], start=j == 0, stop=j == J - 1)
                    ins.then_inc(sem("down_projected"), 1)



def stage_delta_rule(s, i):
    nc = s.nc
    HEADS, DH = 16, 8
    CHUNK = 32
    CHUNKS = SEQ // CHUNK
    INST = BATCH * CHUNKS
    STEPS = 4
    TAPS = 4
    NAMES = ("q", "k", "v")
    with ExitStack() as ctx:
        def sb(name, shape, dt=F32):
            return ctx.enter_context(nc.sbuf_tensor(name, shape, dt))

        w_rows = sb("dr_w_rows", [P, 4, P])
        wb_rows = sb("dr_wb_rows", [HEADS, P])
        w_t = sb("dr_w_t", [P, 4, P])
        wb_t = sb("dr_wb_t", [P, HEADS, 1])
        wb_wide = sb("dr_wb_wide", [P, HEADS, DH])
        taps = sb("dr_taps", [P, 3, TAPS])
        gain = sb("dr_gain", [P, 1])
        half = sb("dr_half", [P, 1])
        xn = sb("dr_xn", [P, BATCH, SEQ])
        spread = sb("spread", [P, DH, HEADS, DH])
        blocks = sb("blocks", [P, HEADS, DH])
        blocks_mean = sb("blocks_mean", [P, HEADS, DH])
        head_sum = sb("head_sum", [P, HEADS])
        eye8 = sb("eye8", [P, 1, DH])
        padded = sb("dr_padded", [P, 3, BATCH, SEQ + TAPS - 1])
        mixed = sb("dr_mixed", [P, 3, BATCH, SEQ])
        tanh = sb("dr_tanh", [P, 3, BATCH, SEQ])
        root_beta = sb("root_beta", [P, BATCH, SEQ])
        lengths = sb("lengths", [P, 2, TILES, HEADS, 1])
        wide = sb("wide_lengths", [P, 2, TILES, HEADS, DH])
        values = sb("dr_values", [P, INST, CHUNK, 2])
        keys8 = sb("keys8", [P, INST, CHUNK, DH])
        queries8 = sb("queries8", [P, INST, CHUNK, DH])
        S = sb("dr_state", [P, STEPS, INST, 2, DH])
        product = sb("dr_product", [P, INST, 2, DH])
        seen = sb("dr_seen", [P, INST, 2])
        change = sb("dr_change", [P, INST, 2, 1])
        update = sb("dr_update", [P, INST, 2, DH])
        asked = sb("dr_asked", [P, STEPS, INST, 2, DH])
        starts = sb("dr_starts", [P, INST, 1, DH])
        keys_flat = keys8[:, :, :, :].rearrange("p i c d -> p (i c d)")
        queries_flat = queries8[:, :, :, :].rearrange("p i c d -> p (i c d)")
        block_m = keys_flat[:, 0:INST * P].rearrange("p (i h d) -> p i h d", i=INST, h=HEADS)
        block_nn = queries_flat[:, 0:INST * P].rearrange("p (i h d) -> p i h d", i=INST, h=HEADS)
        CONSTANTS = 11
        bank, sem = s.bank, s.sem
        k0 = s.ln_count
        s.ln_count += 2
        xn0 = s.xn_count
        s.xn_count += 2
        with nc.Block() as block:
            @block.sync
            def _(sp):
                for j, name in enumerate(("Wq", "Wk", "Wv", "Wo")):
                    sp.dma_start(w_rows[:, j, :], i["L1_attn_" + name]).then_inc(sem("dr_loaded"), 16)
                sp.dma_start(wb_rows[:, :], i["L1_attn_Wb"]).then_inc(sem("dr_loaded"), 16)
                for j, name in enumerate(NAMES):
                    sp.dma_start(taps[:, j, :], i["L1_attn_conv_" + name]).then_inc(sem("dr_loaded"), 16)
                for h in range(HEADS):
                    sp.dma_start(gain[h * DH:(h + 1) * DH, :], i["L1_attn_o_norm_w"].rearrange("(p o) -> p o", o=1)
                                 ).then_inc(sem("dr_gain_loaded"), 16)

            @block.gpsimd
            def _(pool):
                g = nc.gpsimd
                n = 0

                def then(ins):
                    nonlocal n
                    n += 1
                    ins.then_inc(sem("dr_constants"), 1)
                    pool.wait_ge(sem("dr_constants"), n)

                then(g.memset(half[:, :], 0.5))
                then(g.memset(padded[:, :, :, 0:TAPS - 1], 0.0))
                then(g.memset(values[:, :, :, 1:2], 0.0))
                then(g.memset(S[:, 0, :, 0, :], 0.0))
                then(g.memset(spread[:, :, :, :], 0.0))
                then(g.affine_select(out=spread[:, :, :, :], in_=spread[:, :, :, :], compare_op=ALU.not_equal,
                                     fill=1.0, base=0, pattern=[[-1, DH], [-DH, HEADS], [0, DH]],
                                     channel_multiplier=1))
                then(g.memset(blocks[:, :, :], 1.0))
                then(g.affine_select(out=blocks[:, :, :], in_=blocks[:, :, :], compare_op=ALU.is_ge, fill=0.0,
                                     base=0, pattern=[[-DH, HEADS], [0, DH]], channel_multiplier=1))
                then(g.affine_select(out=blocks[:, :, :], in_=blocks[:, :, :], compare_op=ALU.is_ge, fill=0.0,
                                     base=DH - 1, pattern=[[DH, HEADS], [0, DH]], channel_multiplier=-1))
                then(g.tensor_scalar(blocks_mean[:, :, :], blocks[:, :, :], 1.0 / DH, None, ALU.mult))
                then(g.tensor_copy(head_sum[:, :], blocks[:, :, 0]))
                assert n == CONSTANTS

                def ask(st, base):
                    if st == 0:
                        pool.wait_ge(sem("asked_summed"), base)
                    pool.wait_ge(sem("state_step"), 5 * (STEPS * base + st) + 5)
                    g.tensor_tensor(asked[:, st, :, :, :], S[:, (st + 1) % STEPS, :, :, :],
                                    queries8[:, :, bass.ds(STEPS * base + st, 1), :].to_broadcast([P, INST, 2, DH]),
                                    ALU.mult).then_inc(sem("asked"), 1)

                pool.wait_ge(sem("queries_spread"), 16)
                for st in range(STEPS):
                    if st == 0:
                        pool.wait_ge(sem("state_step"), 5)
                    else:
                        pool.wait_ge(sem("state_step"), 5 * st + 5)
                    g.tensor_tensor(asked[:, st, :, :, :], S[:, (st + 1) % STEPS, :, :, :],
                                    queries8[:, :, st:st + 1, :].to_broadcast([P, INST, 2, DH]),
                                    ALU.mult).then_inc(sem("asked"), 1)
                with pool.Fori(1, CHUNK // STEPS) as base:
                    for st in range(STEPS):
                        ask(st, base)

            @block.scalar
            def _(act):
                a = nc.scalar.activation
                norm_all_act(s, act, k0)
                act.wait_ge(sem("w_rows_turned"), 5)
                a(w_t[:, :, :], bank[:, 4, :].rearrange("p (j d) -> p j d", d=P), ACT.Copy
                  ).then_inc(sem("dr_weights"), 1)
                a(wb_t[:, :, :], bank[:, 5, 0:HEADS].rearrange("p (h o) -> p h o", o=1), ACT.Copy
                  ).then_inc(sem("dr_weights"), 1)
                act.wait_ge(sem("dr_weights"), 2)
                a(wb_wide[:, :, :], wb_t[:, :, :].to_broadcast([P, HEADS, DH]), ACT.Copy
                  ).then_inc(sem("dr_weights"), 1)
                act.wait_ge(sem("dr_constants"), CONSTANTS)
                order = (1, 0, 2)
                for n, j in enumerate(order):
                    for b in range(BATCH):
                        act.wait_ge(sem("dr_projected"), 2 * n + b + 1)
                        a(padded[:, j, b, TAPS - 1:], bank[:, (2 * n + b) % 4, :], ACT.Copy
                          ).then_inc(sem("dr_padded"), 1)
                    act.wait_ge(sem("dr_padded"), 2 * n + 2)
                    a(mixed[:, j, :, :], padded[:, j, :, TAPS - 1:], ACT.Copy, scale=taps[:, j, TAPS - 1:TAPS]
                      ).then_inc(sem("last_tap"), 1)
                for b in range(BATCH):
                    act.wait_ge(sem("dr_projected"), 6 + b + 1)
                    a(root_beta[:, b, :], bank[:, 6 + b, :], ACT.Tanh, scale=0.5).then_inc(sem("beta_tanh"), 1)
                for n, j in enumerate(order):
                    act.wait_ge(sem("dr_mixed"), n + 1)
                    a(tanh[:, j, :, :], mixed[:, j, :, :], ACT.Tanh, scale=0.5).then_inc(sem("dr_tanh"), 1)
                for n, j in enumerate(order[:2]):
                    act.wait_ge(sem("dr_silu"), n + 1)
                    a(tanh[:, j, :, :], mixed[:, j, :, :], ACT.Square).then_inc(sem("dr_squared"), 1)
                act.wait_ge(sem("beta_tanh"), 2)
                a(root_beta[:, :, :], root_beta[:, :, :], ACT.Sqrt, scale=0.5, bias=half[:, :]
                  ).then_inc(sem("beta_ready"), 1)
                for n in range(2):
                    act.wait_ge(sem("lengths_summed"), n + 1)
                    a(lengths[:, n, :, :, :].rearrange("p t h o -> p (t h o)"), bank[:, 4 + n, 0:TILES * HEADS],
                      ACT.Sqrt).then_inc(sem("lengths_rooted"), 1)
                for n in range(2):
                    act.wait_ge(sem("lengths_inverse"), n + 1)
                    a(wide[:, n, :, :, :].rearrange("p t h d -> p (t h) d"),
                      lengths[:, n, :, :, :].rearrange("p t h o -> p (t h) o").to_broadcast([P, TILES * HEADS, DH]),
                      ACT.Copy).then_inc(sem("lengths_wide"), 1)
                for n, target in enumerate((keys8, queries8)):
                    for b in range(BATCH):
                        for d in range(DH):
                            m = 16 * n + DH * b + d
                            act.wait_ge(sem("spread_done"), m + 1)
                            a(target[:, b * CHUNKS:(b + 1) * CHUNKS, :, d],
                              bank[:, m % 4, :].rearrange("p (c s) -> p c s", s=CHUNK), ACT.Copy
                              ).then_inc(sem(("keys_spread", "queries_spread")[n]), 1)

                for b in range(BATCH):
                    act.wait_ge(sem("asked_summed"), CHUNK // STEPS)
                    a(tanh[:, 0, b, :], bank[:, 4 + 2 * b, :], ACT.Copy).then_inc(sem("own_outputs"), 1)
                    a(tanh[:, 1, b, :], bank[:, 5 + 2 * b, :], ACT.Copy).then_inc(sem("carried"), 1)
                for b in range(BATCH):
                    act.wait_ge(sem("o_ready"), b + 1)
                    a(tanh[:, 2, b, :], mixed[:, 0, b, :], ACT.Square).then_inc(sem("o_squared"), 1)
                for b in range(BATCH):
                    act.wait_ge(sem("o_mean"), b + 1)
                    a(tanh[:, 2, b, :], bank[:, 2 + b, :], ACT.Sqrt, bias=s.rms_eps[:, :]
                      ).then_inc(sem("o_rooted"), 1)

            @block.vector
            def _(dve):
                v, step = nc.vector, s.dve
                norm_all_dve(s, dve, k0, xn)
                dve.wait_ge(sem("dr_constants"), CONSTANTS)
                v.tensor_reduce(eye8[:, :, :].rearrange("p o d -> p (o d)"), spread[:, :, :, 0],
                                AX.X, ALU.add).then_inc(sem("eye_ready"), 1)
                dve.wait_ge(sem("eye_ready"), 1)
                v.tensor_copy(S[:, 0, :, 1, :], eye8[:, :, :].to_broadcast([P, INST, DH])
                              ).then_inc(sem("eye_ready"), 1)
                order = (1, 0, 2)
                for n, j in enumerate(order):
                    dve.wait_ge(sem("last_tap"), n + 1)
                    for tap in range(TAPS - 1):
                        ins = v.scalar_tensor_tensor(mixed[:, j, :, :], padded[:, j, :, tap:tap + SEQ],
                                                     taps[:, j, tap:tap + 1], mixed[:, j, :, :],
                                                     ALU.mult, ALU.add)
                        if tap < TAPS - 2:
                            step(ins)
                    ins.then_inc(sem("dr_mixed"), 1)
                for n, j in enumerate(order):
                    dve.wait_ge(sem("dr_tanh"), n + 1)
                    v.scalar_tensor_tensor(mixed[:, j, :, :], tanh[:, j, :, :], 1.0, mixed[:, j, :, :],
                                           ALU.add, ALU.mult).then_inc(sem("dr_silu"), 1)
                for n in range(2):
                    dve.wait_ge(sem("lengths_rooted"), n + 1)
                    flat = lengths[:, n, :, :, :].rearrange("p t h o -> p (t h o)")
                    step(v.tensor_scalar(flat, flat, 2e-6, None, ALU.max))
                    v.reciprocal(flat, flat).then_inc(sem("lengths_inverse"), 1)
                dve.wait_ge(sem("beta_ready"), 1)
                for b in range(BATCH):
                    dve.wait_ge(sem("length_rows"), b + 1)
                    step(v.tensor_tensor(mixed[:, 1, b, :], mixed[:, 1, b, :], root_beta[:, b, :], ALU.mult))
                    v.tensor_tensor(mixed[:, 1, b, :], mixed[:, 1, b, :], bank[:, 6 + b, :], ALU.mult
                                    ).then_inc(sem("keys_scaled"), 1)
                for b in range(BATCH):
                    dve.wait_ge(sem("length_rows"), 2 + b + 1)
                    v.scalar_tensor_tensor(mixed[:, 0, b, :], mixed[:, 0, b, :], float(DH ** -0.5),
                                           bank[:, 4 + b, :], ALU.mult, ALU.mult).then_inc(sem("queries_scaled"), 1)
                dve.wait_ge(sem("dr_silu"), 3)
                v.scalar_tensor_tensor(values[:, :, :, 0],
                                       mixed[:, 2, :, :].rearrange("p b (c s) -> p (b c) s", s=CHUNK), 0.5,
                                       root_beta[:, :, :].rearrange("p b (c s) -> p (b c) s", s=CHUNK),
                                       ALU.mult, ALU.mult).then_inc(sem("eye_ready"), 1)
                dve.wait_ge(sem("eye_ready"), 3)
                dve.wait_ge(sem("keys_spread"), 16)

                def advance(base, st, first):
                    at = bass.ds(STEPS * base + st, 1) if not first else slice(st, st + 1)
                    n = 5 * (STEPS * base + st)
                    key = keys8[:, :, at, :].to_broadcast([P, INST, 2, DH])
                    value = values[:, :, at, :].rearrange("p i o k -> p i (o k)")
                    old, new = S[:, st, :, :, :], S[:, (st + 1) % STEPS, :, :, :]
                    done = sem("state_step")
                    v.tensor_tensor(product[:, :, :, :], old, key, ALU.mult).then_inc(done, 1)
                    dve.wait_ge(done, n + 1)
                    v.tensor_reduce(seen[:, :, :], product[:, :, :, :], AX.X, ALU.add).then_inc(done, 1)
                    dve.wait_ge(done, n + 2)
                    v.tensor_tensor(change[:, :, :, 0], value, seen[:, :, :], ALU.subtract).then_inc(done, 1)
                    dve.wait_ge(done, n + 3)
                    v.tensor_tensor(update[:, :, :, :], change[:, :, :, :].to_broadcast([P, INST, 2, DH]), key,
                                    ALU.mult).then_inc(done, 1)
                    dve.wait_ge(done, n + 4)
                    if not first:
                        dve.wait_ge(sem("asked"), STEPS * base + st - 3)
                    v.tensor_tensor(new, old, update[:, :, :, :], ALU.add).then_inc(done, 1)
                    dve.wait_ge(done, n + 5)

                for st in range(STEPS):
                    advance(0, st, True)
                with dve.Fori(1, CHUNK // STEPS) as base:
                    for st in range(STEPS):
                        advance(base, st, False)

                last = S[:, 0, :, :, :]
                dve.wait_ge(sem("asked"), CHUNK)
                for c in range(CHUNKS):
                    for kind, target in ((1, block_m), (0, block_nn)):
                        for b in range(BATCH):
                            n = b * CHUNKS + c
                            if c < CHUNKS - 1:
                                v.tensor_tensor(target[:, n, :, :],
                                                last[:, n:n + 1, kind, :].to_broadcast([P, HEADS, DH]),
                                                blocks[:, :, :], ALU.mult).then_inc(sem("chunk_blocks"), 1)
                    if c:
                        for b in range(BATCH):
                            n = b * CHUNKS + c
                            dve.wait_ge(sem("start_summed"), 2 * (c - 1) + b + 1)
                            v.tensor_copy(starts[:, n, 0, :], bank[:, b, c * DH:(c + 1) * DH]
                                          ).then_inc(sem("start_ready"), 1)
                dve.wait_ge(sem("start_ready"), 2 * (CHUNKS - 1))
                dve.wait_ge(sem("dr_gain_loaded"), 16 * HEADS)
                for b in range(BATCH):
                    for c in range(1, CHUNKS):
                        n = b * CHUNKS + c
                        v.tensor_tensor(block_m[:, n, :, :], starts[:, n, :, :].to_broadcast([P, HEADS, DH]),
                                        blocks[:, :, :], ALU.mult).then_inc(sem("start_blocks"), 1)
                for b in range(BATCH):
                    dve.wait_ge(sem("own_outputs"), b + 1)
                    dve.wait_ge(sem("carried_out"), b + 1)
                    step(v.tensor_copy(mixed[:, 0, b, 0:CHUNK], tanh[:, 0, b, 0:CHUNK]))
                    v.tensor_tensor(mixed[:, 0, b, CHUNK:], tanh[:, 0, b, CHUNK:], bank[:, 2 + b, CHUNK:], ALU.add
                                    ).then_inc(sem("o_ready"), 1)
                for b in range(BATCH):
                    dve.wait_ge(sem("o_rooted"), b + 1)
                    step(v.reciprocal(tanh[:, 2, b, :], tanh[:, 2, b, :]))
                    v.scalar_tensor_tensor(mixed[:, 0, b, :], mixed[:, 0, b, :], gain[:, 0:1], tanh[:, 2, b, :],
                                           ALU.mult, ALU.mult).then_inc(sem("o_normed"), 1)
                for b in range(BATCH):
                    dve.wait_ge(sem("dr_out"), b + 1)
                    step(v.tensor_tensor(s.x[:, b, :], s.x[:, b, :], bank[:, b, :], ALU.add))

            @block.tensor
            def _(pe):
                mm = nc.tensor.matmul
                norm_all_pe(s, pe, k0)
                pe.wait_ge(sem("dr_loaded"), 16 * 8)
                for j in range(4):
                    nc.tensor.transpose(bank[:, 4, j * P:(j + 1) * P], w_rows[:, j, :], s.identity[:, :]
                                        ).then_inc(sem("w_rows_turned"), 1)
                nc.tensor.transpose(bank[:, 5, 0:HEADS], wb_rows[:, :], s.identity[0:HEADS, 0:HEADS]
                                    ).then_inc(sem("w_rows_turned"), 1)
                pe.wait_ge(sem("dr_weights"), 3)
                pe.wait_ge(sem("xn_ready"), xn0 + 2)
                for n, j in enumerate((1, 0, 2)):
                    for b in range(BATCH):
                        if n == 2:
                            pe.wait_ge(sem("dr_padded"), b + 1)
                        mm(bank[:, (2 * n + b) % 4, :], w_t[:, j, :], xn[:, b, :], start=True, stop=True
                           ).then_inc(sem("dr_projected"), 1)
                for b in range(BATCH):
                    mm(bank[:, 6 + b, :], wb_wide[:, :, :].rearrange("p h d -> p (h d)"), xn[:, b, :],
                       start=True, stop=True).then_inc(sem("dr_projected"), 1)
                pe.wait_ge(sem("dr_constants"), CONSTANTS)
                for n, j in enumerate((1, 0)):
                    pe.wait_ge(sem("dr_squared"), n + 1)
                    for tile in range(TILES):
                        ins = mm(bank[:, 4 + n, tile * HEADS:(tile + 1) * HEADS],
                                 tanh[:, j, tile // 4, (tile % 4) * P:(tile % 4 + 1) * P], head_sum[:, :],
                                 start=True, stop=True)
                    ins.then_inc(sem("lengths_summed"), 1)
                pe.wait_ge(sem("beta_tanh"), 2)
                for n in range(2):
                    pe.wait_ge(sem("lengths_wide"), n + 1)
                    if n == 1:
                        pe.wait_ge(sem("lengths_rooted"), 2)
                    for b in range(BATCH):
                        for q in range(4):
                            tile = 4 * b + q
                            ins = mm(bank[:, (6 if n == 0 else 4) + b, q * P:(q + 1) * P],
                                     wide[:, n, tile, :, :].rearrange("p h d -> p (h d)"),
                                     s.identity[:, :], start=True, stop=True)
                        ins.then_inc(sem("length_rows"), 1)
                for n, (j, ready) in enumerate(((1, "keys_scaled"), (0, "queries_scaled"))):
                    for b in range(BATCH):
                        pe.wait_ge(sem(ready), b + 1)
                        for d in range(DH):
                            m = 16 * n + DH * b + d
                            if m >= 4:
                                name, count = ("keys_spread", m - 3) if m < 20 else ("queries_spread", m - 19)
                                pe.wait_ge(sem(name), count)
                            else:
                                pe.wait_ge(sem("dr_padded"), 6)
                            mm(bank[:, m % 4, :], spread[:, d, :, :].rearrange("p h m -> p (h m)"),
                               mixed[:, j, b, :], start=True, stop=True).then_inc(sem("spread_done"), 1)
                pe.wait_ge(sem("queries_scaled"), 2)

                def total(base, first):
                    pe.wait_ge(sem("asked"), STEPS * base + STEPS)
                    for b in range(BATCH):
                        for kind in range(2):
                            at = slice(0, STEPS) if first else bass.ds(STEPS * base, STEPS)
                            out = bank[:, 4 + 2 * b + kind, :].rearrange("p (c s) -> p c s", s=CHUNK)[:, :, at]
                            for d in range(DH):
                                rhs = asked[:, :, b * CHUNKS:(b + 1) * CHUNKS, kind, d].rearrange("p s c -> p c s")
                                ins = mm(out, s.identity[:, :], rhs, start=d == 0, stop=d == DH - 1)
                    ins.then_inc(sem("asked_summed"), 1)

                total(0, True)
                with pe.Fori(1, CHUNK // STEPS) as base:
                    total(base, False)
                pe.wait_ge(sem("keys_spread"), 16)
                pe.wait_ge(sem("queries_spread"), 16)
                for c in range(CHUNKS - 1):
                    for b in range(BATCH):
                        n = b * CHUNKS + c
                        out = bank[:, b, (c + 1) * DH:(c + 2) * DH]
                        pe.wait_ge(sem("chunk_blocks"), 4 * c + 4)
                        if c:
                            pe.wait_ge(sem("start_ready"), 2 * (c - 1) + b + 1)
                            mm(out, block_m[:, n, :, :].rearrange("p h d -> p (h d)"), starts[:, n, 0, :],
                               start=True, stop=False)
                        mm(out, block_nn[:, n, :, :].rearrange("p h d -> p (h d)"), eye8[:, 0, :],
                           start=c == 0, stop=True).then_inc(sem("start_summed"), 1)
                for b in range(BATCH):
                    pe.wait_ge(sem("carried"), b + 1)
                    for c in range(1, CHUNKS):
                        n = b * CHUNKS + c
                        pe.wait_ge(sem("start_blocks"), b * (CHUNKS - 1) + c)
                        ins = mm(bank[:, 2 + b, c * CHUNK:(c + 1) * CHUNK],
                                 block_m[:, n, :, :].rearrange("p h d -> p (h d)"),
                                 tanh[:, 1, b, c * CHUNK:(c + 1) * CHUNK], start=True, stop=True)
                    ins.then_inc(sem("carried_out"), 1)
                for b in range(BATCH):
                    pe.wait_ge(sem("o_squared"), b + 1)
                    mm(bank[:, 2 + b, :], blocks_mean[:, :, :].rearrange("p h d -> p (h d)"), tanh[:, 2, b, :],
                       start=True, stop=True).then_inc(sem("o_mean"), 1)
                for b in range(BATCH):
                    pe.wait_ge(sem("o_normed"), b + 1)
                    mm(bank[:, b, :], w_t[:, 3, :], mixed[:, 0, b, :], start=True, stop=True
                       ).then_inc(sem("dr_out"), 1)



def stage_cross_attention1(s, i):
    nc = s.nc
    QT = SEQ // P
    with ExitStack() as ctx:
        def sb(name, shape, dt=F32):
            return ctx.enter_context(nc.sbuf_tensor(name, shape, dt))

        w_rows = sb("x1_w_rows", [P, 3, P])
        w_t = sb("x1_w_t", [P, 3, P])
        bias = sb("x1_bias", [P, 3])
        xn = sb("x1_xn", [P, BATCH, SEQ])
        queries = sb("x1_queries", [P, BATCH, SEQ])
        keys = sb("x1_keys", [P, BATCH * CTX])
        values = sb("x1_values", [CTX, BATCH, P])
        shift = sb("x1_shift", [P, TILES])
        sums = sb("x1_sums", [P, TILES, 1])
        probs = sb("x1_probs", [P, TILES, CTX])
        probs_t = sb("x1_probs_t", [CTX, BATCH, SEQ])
        bank, sem = s.bank, s.sem
        k0 = s.ln_count
        s.ln_count += 2
        xn0 = s.xn_count
        s.xn_count += 2
        with nc.Block() as block:
            @block.sync
            def _(sp):
                for j, name in enumerate("qkv"):
                    sp.dma_start(w_rows[:, j, :], i["L1_xattn_W" + name]).then_inc(sem("x1_loaded"), 16)
                    sp.dma_start(bias[:, j:j + 1], i["L1_xattn_b" + name].rearrange("(p o) -> p o", o=1)
                                 ).then_inc(sem("x1_loaded"), 16)

            @block.scalar
            def _(act):
                a = nc.scalar.activation
                norm_all_act(s, act, k0)
                act.wait_ge(sem("x1_w_turned"), 1)
                a(w_t[:, :, :].rearrange("p j d -> p (j d)"), bank[:, 4, 0:3 * P], ACT.Copy
                  ).then_inc(sem("x1_weights"), 1)
                act.wait_ge(sem("x1_loaded"), 96)
                act.wait_ge(sem("x1_kv"), 1)
                a(keys[:, :], bank[:, 5, 0:BATCH * CTX], ACT.Identity, bias=bias[:, 1:2]
                  ).then_inc(sem("x1_kv_ready"), 1)
                a(values[:, :, :], bank[0:CTX, 5, 256:512].rearrange("p (b d) -> p b d", b=BATCH), ACT.Copy
                  ).then_inc(sem("x1_kv_ready"), 1)
                for b in range(BATCH):
                    act.wait_ge(sem("x1_projected"), b + 1)
                    a(queries[:, b, :], bank[:, b, :], ACT.Identity, bias=bias[:, 0:1]
                      ).then_inc(sem("x1_queries_ready"), 1)
                for b in range(BATCH):
                    act.wait_ge(sem("x1_shift"), b + 1)
                    for q in range(QT):
                        n = QT * b + q
                        a(probs[:, n, :], bank[:, 6 + b, q * CTX:(q + 1) * CTX], ACT.Exp,
                          bias=shift[:, n:n + 1], accum_out=sums[:, n, :]).then_inc(sem("x1_exp"), 1)
                for b in range(BATCH):
                    act.wait_ge(sem("x1_probs_turned"), b + 1)
                    a(probs_t[:, b, :], bank[0:CTX, 2 + b, :], ACT.Copy).then_inc(sem("x1_probs_ready"), 1)

            @block.vector
            def _(dve):
                v, step = nc.vector, s.dve
                norm_all_dve(s, dve, k0, xn)
                for b in range(BATCH):
                    dve.wait_ge(sem("x1_scored"), b + 1)
                    v.tensor_reduce(shift[:, QT * b:QT * b + QT],
                                    bank[:, 6 + b, 0:QT * CTX].rearrange("p (q k) -> p q k", k=CTX),
                                    AX.X, ALU.max, negate=True).then_inc(sem("x1_shift"), 1)
                for b in range(BATCH):
                    mine = slice(QT * b, QT * b + QT)
                    dve.wait_ge(sem("x1_exp"), QT * b + QT)
                    step(v.reciprocal(sums[:, mine, :], sums[:, mine, :]))
                    v.tensor_tensor(probs[:, mine, :], probs[:, mine, :],
                                    sums[:, mine, :].to_broadcast([P, QT, CTX]), ALU.mult
                                    ).then_inc(sem("x1_normalized"), 1)
                for b in range(BATCH):
                    dve.wait_ge(sem("x1_out"), b + 1)
                    v.scalar_tensor_tensor(s.x[:, b, :], bank[:, b, :], bias[:, 2:3], s.x[:, b, :],
                                           ALU.add, ALU.add).then_inc(sem("x1_done"), 1)

            @block.tensor
            def _(pe):
                mm = nc.tensor.matmul
                norm_all_pe(s, pe, k0)
                pe.wait_ge(sem("x1_loaded"), 96)
                for j in range(3):
                    ins = nc.tensor.transpose(bank[:, 4, j * P:(j + 1) * P], w_rows[:, j, :], s.identity[:, :])
                ins.then_inc(sem("x1_w_turned"), 1)
                pe.wait_ge(sem("x1_weights"), 1)
                mm(bank[:, 5, 0:BATCH * CTX], w_t[:, 1, :], s.ctx_t[:, :], start=True, stop=True)
                for b in range(BATCH):
                    ins = mm(bank[0:CTX, 5, 256 + b * P:256 + (b + 1) * P], s.ctx_t[:, b * CTX:(b + 1) * CTX],
                             w_t[:, 2, :], start=True, stop=True)
                ins.then_inc(sem("x1_kv"), 1)
                for b in range(BATCH):
                    pe.wait_ge(sem("xn_ready"), xn0 + b + 1)
                    mm(bank[:, b, :], w_t[:, 0, :], xn[:, b, :], start=True, stop=True
                       ).then_inc(sem("x1_projected"), 1)
                pe.wait_ge(sem("x1_kv_ready"), 2)
                for b in range(BATCH):
                    pe.wait_ge(sem("x1_queries_ready"), b + 1)
                    for q in range(QT):
                        ins = mm(bank[:, 6 + b, q * CTX:(q + 1) * CTX], queries[:, b, q * P:(q + 1) * P],
                                 keys[:, b * CTX:(b + 1) * CTX], start=True, stop=True)
                    ins.then_inc(sem("x1_scored"), 1)
                for b in range(BATCH):
                    pe.wait_ge(sem("x1_normalized"), b + 1)
                    for q in range(QT):
                        ins = nc.tensor.transpose(bank[0:CTX, 2 + b, q * P:(q + 1) * P],
                                                  probs[:, QT * b + q, :], s.identity[:, :])
                    ins.then_inc(sem("x1_probs_turned"), 1)
                for b in range(BATCH):
                    pe.wait_ge(sem("x1_probs_ready"), b + 1)
                    mm(bank[:, b, :], values[:, b, :], probs_t[:, b, :], start=True, stop=True
                       ).then_inc(sem("x1_out"), 1)



def stage_experts(s, i):
    nc = s.nc
    EXPERTS, INNER = 8, 256
    I = INNER // P
    with ExitStack() as ctx:
        def sb(name, shape, dt=F32):
            return ctx.enter_context(nc.sbuf_tensor(name, shape, dt))

        gate_w = sb("gate_w", [P, EXPERTS])
        sh_gate = sb("sh_gate", [P, INNER])
        sh_up = sb("sh_up", [P, INNER])
        sh_down = sb("sh_down", [P, I, P])
        rt_gate = sb("rt_gate", [P, EXPERTS, INNER])
        rt_up = sb("rt_up", [P, EXPERTS, INNER])
        rt_down = sb("rt_down", [P, EXPERTS, I, P])
        xn = sb("moe_xn", [P, BATCH, SEQ])
        logits = sb("logits", [P, TILES, EXPERTS])
        order = sb("order", [P, 1, EXPERTS])
        top = sb("top", [P, TILES, 1])
        score = sb("score", [P, TILES, 1])
        first = sb("first", [P, TILES, 1])
        chosen = sb("chosen", [P, TILES, EXPERTS])
        chosen16 = sb("chosen16", [P, TILES, EXPERTS], BF16)
        mask = sb("expert_mask", [P, EXPERTS, BATCH, SEQ], BF16)
        scored = sb("scored_x", [P, BATCH, SEQ])
        routed_x = sb("routed_x", [P, EXPERTS, BATCH, SEQ])
        extra = sb("masked_extra", [P, EXPERTS, BATCH, SEQ])
        tanh = sb("moe_tanh", [P, 2, SEQ])
        inner = sb("moe_inner", [P, 2, I, BATCH, SEQ])
        bank, sem = s.bank, s.sem
        k0 = s.ln_count
        s.ln_count += 2
        xn0 = s.xn_count
        s.xn_count += 2

        def masked_inner(j, e, b):
            return routed_x[:, e, b, :] if j == 0 else extra[:, e, b, :]

        UNITS = [(kind, b, j) for kind in range(2) for b in range(BATCH) for j in range(I)]
        with nc.Block() as block:
            @block.sync
            def _(sp):
                sp.dma_start(gate_w[:, :], i["L1_ffn_gate_w"]).then_inc(sem("moe_gate_loaded"), 16)
                sp.dma_start(sh_gate[:, :], i["L1_ffn_sh_gate"]).then_inc(sem("moe_shared_loaded"), 16)
                sp.dma_start(sh_up[:, :], i["L1_ffn_sh_up"]).then_inc(sem("moe_shared_loaded"), 16)
                sp.dma_start(sh_down[:, :, :], i["L1_ffn_sh_down"].rearrange("(j p) n -> p j n", p=P)
                             ).then_inc(sem("moe_shared_loaded"), 16)
                sp.dma_start(rt_gate[:, :, :], i["L1_ffn_rt_gate"].rearrange("e h i -> h e i")
                             ).then_inc(sem("moe_routed_loaded"), 16)
                sp.dma_start(rt_up[:, :, :], i["L1_ffn_rt_up"].rearrange("e h i -> h e i")
                             ).then_inc(sem("moe_routed_loaded"), 16)
                sp.dma_start(rt_down[:, :, :, :], i["L1_ffn_rt_down"].rearrange("e (j p) n -> p e j n", p=P)
                             ).then_inc(sem("moe_routed_loaded"), 16)

            @block.gpsimd
            def _(pool):
                for e in range(EXPERTS):
                    nc.gpsimd.memset(order[:, :, e:e + 1], float(e)).then_inc(sem("order_ready"), 1)
                    pool.wait_ge(sem("order_ready"), e + 1)
                for b in range(BATCH):
                    pool.wait_ge(sem("inner_ready"), 4 + 2 * b + 2)
                    for e in range(EXPERTS):
                        nc.gpsimd.tensor_tensor(masked_inner(1, e, b), inner[:, 1, 1, b, :], mask[:, e, b, :],
                                                ALU.mult).then_inc(sem("pool_masked"), 1)

            @block.scalar
            def _(act):
                a = nc.scalar.activation
                norm_all_act(s, act, k0)
                act.wait_ge(sem("top_ready"), 1)
                a(score[:, :, :], top[:, :, :], ACT.Tanh, scale=0.5).then_inc(sem("score_tanh"), 1)
                for e in range(EXPERTS):
                    for b in range(BATCH):
                        n = 2 * e + b
                        act.wait_ge(sem("mask_spread"), n + 1)
                        a(mask[:, e, b, :], bank[:, 4 + n % 4, :], ACT.Copy).then_inc(sem("mask_ready"), 1)
                for n, (kind, b, j) in enumerate(UNITS):
                    act.wait_ge(sem("gate_done"), n + 1)
                    if n >= 2:
                        act.wait_ge(sem("inner_ready"), n - 1)
                    a(tanh[:, n % 2, :], bank[:, 2 + 2 * (n % 3), :], ACT.Tanh, scale=0.5
                      ).then_inc(sem("moe_tanh"), 1)

            @block.vector
            def _(dve):
                v, step = nc.vector, s.dve
                norm_all_dve(s, dve, k0, xn)
                dve.wait_ge(sem("routed_logits"), 1)
                step(v.tensor_copy(logits[:, :, :], bank[:, 6, 0:TILES * EXPERTS].rearrange(
                    "p (t e) -> p t e", e=EXPERTS)))
                v.tensor_reduce(top[:, :, :].rearrange("p t o -> p (t o)"), logits[:, :, :], AX.X, ALU.max
                                ).then_inc(sem("top_ready"), 1)
                dve.wait_ge(sem("top_ready"), 1)
                dve.wait_ge(sem("order_ready"), EXPERTS)
                step(v.tensor_tensor(chosen[:, :, :], logits[:, :, :], top[:, :, :].to_broadcast([P, TILES, EXPERTS]),
                                     ALU.is_equal))
                step(v.tensor_scalar(chosen[:, :, :], chosen[:, :, :], -float(EXPERTS), float(EXPERTS),
                                     ALU.mult, ALU.add))
                step(v.tensor_tensor(chosen[:, :, :], chosen[:, :, :],
                                     order[:, :, :].to_broadcast([P, TILES, EXPERTS]), ALU.add))
                step(v.tensor_reduce(first[:, :, :].rearrange("p t o -> p (t o)"), chosen[:, :, :], AX.X, ALU.min))
                v.tensor_tensor(chosen16[:, :, :], order[:, :, :].to_broadcast([P, TILES, EXPERTS]),
                                first[:, :, :].to_broadcast([P, TILES, EXPERTS]), ALU.is_equal
                                ).then_inc(sem("chosen_ready"), 1)
                dve.wait_ge(sem("score_tanh"), 1)
                v.tensor_scalar(score[:, :, :], score[:, :, :], 0.5, 0.5, ALU.mult, ALU.add
                                ).then_inc(sem("score_ready"), 1)
                for b in range(BATCH):
                    dve.wait_ge(sem("score_spread"), b + 1)
                    v.tensor_tensor(scored[:, b, :], xn[:, b, :], bank[:, b, :], ALU.mult
                                    ).then_inc(sem("scored_ready"), 1)
                    dve.wait_ge(sem("scored_ready"), b + 1)
                for e in range(EXPERTS):
                    for b in range(BATCH):
                        dve.wait_ge(sem("mask_ready"), 2 * e + b + 1)
                        v.tensor_tensor(routed_x[:, e, b, :], scored[:, b, :], mask[:, e, b, :], ALU.mult
                                        ).then_inc(sem("routed_x_ready"), 1)

                def activate(n):
                    kind, b, j = UNITS[n]
                    target = inner[:, kind, j, b, :]
                    dve.wait_ge(sem("moe_tanh"), n + 1)
                    step(v.scalar_tensor_tensor(target, tanh[:, n % 2, :], 1.0, bank[:, 2 + 2 * (n % 3), :],
                                                ALU.add, ALU.mult))
                    dve.wait_ge(sem("up_done"), n + 1)
                    v.scalar_tensor_tensor(target, target, 0.5, bank[:, 3 + 2 * (n % 3), :], ALU.mult, ALU.mult
                                           ).then_inc(sem("inner_ready"), 1)

                for n in range(8):
                    activate(n)
                dve.wait_ge(sem("routed_up"), 4)
                for b in range(BATCH):
                    dve.wait_ge(sem("inner_ready"), 4 + 2 * b + 2)
                    for e in range(EXPERTS):
                        v.tensor_tensor(masked_inner(0, e, b), inner[:, 1, 0, b, :], mask[:, e, b, :], ALU.mult
                                        ).then_inc(sem("dve_masked"), 1)
                for b in range(BATCH):
                    dve.wait_ge(sem("moe_out"), b + 1)
                    step(v.tensor_tensor(s.x[:, b, :], s.x[:, b, :], bank[:, b, :], ALU.add))

            @block.tensor
            def _(pe):
                mm = nc.tensor.matmul
                norm_all_pe(s, pe, k0)
                pe.wait_ge(sem("moe_gate_loaded"), 16)
                for b in range(BATCH):
                    pe.wait_ge(sem("xn_ready"), xn0 + b + 1)
                    for q in range(4):
                        n = 4 * b + q
                        ins = mm(bank[:, 6, n * EXPERTS:(n + 1) * EXPERTS], xn[:, b, q * P:(q + 1) * P],
                                 gate_w[:, :], start=True, stop=True)
                ins.then_inc(sem("routed_logits"), 1)
                pe.wait_ge(sem("chosen_ready"), 1)

                def spread_mask(n):
                    e, b = n // 2, n % 2
                    if n >= 4:
                        pe.wait_ge(sem("mask_ready"), n - 3)
                    for q in range(4):
                        column = chosen16[:, 4 * b + q, e:e + 1]
                        ins = mm(bank[:, 4 + n % 4, q * P:(q + 1) * P], column.to_broadcast([P, P]),
                                 s.identity16[:, :], start=True, stop=True)
                    ins.then_inc(sem("mask_spread"), 1)

                for n in range(4):
                    spread_mask(n)
                pe.wait_ge(sem("score_ready"), 1)
                for b in range(BATCH):
                    for q in range(4):
                        ins = mm(bank[:, b, q * P:(q + 1) * P], score[:, 4 * b + q, :].to_broadcast([P, P]),
                                 s.identity[:, :], start=True, stop=True)
                    ins.then_inc(sem("score_spread"), 1)
                for n in range(4, 2 * EXPERTS):
                    spread_mask(n)
                pe.wait_ge(sem("moe_shared_loaded"), 48)
                pe.wait_ge(sem("mask_ready"), 2 * EXPERTS)
                pe.wait_ge(sem("scored_ready"), 2)

                def unit(n):
                    kind, b, j = UNITS[n]
                    if n >= 3:
                        pe.wait_ge(sem("inner_ready"), n - 2)
                    for slot, name, shared, routed in ((2, "gate_done", sh_gate, rt_gate),
                                                       (3, "up_done", sh_up, rt_up)):
                        out = bank[:, slot + 2 * (n % 3), :]
                        at = slice(j * P, (j + 1) * P)
                        if kind == 0:
                            ins = mm(out, shared[:, at], xn[:, b, :], start=True, stop=True)
                        else:
                            for e in range(EXPERTS):
                                if n == 4 + 2 * b and name == "gate_done":
                                    pe.wait_ge(sem("routed_x_ready"), 2 * e + b + 1)
                                ins = mm(out, routed[:, e, at], routed_x[:, e, b, :], start=e == 0,
                                         stop=e == EXPERTS - 1)
                        ins.then_inc(sem(name), 1)

                for n in range(4):
                    unit(n)
                pe.wait_ge(sem("moe_routed_loaded"), 48)
                for n in range(4, 8):
                    unit(n)
                for b in range(BATCH):
                    for j in range(I):
                        pe.wait_ge(sem("inner_ready"), 4)
                        mm(bank[:, b, :], sh_down[:, j, :], inner[:, 0, j, b, :], start=j == 0, stop=False
                           ).then_inc(sem("routed_up"), 1)
                for b in range(BATCH):
                    for j in range(I):
                        for e in range(EXPERTS):
                            pe.wait_ge(sem(("dve_masked", "pool_masked")[j]), EXPERTS * b + e + 1)
                            ins = mm(bank[:, b, :], rt_down[:, e, j, :], masked_inner(j, e, b), start=False,
                                     stop=j == I - 1 and e == EXPERTS - 1)
                    ins.then_inc(sem("moe_out"), 1)


def stage_output(s, out):
    nc = s.nc
    with ExitStack() as ctx:
        rows = ctx.enter_context(nc.sbuf_tensor("out_rows", [P, TILES, P], F32))
        with nc.Block() as block:
            @block.tensor
            def _(pe):
                for n in range(TILES):
                    nc.tensor.transpose(s.bank[:, n // 2, (n % 2) * P:(n % 2 + 1) * P],
                                        s.x[:, n // 4, (n % 4) * P:(n % 4 + 1) * P], s.identity[:, :]
                                        ).then_inc(s.sem("out_transposed"), 1)

            @block.scalar
            def _(act):
                for b in range(BATCH):
                    act.wait_ge(s.sem("out_transposed"), 4 * b + 4)
                    nc.scalar.activation(rows[:, 4 * b:4 * b + 4, :].rearrange("p (k n) d -> p k (n d)", n=2),
                                         s.bank[:, 2 * b:2 * b + 2, 0:2 * P], ACT.Copy
                                         ).then_inc(s.sem("out_rows_ready"), 1)

            @block.sync
            def _(sp):
                for b in range(BATCH):
                    sp.wait_ge(s.sem("out_rows_ready"), b + 1)
                    sp.dma_start(out[b].rearrange("(n p) d -> p n d", p=P), rows[:, 4 * b:4 * b + 4, :]
                                 ).then_inc(s.sem("stored"), 16)
                sp.wait_ge(s.sem("stored"), 32)


def build(nc, i, out):
    with ExitStack() as ctx:
        s = Shared(nc, ctx)

        def sb(name, shape, dt=F32):
            return ctx.enter_context(nc.sbuf_tensor(name, shape, dt))

        s.bank = ctx.enter_context(nc.psum_tensor("bank", [P, 8, 512], F32))
        s.x = sb("residual", [P, BATCH, SEQ])
        s.identity = sb("identity", [P, P])
        s.identity16 = sb("identity16", [P, P], BF16)
        s.mean_weights = sb("mean_weights", [P, P])
        s.ln_eps = sb("ln_eps", [P, 1])
        s.rms_eps = sb("rms_eps", [P, 1])
        s.centered = sb("centered", [P, 2, SEQ])
        s.squared = sb("squared", [P, 2, SEQ])
        s.deviation = sb("deviation", [P, 2, SEQ])
        s.ctx_t = sb("ctx_t", [P, BATCH * CTX])
        stage_recurrence(s, i)
        s.end_stage()
        stage_cross_attention0(s, i)
        s.end_stage()
        stage_ternary_ffn(s, i)
        stage_delta_rule(s, i)
        stage_cross_attention1(s, i)
        stage_experts(s, i)
        stage_output(s, out)


def kernel(**inputs):
    import numpy as _np
    import concourse.bacc as _bacc
    from concourse import mybir as _mybir
    from concourse.bass_utils import run_bass_kernel_spmd as _run

    nc = _bacc.Bacc("TRN2", target_bir_lowering=False, num_devices=1)
    arrays, aps = {}, {}
    for name, value in inputs.items():
        a = _np.ascontiguousarray(value)
        arrays["in_" + name] = a
        aps[name] = nc.dram_tensor("in_" + name, a.shape, _mybir.dt.from_np(a.dtype), kind="ExternalInput").ap()
    out = nc.dram_tensor("out", (BATCH, SEQ, P), F32, kind="ExternalOutput").ap()
    build(nc, aps, out)
    result = _run(nc, [arrays], core_ids=[0])
    return result.results[0]["out"]
```

```python
from contextlib import ExitStack

import numpy as np
import concourse.bass as bass
from concourse import mybir

F32 = mybir.dt.float32
BF16 = mybir.dt.bfloat16
F32R = mybir.dt.float32r
I32 = mybir.dt.int32
ALU = mybir.AluOpType
ACT = mybir.ActivationFunctionType
AX = mybir.AxisListType

P = 128
BATCH, SEQ, CTX = 2, 512, 77
TOK = BATCH * SEQ
TILES = TOK // P
KEYS = SEQ + CTX
STATES = 32
HEADS0, DH0 = 16, 64
LN_EPS, RMS_EPS = 1e-5, 1e-6
ROUND = 12582912.0


class Chain:

    def __init__(self, engine, semaphore):
        self.engine, self.semaphore, self.count = engine, semaphore, 0

    def __call__(self, instruction):
        self.count += 1
        instruction.then_inc(self.semaphore, 1)
        self.engine.wait_ge(self.semaphore, self.count)


class Shared:

    def __init__(self, nc, ctx):
        self.nc, self.ctx, self.semaphores = nc, ctx, {}
        self.ln_count = self.uncentered = self.xn_count = 0
        self.dve = Chain(nc.vector, self.sem("vector_step"))
        self.act = Chain(nc.scalar, self.sem("scalar_step"))
        self.pool = Chain(nc.gpsimd, self.sem("gpsimd_step"))

    def sem(self, name):
        if name not in self.semaphores:
            self.semaphores[name] = self.nc.alloc_semaphore(name=name)
        return self.semaphores[name]

    def end_stage(self):
        own = [name for name in self.semaphores
               if not (name.startswith(("ln_", "xn_ready")) or name.endswith(("_step", "_loaded")))
               or name in ("state_step", "pair_loaded")]
        self.nc.clear_and_free_semaphores([self.semaphores.pop(name) for name in own])
        self.nc.all_engine_barrier()



def norm_mean(s, pe, k, source):
    n = source.shape[-1]
    s.nc.tensor.matmul(s.bank[:, k % 2, 0:n], s.mean_weights[:, :], source,
                       start=True, stop=True).then_inc(s.sem("ln_mean"), 1)


def norm_center(s, dve, k, source):
    n = source.shape[-1]
    dve.wait_ge(s.sem("ln_mean"), k - s.uncentered + 1)
    s.nc.vector.tensor_tensor(s.centered[:, k % 2, 0:n], source, s.bank[:, k % 2, 0:n],
                              ALU.subtract).then_inc(s.sem("ln_centered"), 1)


def norm_square(s, act, k, n):
    act.wait_ge(s.sem("ln_centered"), k - s.uncentered + 1)
    s.nc.scalar.activation(s.squared[:, k % 2, 0:n], s.centered[:, k % 2, 0:n],
                           ACT.Square).then_inc(s.sem("ln_squared"), 1)


def norm_variance(s, pe, k, n, tile=P):
    pe.wait_ge(s.sem("ln_squared"), k + 1)
    for t in range(n // tile):
        ins = s.nc.tensor.matmul(s.bank[0:tile, 2 + k % 2, t:t + 1], s.squared[:, k % 2, t * tile:(t + 1) * tile],
                                 s.mean_weights[:, 0:1], start=True, stop=True)
    ins.then_inc(s.sem("ln_variance"), 1)


def norm_deviation(s, act, k, n, eps, tile=P):
    act.wait_ge(s.sem("ln_variance"), k + 1)
    s.nc.scalar.activation(s.deviation[0:tile, k % 2, 0:n // tile], s.bank[0:tile, 2 + k % 2, 0:n // tile],
                           ACT.Sqrt, bias=eps[0:tile, :]).then_inc(s.sem("ln_deviation"), 1)


def norm_inverse(s, dve, k, n, tile=P):
    dve.wait_ge(s.sem("ln_deviation"), k + 1)
    compact = s.deviation[0:tile, k % 2, 0:n // tile]
    s.nc.vector.reciprocal(compact, compact).then_inc(s.sem("ln_inverse"), 1)


def norm_rows(s, pe, k, n, tile=P):
    pe.wait_ge(s.sem("ln_inverse"), k + 1)
    for t in range(n // tile):
        ins = s.nc.tensor.matmul(s.bank[:, 2 + k % 2, t * tile:(t + 1) * tile],
                                 s.deviation[0:tile, k % 2, t:t + 1].to_broadcast([tile, P]),
                                 s.identity[0:tile, 0:tile], start=True, stop=True)
    ins.then_inc(s.sem("ln_rows"), 1)


def norm_apply(s, dve, k, n, target, gain=None, source=None):
    dve.wait_ge(s.sem("ln_rows"), k + 1)
    source = s.centered[:, k % 2, 0:n] if source is None else source
    if gain is None:
        return s.nc.vector.tensor_tensor(target, source, s.bank[:, 2 + k % 2, 0:n], ALU.mult)
    return s.nc.vector.scalar_tensor_tensor(target, source, gain, s.bank[:, 2 + k % 2, 0:n],
                                            ALU.mult, ALU.mult)



def allocate_weights(s, sb):
    s.ctx_rows, s.x0_gains = sb("ctx_rows", [CTX, BATCH, P]), sb("x0_gains", [P, 4])
    s.ffn_w1, s.ffn_w2 = sb("ffn_w1", [P, 4, P]), sb("ffn_w2", [P, 4 * P])
    s.ffn_taps, s.ffn_tap_bias = sb("ffn_taps", [P, 4, 3]), sb("ffn_tap_bias", [P, 4])
    s.dr_w_rows, s.dr_wb_rows = sb("dr_w_rows", [P, 4, P]), sb("dr_wb_rows", [16, P])
    s.dr_taps, s.dr_gain = sb("dr_taps", [P, 3, 4]), sb("dr_gain", [P, 1])
    s.x1_w_rows, s.x1_bias = sb("x1_w_rows", [P, 3, P]), sb("x1_bias", [P, 3])


def load_weights(s, i, sp):
    sp.dma_start(s.ctx_rows[:, :, :], i["ctx_1024"].rearrange("b p d -> p b d")
                 ).then_inc(s.sem("ctx_loaded"), 16)
    for j, name in enumerate(("ln2_g", "ln2_b", "ln1_g", "ln1_b")):
        sp.dma_start(s.x0_gains[:, j:j + 1], i["L0_xattn_" + name].rearrange("(p o) -> p o", o=1)
                     ).then_inc(s.sem("gains_loaded"), 16)
    sp.dma_start(s.ffn_w1[:, :, :], i["L0_ffn_w1"].rearrange("(j p) d -> p j d", p=P)
                 ).then_inc(s.sem("ffn_loaded"), 16)
    sp.dma_start(s.ffn_w2[:, :], i["L0_ffn_w2"]).then_inc(s.sem("ffn_loaded"), 16)
    sp.dma_start(s.ffn_taps[:, :, :], i["L0_ffn_conv_w"].rearrange("(j p) o k -> p j (o k)", p=P)
                 ).then_inc(s.sem("ffn_loaded"), 16)
    sp.dma_start(s.ffn_tap_bias[:, :], i["L0_ffn_conv_b"].rearrange("(j p) -> p j", p=P),
                 allow_slow_non_contiguous=True).then_inc(s.sem("ffn_loaded"), 16)
    for j, name in enumerate(("Wq", "Wk", "Wv", "Wo")):
        sp.dma_start(s.dr_w_rows[:, j, :], i["L1_attn_" + name]).then_inc(s.sem("dr_loaded"), 16)
    sp.dma_start(s.dr_wb_rows[:, :], i["L1_attn_Wb"]).then_inc(s.sem("dr_loaded"), 16)
    for j, name in enumerate("qkv"):
        sp.dma_start(s.dr_taps[:, j, :], i["L1_attn_conv_" + name]).then_inc(s.sem("dr_loaded"), 16)
    for h in range(16):
        sp.dma_start(s.dr_gain[h * 8:(h + 1) * 8, :], i["L1_attn_o_norm_w"].rearrange("(p o) -> p o", o=1)
                     ).then_inc(s.sem("dr_gain_loaded"), 16)
    for j, name in enumerate("qkv"):
        sp.dma_start(s.x1_w_rows[:, j, :], i["L1_xattn_W" + name]).then_inc(s.sem("x1_loaded"), 16)
        sp.dma_start(s.x1_bias[:, j:j + 1], i["L1_xattn_b" + name].rearrange("(p o) -> p o", o=1)
                     ).then_inc(s.sem("x1_loaded"), 16)



def constants(s, block):
    nc = s.nc

    @block.gpsimd
    def _(pool):
        s.pool(nc.gpsimd.memset(s.identity[:, :], 0.0))
        s.pool(nc.gpsimd.affine_select(out=s.identity[:, :], in_=s.identity[:, :],
                                       compare_op=ALU.not_equal, fill=1.0, base=0,
                                       pattern=[[-1, P]], channel_multiplier=1))
        s.pool(nc.gpsimd.tensor_copy(s.identity16[:, :], s.identity[:, :]))
        s.pool(nc.gpsimd.memset(s.mean_weights[:, :], 1.0 / P))
        s.pool(nc.gpsimd.memset(s.ln_eps[:, :], LN_EPS))
        s.pool(nc.gpsimd.memset(s.rms_eps[:, :], RMS_EPS))



def stage_recurrence(s, i):
    nc = s.nc
    RI = 2 * STATES
    with ExitStack() as ctx:
        def sb(name, shape, dt=F32):
            return ctx.enter_context(nc.sbuf_tensor(name, shape, dt))

        x_rows = sb("x_rows", [P, TILES, P])
        b_first = sb("b_first", [P, P])
        b_second = sb("b_second", [P, P])
        b_bar = sb("b_bar", [P, P])
        b_bar_t = sb("b_bar_t", [P, P])
        c_raw = sb("c_raw", [P, 2, STATES])
        c_cos = sb("c_cos", [P, P])
        c_sin = sb("c_sin", [P, P])
        c_cos_t = sb("c_cos_t", [P, P])
        c_sin_t = sb("c_sin_t", [P, P])
        small = sb("ssm_small", [P, 48])
        power_bits = sb("power_bits", [P, 1], I32)
        series = sb("series", [P, 12, 2])
        cos_table = sb("cos_table", [P, SEQ])
        sin_table = sb("sin_table", [P, SEQ])
        turned = sb("turned", [P, SEQ])
        turned2 = sb("turned2", [P, SEQ])
        radius = sb("radius", [P, SEQ])
        state = sb("ssm_state", [P, SEQ])
        h = sb("h", [P, BATCH, SEQ])
        u = sb("u", [P, BATCH, SEQ])
        columns = {}

        def col(name):
            j = columns.setdefault(name, len(columns))
            assert j < 48
            return small[:, j:j + 1]

        LEVELS = SEQ.bit_length() - 2
        step_cos = sb("step_cos", [P, LEVELS + 1])
        step_sin = sb("step_sin", [P, LEVELS + 1])
        product = sb("step_product", [P, 2])
        loaded, vectors, matrices = s.sem("x_loaded"), s.sem("ssm_vectors"), s.sem("ssm_matrices")
        with nc.Block() as block:
            constants(s, block)

            @block.sync
            def _(sp):
                for name in ("log_step", "Lambda_re", "Lambda_im"):
                    for part in range(4):
                        sp.dma_start(col(name)[part * STATES:(part + 1) * STATES, :],
                                     i["L0_attn_" + name].rearrange("(p o) -> p o", o=1)
                                     ).then_inc(vectors, 16)
                load_weights(s, i, sp)

            @block.gpsimd
            def _(pool):
                order = (("B_re", "B_im", "B_im", "B_re"), ("B_im", "B_re", "B_re", "B_im"))
                for target, names in zip((b_first, b_second), order):
                    for part, name in enumerate(names):
                        pool.dma_start(target[part * STATES:(part + 1) * STATES, :],
                                     i["L0_attn_" + name]).then_inc(matrices, 16)
                for part, name in enumerate(("C_re", "C_im")):
                    pool.dma_start(c_raw[:, part, :], i["L0_attn_" + name]).then_inc(matrices, 16)
                for name in ("norm_weight", "D"):
                    pool.dma_start(col(name), i["L0_attn_" + name].rearrange("(p o) -> p o", o=1)
                                 ).then_inc(matrices, 16)

                def then(ins):
                    s.pool(ins)

                tt = nc.gpsimd.tensor_tensor
                pool.wait_ge(s.sem("angle_ready"), 2)
                for level in range(LEVELS):
                    at, to = slice(level, level + 1), slice(level + 1, level + 2)
                    c, sn = step_cos[:, at], step_sin[:, at]
                    then(tt(product[:, 0:1], sn, sn, ALU.mult))
                    then(tt(product[:, 1:2], c, sn, ALU.mult))
                    then(tt(step_cos[:, to], c, c, ALU.mult))
                    then(tt(step_cos[:, to], step_cos[:, to], product[:, 0:1], ALU.subtract))
                    tt(step_sin[:, to], product[:, 1:2], product[:, 1:2], ALU.add
                       ).then_inc(s.sem("angle_doubled"), 1)
                    pool.wait_ge(s.sem("angle_doubled"), level + 1)

            @block.scalar
            def _(act):
                act.dma_start(x_rows[:, :, :],
                              i["x"].rearrange("b (n p) d -> p (b n) d", p=P)).then_inc(loaded, 16)
                for b in range(BATCH):
                    for half in range(2):
                        act.wait_ge(s.sem("x_transposed"), 2 * b + half + 1)
                        nc.scalar.activation(s.x[:, b, half * 256:half * 256 + 256],
                                             s.bank[:, 4 + 2 * b + half, 0:256], ACT.Copy
                                             ).then_inc(s.sem("x_ready"), 1)
                for b in range(BATCH):
                    norm_square(s, act, b, SEQ)
                act.wait_ge(s.sem("gpsimd_step"), 6)
                for b in range(BATCH):
                    norm_deviation(s, act, b, SEQ, s.ln_eps[:, :])
                for b in range(BATCH):
                    act.wait_ge(s.sem("h_ready"), b + 1)
                    nc.scalar.activation(s.squared[:, b, :], h[:, b, :], ACT.Square
                                         ).then_inc(s.sem("ln_squared"), 1)
                for b in range(BATCH):
                    norm_deviation(s, act, 2 + b, SEQ, s.rms_eps[:, :])
                act.wait_ge(s.sem("ssm_transposed"), 3)
                for source, target in ((1, b_bar_t), (2, c_cos_t), (3, c_sin_t)):
                    ins = nc.scalar.activation(target[:, :], s.bank[:, 4 + source, 0:P], ACT.Copy)
                ins.then_inc(s.sem("ssm_weights"), 1)

            @block.vector
            def _(dve):
                v, step = nc.vector, s.dve
                for j in range(12):
                    for c in range(2):
                        fact = float(np.prod(np.arange(1.0, 2 * j + 2 - c)))
                        v.memset(series[:, j, c:c + 1], (-1.0) ** j / fact)
                sign_first, sign_second = col("sign_first"), col("sign_second")
                step(v.memset(sign_first, 1.0))
                step(v.memset(sign_second, 1.0))
                step(v.memset(sign_first[96:128, :], -1.0))
                step(v.memset(sign_second[0:32, :], -1.0))
                dve.wait_ge(vectors, 16 * 3 * 4)

                def exponential(out, source):
                    n, r, q = col("exp_n"), col("exp_r"), col("exp_q")
                    step(v.tensor_scalar(n, source, float(np.log2(np.e)), ROUND, ALU.mult, ALU.add))
                    step(v.tensor_scalar(n, n, ROUND, -126.0, ALU.subtract, ALU.max))
                    step(v.tensor_scalar(n, n, 127.0, None, ALU.min))
                    step(v.scalar_tensor_tensor(r, n, -0.693359375, source, ALU.mult, ALU.add))
                    step(v.scalar_tensor_tensor(r, n, 2.12194440e-4, r, ALU.mult, ALU.add))
                    fact = [float(np.prod(np.arange(1.0, j + 1))) for j in range(8)]
                    step(v.tensor_scalar(q, r, 1 / fact[7], 1 / fact[6], ALU.mult, ALU.add))
                    for j in range(5, -1, -1):
                        step(v.tensor_scalar(q, q, r, 1 / fact[j], ALU.mult, ALU.add))
                    step(v.tensor_scalar(power_bits[:, :], n, 127.0, float(2 ** 23), ALU.add, ALU.mult))
                    step(v.tensor_tensor(out, q, power_bits[:, :].bitcast(F32), ALU.mult))

                dt, decay, angle, rad = col("dt"), col("decay"), col("angle"), col("rad")
                exponential(dt, col("log_step"))
                step(v.tensor_tensor(decay, col("Lambda_re"), dt, ALU.mult))
                step(v.tensor_tensor(angle, col("Lambda_im"), dt, ALU.mult))
                exponential(rad, decay)
                for b in range(BATCH):
                    dve.wait_ge(s.sem("x_ready"), 2 * b + 2)
                    norm_center(s, dve, b, s.x[:, b, :])
                turns, a, a2 = col("turns"), col("a"), col("a2")
                step(v.tensor_scalar(turns, angle, float(1 / (2 * np.pi)), ROUND, ALU.mult, ALU.add))
                step(v.tensor_scalar(turns, turns, ROUND, None, ALU.subtract))
                two_pi = 2 * np.pi
                first = 6.28125
                second = float(np.float32(np.round((two_pi - first) * 2 ** 20) / 2 ** 20))
                third = two_pi - first - second
                step(v.scalar_tensor_tensor(a, turns, -first, angle, ALU.mult, ALU.add))
                step(v.scalar_tensor_tensor(a, turns, -second, a, ALU.mult, ALU.add))
                step(v.scalar_tensor_tensor(a, turns, -third, a, ALU.mult, ALU.add))
                step(v.tensor_tensor(a2, a, a, ALU.mult))
                col("sine"), col("cosine")
                j = columns["sine"]
                both = small[:, j:j + 2]
                step(v.scalar_tensor_tensor(both, series[:, 11, :], a2, series[:, 10, :], ALU.mult, ALU.add))
                for j in range(9, -1, -1):
                    step(v.scalar_tensor_tensor(both, both, a2, series[:, j, :], ALU.mult, ALU.add))
                sine, cosine = col("sine"), col("cosine")
                step(v.tensor_tensor(sine, sine, a, ALU.mult))
                v.tensor_copy(step_cos[:, 0:1], cosine).then_inc(s.sem("angle_ready"), 1)
                v.tensor_copy(step_sin[:, 0:1], sine).then_inc(s.sem("angle_ready"), 1)
                for b in range(BATCH):
                    norm_inverse(s, dve, b, SEQ)
                for b in range(BATCH):
                    norm_apply(s, dve, b, SEQ, h[:, b, :]).then_inc(s.sem("h_ready"), 1)
                re, im = col("Lambda_re"), col("Lambda_im")
                lre, lim, norm, coef_re, coef_im, t = (
                    col(n) for n in ("lre", "lim", "norm", "coef_re", "coef_im", "t"))
                v.tensor_tensor(lim, rad, sine, ALU.mult)
                v.tensor_tensor(norm, im, im, ALU.mult)
                step(v.tensor_tensor(lre, rad, cosine, ALU.mult))
                step(v.tensor_scalar(lre, lre, 1.0, None, ALU.subtract))
                step(v.scalar_tensor_tensor(norm, re, re, norm, ALU.mult, ALU.add))
                step(v.reciprocal(norm, norm))
                step(v.tensor_tensor(t, lim, im, ALU.mult))
                step(v.scalar_tensor_tensor(coef_re, lre, re, t, ALU.mult, ALU.add))
                step(v.tensor_tensor(t, lre, im, ALU.mult))
                step(v.scalar_tensor_tensor(coef_im, lim, re, t, ALU.mult, ALU.subtract))
                step(v.tensor_scalar(coef_re, coef_re, norm, sign_first, ALU.mult, ALU.mult))
                step(v.tensor_scalar(coef_im, coef_im, norm, sign_second, ALU.mult, ALU.mult))
                dve.wait_ge(matrices, 16 * 12)
                step(v.tensor_scalar(b_bar[:, :], b_first[:, :], coef_re, None, ALU.mult))
                v.scalar_tensor_tensor(b_bar[:, :], b_second[:, :], coef_im, b_bar[:, :],
                                       ALU.mult, ALU.add).then_inc(s.sem("ssm_rows"), 1)
                for part, (c, cs, ss) in enumerate(((0, 2.0, -2.0), (1, -2.0, -2.0))):
                    for b in range(BATCH):
                        at = slice(b * RI + part * STATES, b * RI + (part + 1) * STATES)
                        v.tensor_scalar(c_cos[:, at], c_raw[:, c, :], cs, None, ALU.mult
                                        ).then_inc(s.sem("ssm_rows"), 1)
                        v.tensor_scalar(c_sin[:, at], c_raw[:, 1 - c, :], ss, None, ALU.mult
                                        ).then_inc(s.sem("ssm_rows"), 1)
                step(v.memset(cos_table[:, 0:1], 1.0))
                step(v.memset(sin_table[:, 0:1], 0.0))
                step(v.memset(radius[:, :], 1.0))
                step(v.tensor_scalar(radius[:, :], radius[:, :], rad, None, ALU.mult))
                for level in range(LEVELS + 1):
                    k = 2 ** level
                    old, new = slice(0, k), slice(k, 2 * k)
                    ck, sk = step_cos[:, level:level + 1], step_sin[:, level:level + 1]
                    if level:
                        dve.wait_ge(s.sem("angle_doubled"), level)
                    v.tensor_scalar(turned[:, old], sin_table[:, old], sk, None, ALU.mult)
                    step(v.tensor_scalar(turned2[:, old], cos_table[:, old], sk, None, ALU.mult))
                    v.scalar_tensor_tensor(cos_table[:, new], cos_table[:, old], ck, turned[:, old],
                                           ALU.mult, ALU.subtract)
                    step(v.scalar_tensor_tensor(sin_table[:, new], sin_table[:, old], ck, turned2[:, old],
                                                ALU.mult, ALU.add))
                    if level == 3:
                        for b in range(BATCH):
                            norm_inverse(s, dve, 2 + b, SEQ)
                        for b in range(BATCH):
                            dve.wait_ge(s.sem("h_ready"), b + 1)
                            norm_apply(s, dve, 2 + b, SEQ, u[:, b, :], gain=col("norm_weight"),
                                       source=h[:, b, :]).then_inc(s.sem("u_ready"), 1)
                dve.wait_ge(s.sem("bu_ready"), 2)
                v.tensor_tensor(turned[:, :], cos_table[:, :], s.bank[:, 4, :], ALU.mult)
                step(v.tensor_tensor(turned2[:, :], sin_table[:, :], s.bank[:, 5, :], ALU.mult))
                step(v.tensor_tensor(turned[:, :], turned[:, :], turned2[:, :], ALU.add))
                step(v.tensor_tensor_scan(state[:, :], radius[:, :], turned[:, :], 0.0, ALU.mult, ALU.add))
                v.tensor_tensor(turned[:, :], cos_table[:, :], state[:, :], ALU.mult
                                ).then_inc(s.sem("state_turned"), 1)
                v.tensor_tensor(turned2[:, :], sin_table[:, :], state[:, :], ALU.mult
                                ).then_inc(s.sem("state_turned"), 1)
                for b in range(BATCH):
                    step(v.scalar_tensor_tensor(h[:, b, :], u[:, b, :], col("D"), h[:, b, :],
                                                ALU.mult, ALU.add))
                for b in range(BATCH):
                    step(v.tensor_tensor(h[:, b, :], h[:, b, :], s.x[:, b, :], ALU.add))
                for b in range(BATCH):
                    dve.wait_ge(s.sem("y_ready"), b + 1)
                    step(v.tensor_tensor(s.x[:, b, :], h[:, b, :], s.bank[:, 6 + b, :], ALU.add))

            @block.tensor
            def _(pe):
                pe.wait_ge(loaded, 16)
                pe.wait_ge(s.sem("gpsimd_step"), 6)
                for n in range(TILES):
                    ins = nc.tensor.transpose(s.bank[:, 4 + n // 2, (n % 2) * P:(n % 2 + 1) * P],
                                              x_rows[:, n, :], s.identity[:, :])
                    if n % 2:
                        ins.then_inc(s.sem("x_transposed"), 1)
                for b in range(BATCH):
                    pe.wait_ge(s.sem("x_ready"), 2 * b + 2)
                    norm_mean(s, pe, b, s.x[:, b, :])
                for b in range(BATCH):
                    norm_variance(s, pe, b, SEQ)
                for b in range(BATCH):
                    norm_rows(s, pe, b, SEQ)
                for b in range(BATCH):
                    norm_variance(s, pe, 2 + b, SEQ)
                for b in range(BATCH):
                    norm_rows(s, pe, 2 + b, SEQ)
                pe.wait_ge(s.sem("ssm_rows"), 9)
                for slot, source in ((5, b_bar), (6, c_cos), (7, c_sin)):
                    nc.tensor.transpose(s.bank[:, slot, 0:P], source[:, :], s.identity[:, :]
                                        ).then_inc(s.sem("ssm_transposed"), 1)
                pe.wait_ge(s.sem("ssm_weights"), 1)
                for b in range(BATCH):
                    pe.wait_ge(s.sem("u_ready"), b + 1)
                    at = slice(b * RI, (b + 1) * RI)
                    nc.tensor.matmul(s.bank[at, 4, :], b_bar_t[:, 0:RI], u[:, b, :], start=True, stop=True)
                    nc.tensor.matmul(s.bank[at, 5, :], b_bar_t[:, RI:P], u[:, b, :], start=True, stop=True
                                     ).then_inc(s.sem("bu_ready"), 1)
                pe.wait_ge(s.sem("state_turned"), 2)
                for b in range(BATCH):
                    at = slice(b * RI, (b + 1) * RI)
                    nc.tensor.matmul(s.bank[:, 6 + b, :], c_cos_t[at, :], turned[at, :], start=True, stop=False)
                    nc.tensor.matmul(s.bank[:, 6 + b, :], c_sin_t[at, :], turned2[at, :], start=False, stop=True
                                     ).then_inc(s.sem("y_ready"), 1)
        s.ln_count = 4
        s.uncentered = 2



def stage_cross_attention0(s, i):
    nc = s.nc
    PAIRS = HEADS0 // 2
    UNITS = HEADS0 * BATCH
    QT = SEQ // P
    KT = -(-KEYS // P)
    widths = [min(P, KEYS - kt * P) for kt in range(KT)]
    TAIL = widths[-1]
    SCALE = float(1.0 / np.sqrt(np.sqrt(DH0)))
    A, B, MAX, SCORE, OUT = 0, 1, 2, 4, 6
    ROW = 96
    with ExitStack() as ctx:
        def sb(name, shape, dt=F32):
            return ctx.enter_context(nc.sbuf_tensor(name, shape, dt))

        ctx_rows, gains = s.ctx_rows, s.x0_gains
        h = sb("x0_h", [P, BATCH, SEQ])
        kv = sb("kv_in", [P, BATCH, KEYS])
        wq, wk, wv = (sb(n, [P, P]) for n in ("wq_slot", "wk_slot", "wv_slot"))
        wo = sb("wo0", [P, PAIRS, P])
        q_high2 = sb("q_high2", [P, BATCH, 2, SEQ], F32R)
        q_low = sb("q_low", [DH0 + 1, BATCH, 2, SEQ], F32R)
        k_both = sb("k_both", [P, BATCH, 2, KEYS], F32R)
        k_high = sb("k_high", [DH0 + 1, BATCH, 2, KEYS], F32R)
        queries16 = sb("queries16", [DH0, BATCH, 2, SEQ], BF16)
        keys16 = sb("keys16", [DH0, BATCH, 2, KEYS], BF16)
        v_high = sb("v_high", [P, BATCH, KT, 2, DH0 + 1], F32R)
        v_low = sb("v_low", [P, BATCH, KT, 2, DH0 + 1], F32R)
        probs = sb("probs", [P, KT, SEQ])
        p_high = sb("p_high", [P, 2, KT, SEQ], F32R)
        p_low = sb("p_low", [P, 2, KT, SEQ], F32R)
        zero = sb("zero", [DH0, 1])
        shift = sb("shift", [P, 2, QT], BF16)
        sum_rows = sb("sum_rows", [DH0 + 1, 4, SEQ])
        sums_stored = nc.dram_tensor("sums_stored", (UNITS, SEQ), F32, kind="Internal").ap()
        sums, last_sums = sb("prob_sums", [UNITS - 4, SEQ]), sb("last_sums", [4, SEQ])
        sums_high, last_high = sb("sums_high", [UNITS - 4, SEQ], F32R), sb("last_high", [4, SEQ], F32R)
        sums_low, last_low = sb("sums_low", [UNITS - 4, SEQ], F32R), sb("last_low", [4, SEQ], F32R)
        share_unit_r = sb("share_unit_r", [UNITS, PAIRS * BATCH, 2, DH0], F32R)
        attended_t = sb("attended_t", [P, PAIRS, BATCH, SEQ])
        share_unit = attended_t[0:UNITS, 0:2, :, :].rearrange("p a b n -> p (a b n)").rearrange(
            "p (g h d) -> p g h d", g=PAIRS * BATCH, h=2)
        bank, sem = s.bank, s.sem
        maxima = bank[:, MAX:MAX + 2, :].rearrange("p k n -> p (k n)")[:, 0:KEYS]
        k0 = s.ln_count
        s.ln_count += 5

        def split(u):
            return u // 2, u // 2 % 2, u % 2

        with nc.Block() as block:
            @block.sync
            def _(sp):
                sp.dma_start(wo[:, :, :], i["L0_xattn_Wo"].rearrange("(j p) n -> p j n", p=P)
                             ).then_inc(sem("wo0_loaded"), 16)

                def load(pair):
                    cols = bass.ds(pair * P, P)
                    vcols = bass.ds(pair * P + HEADS0 * DH0, P)
                    sp.dma_start(wq[:, :], i["L0_xattn_Wq"][:, cols]).then_inc(sem("pair_loaded"), 16)
                    sp.dma_start(wk[:, :], i["L0_xattn_Wkv"][:, cols]).then_inc(sem("pair_loaded"), 16)
                    sp.dma_start(wv[:, :], i["L0_xattn_Wkv"][:, vcols]).then_inc(sem("pair_loaded"), 16)

                def gather(pair, u):
                    w = 4 * pair + u
                    sp.wait_ge(sem("sum_kept"), w + 1)
                    to = slice(w, w + 1) if isinstance(pair, int) else bass.ds(w, 1)
                    sp.dma_start(sums_stored[to, :], sum_rows[DH0:DH0 + 1, u, :]
                                 ).then_inc(sem(f"sum_gathered_{u}"), 16)

                def repeat(g, b):
                    sp.wait_ge(sem("q_ready"), 2 * g + 2)
                    sp.dma_start(q_high2[DH0:P, b, :, :].bitcast(F32), q_high2[0:DH0, b, :, :].bitcast(F32)).then_inc(sem("q_copied"), 16)
                    sp.wait_ge(sem("k_ready"), 2 * g + 2)
                    sp.wait_ge(sem("k_tail_ready"), 2 * g + 2)
                    sp.dma_start(k_high[0:DH0, b, :, :].bitcast(F32), k_both[0:DH0, b, :, :].bitcast(F32)).then_inc(sem("k_copied"), 16)

                def pair_of_units(pair, first, last):
                    repeat(2 * pair + 1, 1)
                    if not first:
                        gather(pair - 1, 2)
                    if not last:
                        sp.wait_ge(sem("v_projected"), 2 * pair + 2)
                        load(pair + 1)
                    if not first:
                        gather(pair - 1, 3)
                    if not last:
                        repeat(2 * pair + 2, 0)
                    gather(pair, 0)
                    gather(pair, 1)

                load(0)
                repeat(0, 0)
                pair_of_units(0, True, False)
                with sp.Fori(1, PAIRS - 1) as pair:
                    pair_of_units(pair, False, False)
                pair_of_units(PAIRS - 1, False, True)
                for u in range(4):
                    sp.wait_ge(sem(f"sum_gathered_{u}"), 16 * (PAIRS - (1 if u >= 2 else 0)))
                sp.dma_start(sums[:, :], sums_stored[0:UNITS - 4, :]).then_inc(sem("sums_loaded"), 16)
                gather(PAIRS - 1, 2)
                gather(PAIRS - 1, 3)
                for u in range(4):
                    sp.wait_ge(sem(f"sum_gathered_{u}"), 16 * PAIRS)
                sp.wait_ge(sem("sums_loaded"), 16)
                sp.dma_start(last_sums[:, :], sums_stored[UNITS - 4:UNITS, :]).then_inc(sem("sums_loaded"), 16)

            @block.scalar
            def _(act):
                for b in range(BATCH):
                    norm_square(s, act, k0 + b, SEQ)
                for b in range(BATCH):
                    norm_deviation(s, act, k0 + b, SEQ, s.ln_eps[:, :])
                for b in range(BATCH):
                    norm_square(s, act, k0 + 2 + b, SEQ)
                for b in range(BATCH):
                    norm_deviation(s, act, k0 + 2 + b, SEQ, s.ln_eps[:, :])
                norm_square(s, act, k0 + 4, BATCH * CTX)
                norm_deviation(s, act, k0 + 4, BATCH * CTX, s.ln_eps[:, :], CTX)

                def high_part(semaphore, hh, target, source):
                    nc.scalar.activation(target, source[hh * DH0:(hh + 1) * DH0, :],
                                         ACT.Copy, scale=SCALE).then_inc(sem(semaphore), 1)

                def evacuate_q(g, b):
                    act.wait_ge(sem("q_projected"), g + 1)
                    for hh in range(2):
                        high_part("q_ready", hh, q_high2[0:DH0, b, hh, :], bank[:, A, :])

                def evacuate_k(g, b):
                    act.wait_ge(sem("k_projected"), g + 1)
                    for hh in range(2):
                        high_part("k_ready", hh, k_both[0:DH0, b, hh, 0:SEQ], bank[:, B, :])

                def evacuate_tail(g, b):
                    act.wait_ge(sem("tail_projected"), g + 1)
                    for hh in range(2):
                        high_part("k_tail_ready", hh, k_both[0:DH0, b, hh, SEQ:KEYS], bank[:, A, 0:CTX])

                def row(w, b, hh):
                    act.wait_ge(sem("shift_turned"), w + 1)
                    nc.scalar.activation(q_low[DH0:DH0 + 1, b, hh, :], bank[ROW:ROW + 1, OUT, :],
                                         ACT.Copy).then_inc(sem("shift_ready"), 1)

                def keep(w, pair, u, first):
                    _, b, hh = split(u)
                    act.wait_ge(sem("pv_done"), w + 1)
                    nc.scalar.activation(attended_t[hh * DH0:(hh + 1) * DH0, pair, b, :], bank[0:DH0, OUT + hh, :],
                                         ACT.Copy).then_inc(sem("attended_kept"), 1)
                    if not first:
                        for slot in ((0,), (1, 2, 3), (), ())[u]:
                            act.wait_ge(sem(f"sum_gathered_{slot}"), 16 * pair)
                    nc.scalar.activation(sum_rows[DH0:DH0 + 1, u, :], bank[DH0:DH0 + 1, OUT + hh, :],
                                         ACT.Copy).then_inc(sem("sum_kept"), 1)

                def unit(pair, u, first, last):
                    w = 4 * pair + u
                    gg, b, hh = split(u)
                    g = 2 * pair + gg
                    next_group = hh == 0 and not (last and b == 1)
                    for kt in range(KT):
                        if not (first and u == 0):
                            if kt < QT:
                                act.wait_ge(sem("p_low_ready"), QT * (w - 1) + kt + 1)
                            else:
                                act.wait_ge(sem("p_last_low_ready"), w)
                        act.wait_ge(sem("scored"), KT * w + kt + 1)
                        nc.scalar.activation(probs[0:widths[kt], kt, :],
                                             bank[0:widths[kt], SCORE + kt % 2, :], ACT.Exp
                                             ).then_inc(sem("probs_ready"), 1)
                        if kt == 3 and not (first and u < 2):
                            keep(w - 2, pair if u >= 2 else pair - 1, (u - 2) % 4, first)
                        if next_group and kt == 1:
                            evacuate_q(g + 1, 1 - b)
                        if next_group and kt == 2:
                            evacuate_k(g + 1, 1 - b)
                        if next_group and kt == 3:
                            evacuate_tail(g + 1, 1 - b)
                    if not (last and u == 3):
                        row(w + 1, (u + 1) // 2 % 2, 1 - hh)

                evacuate_q(0, 0)
                evacuate_k(0, 0)
                evacuate_tail(0, 0)
                row(0, 0, 0)
                for u in range(4):
                    unit(0, u, True, False)
                with act.Fori(1, PAIRS - 1) as pair:
                    for u in range(4):
                        unit(pair, u, False, False)
                for u in range(4):
                    unit(PAIRS - 1, u, False, True)
                keep(UNITS - 2, PAIRS - 1, 2, False)
                keep(UNITS - 1, PAIRS - 1, 3, False)
                for n, (high, inverse) in enumerate(((sums_high, sums), (last_high, last_sums))):
                    act.wait_ge(sem("sums_inverse"), n + 1)
                    nc.scalar.activation(high[:, :], inverse[:, :], ACT.Copy).then_inc(sem("sums_high_ready"), 1)

            @block.gpsimd
            def _(pool):
                s.pool(nc.gpsimd.memset(zero[:, :], 0.0))
                nc.gpsimd.memset(k_high[DH0:DH0 + 1, :, :, :].bitcast(F32), 1.0).then_inc(sem("x0_ones"), 1)
                pool.wait_ge(sem("x0_ones"), 1)
                nc.gpsimd.memset(v_high[:, :, :, :, DH0:DH0 + 1].bitcast(F32), 1.0).then_inc(sem("x0_ones"), 1)
                pool.wait_ge(sem("x0_ones"), 2)
                nc.gpsimd.memset(v_low[:, :, :, :, DH0:DH0 + 1].bitcast(F32), 0.0).then_inc(sem("x0_ones"), 1)
                pool.wait_ge(sem("x0_ones"), 3)
                s.pool(nc.gpsimd.memset(share_unit[:, :, :, :], 0.0))
                s.pool(nc.gpsimd.affine_select(out=share_unit[:, :, :, :], in_=share_unit[:, :, :, :],
                                               compare_op=ALU.not_equal, fill=1.0, base=0,
                                               pattern=[[-2, PAIRS * BATCH], [-1, 2], [0, DH0]],
                                               channel_multiplier=1))
                nc.gpsimd.tensor_copy(share_unit_r[:, :, :, :], share_unit[:, :, :, :]).then_inc(sem("x0_ones"), 1)

                def narrow(target, source, n):
                    nc.gpsimd.tensor_tensor(target, source.bitcast(F32),
                                            zero[:, :, None].to_broadcast([DH0, 2, n]), ALU.add
                                            ).then_inc(sem("narrowed"), 1)

                def narrow_queries(g, b):
                    pool.wait_ge(sem("q_ready"), 2 * g + 2)
                    narrow(queries16[:, b, :, :], q_high2[0:DH0, b, :, :], SEQ)

                def narrow_keys(g, b):
                    pool.wait_ge(sem("k_ready"), 2 * g + 2)
                    narrow(keys16[:, b, :, 0:SEQ], k_both[0:DH0, b, :, 0:SEQ], SEQ)
                    pool.wait_ge(sem("k_tail_ready"), 2 * g + 2)
                    narrow(keys16[:, b, :, SEQ:KEYS], k_both[0:DH0, b, :, SEQ:KEYS], CTX)

                def low_prob(w, hh, kt):
                    pool.wait_ge(sem("p_high_ready"), KT * w + kt + 1)
                    nc.gpsimd.tensor_tensor(p_low[:, hh, kt, :], probs[:, kt, :],
                                            p_high[:, hh, kt, :].bitcast(F32), ALU.subtract
                                            ).then_inc(sem("p_low_ready"), 1)

                def unit(pair, u, last):
                    gg, b, hh = split(u)
                    w, g = 4 * pair + u, 2 * pair + gg
                    next_group = hh == 0 and not (last and b == 1)
                    low_prob(w, hh, 0)
                    low_prob(w, hh, 1)
                    if next_group:
                        narrow_queries(g + 1, 1 - b)
                    low_prob(w, hh, 2)
                    if next_group:
                        narrow_keys(g + 1, 1 - b)
                    low_prob(w, hh, 3)

                narrow_queries(0, 0)
                narrow_keys(0, 0)
                with pool.Fori(0, PAIRS - 1) as pair:
                    for u in range(4):
                        unit(pair, u, False)
                for u in range(4):
                    unit(PAIRS - 1, u, True)

            @block.vector
            def _(dve):
                v, step = nc.vector, s.dve
                for b in range(BATCH):
                    norm_center(s, dve, k0 + b, s.x[:, b, :])
                for b in range(BATCH):
                    norm_inverse(s, dve, k0 + b, SEQ)
                for b in range(BATCH):
                    norm_apply(s, dve, k0 + b, SEQ, h[:, b, :]).then_inc(sem("x0_h"), 1)
                for b in range(BATCH):
                    norm_center(s, dve, k0 + 2 + b, h[:, b, :])
                for b in range(BATCH):
                    norm_inverse(s, dve, k0 + 2 + b, SEQ)
                dve.wait_ge(sem("gains_loaded"), 64)
                for b in range(BATCH):
                    step(norm_apply(s, dve, k0 + 2 + b, SEQ, kv[:, b, 0:SEQ]))
                    v.tensor_scalar(kv[:, b, 0:SEQ], kv[:, b, 0:SEQ], gains[:, 0:1], gains[:, 1:2],
                                    ALU.mult, ALU.add).then_inc(sem("kv_in_ready"), 1)
                dve.wait_ge(sem("ctx_turned"), 2)
                v.tensor_copy(s.ctx_t[:, :], bank[:, B, 0:BATCH * CTX]).then_inc(sem("ctx_ready"), 1)
                dve.wait_ge(sem("ctx_ready"), 1)
                norm_center(s, dve, k0 + 4, s.ctx_t[:, :])
                norm_inverse(s, dve, k0 + 4, BATCH * CTX, CTX)
                tail = kv[:, :, SEQ:KEYS]
                step(norm_apply(s, dve, k0 + 4, BATCH * CTX, h[:, 0, 0:BATCH * CTX]))
                v.tensor_scalar(tail, h[:, 0, 0:BATCH * CTX].rearrange("p (b n) -> p b n", b=BATCH),
                                gains[:, 2:3], gains[:, 3:4], ALU.mult, ALU.add
                                ).then_inc(sem("kv_in_ready"), 1)
                dve.wait_ge(sem("x0_ones"), 4)

                def maximum(w, hh, qt):
                    dve.wait_ge(sem("max_scored"), QT * w + qt + 1)
                    v.tensor_reduce(shift[:, hh, qt:qt + 1], maxima, AX.X, ALU.max, negate=True
                                    ).then_inc(sem("max_taken"), 1)

                def high_prob(w, hh, kt, first):
                    if kt == 0 and not first:
                        dve.wait_ge(sem("pv_done"), w - 1)
                    n = widths[kt]
                    dve.wait_ge(sem("probs_ready"), KT * w + kt + 1)
                    v.tensor_copy(p_high[0:n, hh, kt, :], probs[0:n, kt, :]).then_inc(sem("p_high_ready"), 1)
                    if kt == KT - 1:
                        dve.wait_ge(sem("p_high_ready"), KT * (w + 1))
                        v.tensor_tensor(p_low[0:n, hh, kt, :], probs[0:n, kt, :], p_high[0:n, hh, kt, :].bitcast(F32),
                                        ALU.subtract).then_inc(sem("p_last_low_ready"), 1)

                def low_part(semaphore, target, high, source):
                    v.scalar_tensor_tensor(target, source, SCALE, high.bitcast(F32), ALU.mult, ALU.subtract
                                           ).then_inc(sem(semaphore), 1)

                def q_lows(g, b):
                    dve.wait_ge(sem("q_ready"), 2 * g + 2)
                    for hh in range(2):
                        low_part("q_low_ready", q_low[0:DH0, b, hh, :], q_high2[0:DH0, b, hh, :],
                                 bank[hh * DH0:(hh + 1) * DH0, A, :])

                def k_lows(g, b):
                    dve.wait_ge(sem("k_ready"), 2 * g + 2)
                    for hh in range(2):
                        low_part("k_low_ready", k_both[DH0:P, b, hh, 0:SEQ], k_both[0:DH0, b, hh, 0:SEQ],
                                 bank[hh * DH0:(hh + 1) * DH0, B, :])

                def tail_lows(g, b):
                    dve.wait_ge(sem("k_tail_ready"), 2 * g + 2)
                    for hh in range(2):
                        low_part("k_low_ready", k_both[DH0:P, b, hh, SEQ:KEYS], k_both[0:DH0, b, hh, SEQ:KEYS],
                                 bank[hh * DH0:(hh + 1) * DH0, A, 0:CTX])

                def split_values(g, n, b, tiles, source, semaphore):
                    high, low = v_high[0:n, b, tiles, :, 0:DH0], v_low[0:n, b, tiles, :, 0:DH0]
                    high, low = (t.rearrange("p k h d -> p (k h) d") for t in (high, low))
                    source = source.rearrange("p (k d) -> p k d", d=DH0)
                    v.tensor_copy(high, source).then_inc(sem(semaphore), 1)
                    dve.wait_ge(sem(semaphore), 2 * g + 1)
                    v.tensor_tensor(low, source, high.bitcast(F32), ALU.subtract).then_inc(sem(semaphore), 1)

                def value_tail(g, b):
                    split_values(g, TAIL, b, slice(KT - 1, KT), bank[0:TAIL, A, P:2 * P], "v_tail_ready")

                def value(g, b):
                    dve.wait_ge(sem("v_projected"), g + 1)
                    split_values(g, P, b, slice(0, KT - 1), bank[:, A, :], "v_ready")

                def unit(pair, u, first, last):
                    w = 4 * pair + u
                    gg, b, hh = split(u)
                    g = 2 * pair + gg
                    next_group = not (last and b == 1)

                    def max_after(qt):
                        if not (last and u == 3):
                            maximum(w + 1, 1 - hh, qt)

                    for kt in range(2):
                        high_prob(w, hh, kt, first and u < 2)
                    max_after(0)
                    if hh == 1 and next_group:
                        value_tail(g + 1, 1 - b)
                    if hh == 0 and next_group:
                        q_lows(g + 1, 1 - b)
                    high_prob(w, hh, 2, first and u < 2)
                    max_after(1)
                    high_prob(w, hh, 3, False)
                    max_after(2)
                    max_after(3)
                    if hh == 1 and next_group:
                        value(g + 1, 1 - b)
                    if hh == 0 and next_group:
                        k_lows(g + 1, 1 - b)
                    high_prob(w, hh, 4, False)
                    if hh == 0 and next_group:
                        tail_lows(g + 1, 1 - b)

                def invert(n, inverse, high, low):
                    dve.wait_ge(sem("sums_loaded"), 16 * n + 16)
                    v.reciprocal(inverse[:, :], inverse[:, :]).then_inc(sem("sums_inverse"), 1)
                    dve.wait_ge(sem("sums_high_ready"), n + 1)
                    v.tensor_tensor(low[:, :], inverse[:, :], high[:, :].bitcast(F32), ALU.subtract
                                    ).then_inc(sem("sums_low_ready"), 1)

                def divide(n):
                    b, j = n // PAIRS, n % PAIRS
                    dve.wait_ge(sem("inverse_spread"), n + 1)
                    v.tensor_tensor(attended_t[:, j, b, :], attended_t[:, j, b, :], bank[:, MAX + n % 2, :],
                                    ALU.mult).then_inc(sem("attended_ready"), 1)

                q_lows(0, 0)
                k_lows(0, 0)
                tail_lows(0, 0)
                value_tail(0, 0)
                value(0, 0)
                for qt in range(QT):
                    maximum(0, 0, qt)
                for u in range(4):
                    unit(0, u, True, False)
                with dve.Fori(1, PAIRS - 1) as pair:
                    for u in range(4):
                        unit(pair, u, False, False)
                for u in range(4):
                    unit(PAIRS - 1, u, False, True)
                invert(0, sums, sums_high, sums_low)
                dve.wait_ge(sem("attended_kept"), UNITS)
                divide(0)
                divide(1)
                invert(1, last_sums, last_high, last_low)
                for n in range(2, BATCH * PAIRS):
                    divide(n)
                for b in range(BATCH):
                    dve.wait_ge(sem("x0_projected"), b + 1)
                    step(v.tensor_tensor(s.x[:, b, :], s.x[:, b, :], bank[:, SCORE + b, :], ALU.add))

            @block.tensor
            def _(pe):
                mm = nc.tensor.matmul
                for b in range(BATCH):
                    norm_mean(s, pe, k0 + b, s.x[:, b, :])
                for b in range(BATCH):
                    norm_variance(s, pe, k0 + b, SEQ)
                for b in range(BATCH):
                    norm_rows(s, pe, k0 + b, SEQ)
                pe.wait_ge(sem("x0_h"), 2)
                for b in range(BATCH):
                    norm_mean(s, pe, k0 + 2 + b, h[:, b, :])
                for b in range(BATCH):
                    norm_variance(s, pe, k0 + 2 + b, SEQ)
                for b in range(BATCH):
                    norm_rows(s, pe, k0 + 2 + b, SEQ)
                pe.wait_ge(sem("ctx_loaded"), 16)
                pe.wait_ge(sem("kv_in_ready"), 1)
                for b in range(BATCH):
                    nc.tensor.transpose(bank[:, B, b * CTX:(b + 1) * CTX], ctx_rows[:, b, :],
                                        s.identity[0:CTX, 0:CTX]).then_inc(sem("ctx_turned"), 1)
                pe.wait_ge(sem("ctx_ready"), 1)
                norm_mean(s, pe, k0 + 4, s.ctx_t[:, :])
                norm_variance(s, pe, k0 + 4, BATCH * CTX, CTX)
                norm_rows(s, pe, k0 + 4, BATCH * CTX, CTX)
                pe.wait_ge(sem("kv_in_ready"), 3)

                def project_q(pair, g, b):
                    pe.wait_ge(sem("pair_loaded"), 48 * pair + 48)
                    if not (isinstance(g, int) and g == 0):
                        pe.wait_ge(sem("v_ready"), 2 * g)
                    mm(bank[:, A, :], wq[:, :], kv[:, b, 0:SEQ], start=True, stop=True
                       ).then_inc(sem("q_projected"), 1)

                def project_k(g, b):
                    if not (isinstance(g, int) and g == 0):
                        pe.wait_ge(sem("k_low_ready"), 4 * g)
                    mm(bank[:, B, :], wk[:, :], kv[:, b, 0:SEQ], start=True, stop=True
                       ).then_inc(sem("k_projected"), 1)

                def project_tail(g, b):
                    pe.wait_ge(sem("q_low_ready"), 2 * g + 2)
                    mm(bank[:, A, 0:CTX], wk[:, :], kv[:, b, SEQ:KEYS], start=True, stop=True)
                    mm(bank[0:TAIL, A, P:2 * P], kv[:, b, KEYS - TAIL:KEYS], wv[:, :], start=True, stop=True
                       ).then_inc(sem("tail_projected"), 1)

                def project_v(g, b):
                    pe.wait_ge(sem("v_tail_ready"), 2 * g + 2)
                    for kt in range(KT - 1):
                        ins = mm(bank[:, A, kt * P:(kt + 1) * P], kv[:, b, kt * P:(kt + 1) * P], wv[:, :],
                                 start=True, stop=True)
                    ins.then_inc(sem("v_projected"), 1)

                def score_high(w, g, b, hh, kt, first):
                    if kt == 0:
                        pe.wait_ge(sem("k_low_ready"), 4 * g + 4)
                        pe.wait_ge(sem("q_copied"), 16 * g + 16)
                    if not (first and kt < 2):
                        pe.wait_ge(sem("probs_ready"), KT * w + kt - 1 if kt >= 2 else KT * w - kt)
                    mm(bank[0:widths[kt], SCORE + kt % 2, :], k_both[:, b, hh, kt * P:kt * P + widths[kt]],
                       q_high2[:, b, hh, :], start=True, stop=False)

                def score_low(w, g, b, hh, kt):
                    if kt == 0:
                        pe.wait_ge(sem("q_low_ready"), 2 * g + 2)
                        pe.wait_ge(sem("k_copied"), 16 * g + 16)
                        pe.wait_ge(sem("shift_ready"), w + 1)
                    mm(bank[0:widths[kt], SCORE + kt % 2, :], k_high[:, b, hh, kt * P:kt * P + widths[kt]],
                       q_low[:, b, hh, :], start=False, stop=True).then_inc(sem("scored"), 1)

                def weigh(w, g, b, hh, kt, first, parts=(0, 1, 2)):
                    if kt == 0:
                        pe.wait_ge(sem("v_ready"), 2 * g + 2)
                        pe.wait_ge(sem("v_tail_ready"), 2 * g + 2)
                        if not first:
                            pe.wait_ge(sem("sum_kept"), w - 1)
                    if kt < QT:
                        pe.wait_ge(sem("p_low_ready"), QT * w + kt + 1)
                    else:
                        pe.wait_ge(sem("p_last_low_ready"), w + 1)
                    n = widths[kt]
                    out = bank[0:DH0 + 1, OUT + hh, :]
                    factors = ((v_high, p_high), (v_high, p_low), (v_low, p_high))
                    for part in parts:
                        value, prob = factors[part]
                        ins = mm(out, value[0:n, b, kt, hh, :], prob[0:n, hh, kt, :],
                                 start=kt == 0 and part == 0, stop=kt == KT - 1 and part == 2)
                    if kt == KT - 1 and part == 2:
                        ins.then_inc(sem("pv_done"), 1)

                def score_max(w, g, b, hh, qt, first):
                    if qt == 0:
                        pe.wait_ge(sem("narrowed"), 3 * g + 3)
                    if not (first and qt == 0):
                        pe.wait_ge(sem("max_taken"), QT * w + qt)
                    lhs = queries16[:, b, hh, qt * P:(qt + 1) * P]
                    mm(maxima[:, 0:SEQ], lhs, keys16[:, b, hh, 0:SEQ], start=True, stop=True)
                    mm(maxima[:, SEQ:KEYS], lhs, keys16[:, b, hh, SEQ:KEYS], start=True, stop=True
                       ).then_inc(sem("max_scored"), 1)

                def turn_shift(w, hh):
                    pe.wait_ge(sem("max_taken"), QT * w + QT)
                    for qt in range(QT):
                        ins = mm(bank[ROW:ROW + 1, OUT, qt * P:(qt + 1) * P], shift[:, hh, qt:qt + 1],
                                 s.identity16[:, :], start=True, stop=True)
                    ins.then_inc(sem("shift_turned"), 1)

                def unit(pair, u, first, last):
                    w = 4 * pair + u
                    gg, b, hh = split(u)
                    g = 2 * pair + gg
                    before, after = (u - 1) // 2, (u + 1) // 2
                    start, ends = first and u == 0, last and u == 3
                    next_group = not (last and b == 1)

                    def weigh_before(kt, parts=(0, 1, 2)):
                        if not start:
                            weigh(w - 1, 2 * pair + before, before % 2, 1 - hh, kt, first and u <= 2, parts)

                    def max_after(qt):
                        if not ends:
                            score_max(w + 1, 2 * pair + after, after % 2, 1 - hh, qt, False)

                    def score(kt):
                        score_high(w, g, b, hh, kt, start)
                        score_low(w, g, b, hh, kt)

                    score_high(w, g, b, hh, 0, start)
                    score_high(w, g, b, hh, 1, start)
                    score_low(w, g, b, hh, 0)
                    score_low(w, g, b, hh, 1)
                    if hh == 0 and next_group:
                        project_q(pair + b, g + 1, 1 - b)
                    weigh_before(0)
                    max_after(0)
                    score(2)
                    if hh == 0 and next_group:
                        project_k(g + 1, 1 - b)
                    weigh_before(1)
                    max_after(1)
                    score(3)
                    if hh == 0 and next_group:
                        project_tail(g + 1, 1 - b)
                    weigh_before(2)
                    max_after(2)
                    if hh == 1 and next_group:
                        project_v(g + 1, 1 - b)
                    score(4)
                    max_after(3)
                    weigh_before(3)
                    weigh_before(4, (0, 1))
                    if not ends:
                        turn_shift(w + 1, 1 - hh)
                    weigh_before(4, (2,))

                project_q(0, 0, 0)
                project_k(0, 0)
                project_tail(0, 0)
                project_v(0, 0)
                for qt in range(QT):
                    score_max(0, 0, 0, 0, qt, True)
                turn_shift(0, 0)
                for u in range(4):
                    unit(0, u, True, False)
                with pe.Fori(1, PAIRS - 1) as pair:
                    for u in range(4):
                        unit(pair, u, False, False)
                for u in range(4):
                    unit(PAIRS - 1, u, False, True)
                for kt in range(KT):
                    weigh(UNITS - 1, 2 * PAIRS - 1, 1, 1, kt, False)
                pe.wait_ge(sem("wo0_loaded"), 16)
                pe.wait_ge(sem("probs_ready"), KT * UNITS)
                pe.wait_ge(sem("x0_ones"), 4)
                pe.wait_ge(sem("sums_low_ready"), 1)

                def spread_inverse(n):
                    b, j = n // PAIRS, n % PAIRS
                    if n >= 2:
                        pe.wait_ge(sem("attended_ready"), n - 1)
                    if j < PAIRS - 1:
                        rows, high, low = share_unit_r[0:UNITS - 4, BATCH * j + b, :, :], sums_high, sums_low
                    else:
                        pe.wait_ge(sem("sums_low_ready"), 2)
                        rows, high, low = share_unit_r[0:4, b, :, :], last_high, last_low
                    rows = rows.rearrange("w h d -> w (h d)")
                    mm(bank[:, MAX + n % 2, :], rows, high[:, :], start=True, stop=False)
                    mm(bank[:, MAX + n % 2, :], rows, low[:, :], start=False, stop=True
                       ).then_inc(sem("inverse_spread"), 1)

                spread_inverse(0)
                spread_inverse(1)
                for b in range(BATCH):
                    for j in range(PAIRS):
                        n = b * PAIRS + j
                        pe.wait_ge(sem("attended_ready"), n + 1)
                        if n + 2 < PAIRS * BATCH:
                            spread_inverse(n + 2)
                        ins = mm(bank[:, SCORE + b, :], wo[:, j, :], attended_t[:, j, b, :],
                                 start=j == 0, stop=j == PAIRS - 1)
                    ins.then_inc(sem("x0_projected"), 1)



def norm_all_pe(s, pe, k):
    for b in range(BATCH):
        norm_mean(s, pe, k + b, s.x[:, b, :])
    for b in range(BATCH):
        norm_variance(s, pe, k + b, SEQ)
    for b in range(BATCH):
        norm_rows(s, pe, k + b, SEQ)


def norm_all_act(s, act, k):
    for b in range(BATCH):
        norm_square(s, act, k + b, SEQ)
    for b in range(BATCH):
        norm_deviation(s, act, k + b, SEQ, s.ln_eps[:, :])


def norm_all_dve(s, dve, k, target):
    for b in range(BATCH):
        norm_center(s, dve, k + b, s.x[:, b, :])
    for b in range(BATCH):
        norm_inverse(s, dve, k + b, SEQ)
    for b in range(BATCH):
        norm_apply(s, dve, k + b, SEQ, target[:, b, :]).then_inc(s.sem("xn_ready"), 1)



def stage_ternary_ffn(s, i):
    nc = s.nc
    HIDDEN = 512
    J = HIDDEN // P
    WEIGHTS = HIDDEN * P
    with ExitStack() as ctx:
        def sb(name, shape, dt=F32):
            return ctx.enter_context(nc.sbuf_tensor(name, shape, dt))

        w1, w2, taps, tap_bias = s.ffn_w1, s.ffn_w2, s.ffn_taps, s.ffn_tap_bias
        w1_t16 = sb("w1_t16", [P, J, P], BF16)
        w2_t16 = sb("w2_t16", [P, J, P], BF16)
        ternary = sb("ternary", [P, 2, HIDDEN], BF16)
        rounded = sb("w_rounded", [P, HIDDEN])
        mass = sb("mass", [P, 2])
        share = sb("share", [P, P])
        wscale = sb("wscale", [P, 4])
        xn = sb("ffn_xn", [P, BATCH, SEQ])
        peak = sb("peak", [P, 3, TILES])
        scale = sb("token_scale", [P, BATCH, SEQ])
        unscale = sb("token_unscale", [P, BATCH, SEQ])
        q1 = sb("q1", [P, BATCH, SEQ], BF16)
        hidden = sb("hidden", [P, J, BATCH, SEQ + 2])
        conv = sb("conv", [P, J, BATCH, SEQ])
        tanh = sb("tanh", [P, J, BATCH, SEQ])
        q2 = sb("q2", [P, J, BATCH, SEQ], BF16)
        OF_TENSOR = (2, 3)
        OF_VECTOR = (0, 1)
        diagonals = sb("tap_diagonals", [P, len(OF_TENSOR), 3, P])
        bank, sem = s.bank, s.sem
        k0 = s.ln_count
        s.ln_count += 2
        xn0 = s.xn_count
        s.xn_count += 2
        with nc.Block() as block:
            @block.gpsimd
            def _(pool):
                nc.gpsimd.memset(share[:, :], 1.0 / WEIGHTS).then_inc(sem("ffn_constants"), 1)
                nc.gpsimd.memset(hidden[:, :, :, 0:1], 0.0).then_inc(sem("ffn_constants"), 1)
                nc.gpsimd.memset(hidden[:, :, :, SEQ + 1:SEQ + 2], 0.0).then_inc(sem("ffn_constants"), 1)

            @block.scalar
            def _(act):
                act.wait_ge(sem("ffn_loaded"), 64)
                for n, j in enumerate(OF_TENSOR):
                    for tap in range(3):
                        nc.scalar.activation(diagonals[:, n, tap, :], s.identity[:, :], ACT.Copy,
                                             scale=taps[:, j, tap:tap + 1]).then_inc(sem("diagonals_ready"), 1)
                norm_all_act(s, act, k0)
                for b in range(BATCH):
                    act.wait_ge(sem("unscale_rows"), b + 1)
                    nc.scalar.activation(unscale[:, b, :], bank[:, 6 + b, :], ACT.Copy,
                                         ).then_inc(sem("unscale_ready"), 1)
                for n, j in enumerate(OF_VECTOR):
                    act.wait_ge(sem("hidden_ready"), 4 + 2 * n + 2)
                    nc.scalar.activation(conv[:, j, :, :], hidden[:, j, :, 1:SEQ + 1], ACT.Identity,
                                         scale=taps[:, j, 1:2], bias=tap_bias[:, j:j + 1]
                                         ).then_inc(sem("middle_tap"), 1)
                def half_tanh(j):
                    nc.scalar.activation(tanh[:, j, :, :], conv[:, j, :, :], ACT.Tanh, scale=0.5
                                         ).then_inc(sem("tanh_ready"), 1)

                def add_bias(n, j):
                    act.wait_ge(sem("tensor_convolved"), BATCH * (n + 1))
                    nc.scalar.activation(conv[:, j, :, :], bank[:, 4 + 2 * n:6 + 2 * n, :], ACT.Identity,
                                         bias=tap_bias[:, j:j + 1]).then_inc(sem("bias_added"), 1)

                act.wait_ge(sem("convolved"), 1)
                half_tanh(0)
                add_bias(0, OF_TENSOR[0])
                act.wait_ge(sem("convolved"), 2)
                half_tanh(1)
                act.wait_ge(sem("bias_added"), 1)
                half_tanh(OF_TENSOR[0])
                add_bias(1, OF_TENSOR[1])
                act.wait_ge(sem("bias_added"), 2)
                half_tanh(OF_TENSOR[1])
                for j in range(J):
                    act.wait_ge(sem("silu_ready"), j + 1)
                    nc.scalar.activation(tanh[:, j, :, :], conv[:, j, :, :], ACT.Abs
                                         ).then_inc(sem("silu_absolute"), 1)
                for b in range(BATCH):
                    act.wait_ge(sem("unscale_rows"), 2 + b + 1)
                    nc.scalar.activation(unscale[:, b, :], bank[:, 6 + b, :], ACT.Copy,
                                         ).then_inc(sem("unscale_ready"), 1)

            @block.vector
            def _(dve):
                v, step = nc.vector, s.dve
                dve.wait_ge(sem("ffn_loaded"), 64)
                w1_flat = w1[:, :, :].rearrange("p j d -> p (j d)")
                v.tensor_reduce(mass[:, 0:1], w1_flat, AX.X, ALU.add, apply_absolute_value=True
                                ).then_inc(sem("mass_ready"), 1)
                v.tensor_reduce(mass[:, 1:2], w2[:, :], AX.X, ALU.add, apply_absolute_value=True
                                ).then_inc(sem("mass_ready"), 1)
                norm_center(s, dve, k0, s.x[:, 0, :])
                norm_center(s, dve, k0 + 1, s.x[:, 1, :])
                dve.wait_ge(sem("mass_shared"), 1)
                step(v.tensor_scalar(wscale[:, 0:2], bank[:, 4, 0:2], 1e-5, None, ALU.max))
                step(v.reciprocal(wscale[:, 2:4], wscale[:, 0:2]))
                for n, w in enumerate((w1_flat, w2[:, :])):
                    step(v.tensor_scalar(rounded[:, :], w, wscale[:, 2 + n:3 + n], ROUND, ALU.mult, ALU.add))
                    step(v.tensor_scalar(rounded[:, :], rounded[:, :], ROUND, 1.0, ALU.subtract, ALU.min))
                    v.tensor_scalar(ternary[:, n, :], rounded[:, :], -1.0, None, ALU.max
                                    ).then_inc(sem("ternary_rows"), 1)
                    dve.wait_ge(sem("ternary_rows"), n + 1)
                step(v.tensor_scalar(wscale[:, 0:1], wscale[:, 0:1], 1 / 127.0, None, ALU.mult))
                step(v.tensor_scalar(wscale[:, 1:2], wscale[:, 1:2], 0.5 / 127.0, None, ALU.mult))
                dve.wait_ge(sem("w_turned"), 2)
                step(v.tensor_copy(w1_t16[:, :, :].rearrange("p j d -> p (j d)"),
                                   bank[:, 4, 0:256].bitcast(BF16)))
                v.tensor_copy(w2_t16[:, :, :].rearrange("p j d -> p (j d)"),
                              bank[:, 5, 0:256].bitcast(BF16)).then_inc(sem("ternary_ready"), 1)
                for b in range(BATCH):
                    norm_inverse(s, dve, k0 + b, SEQ)
                for b in range(BATCH):
                    norm_apply(s, dve, k0 + b, SEQ, xn[:, b, :]).then_inc(sem("xn_ready"), 1)

                def token_scales(n, floor):
                    for b in range(BATCH):
                        dve.wait_ge(sem("peak_turned"), 2 * n + b + 1)
                        step(v.tensor_reduce(peak[:, 0, 4 * b:4 * b + 4],
                                             bank[:, 4 + b, :].rearrange("p (n d) -> p n d", d=P),
                                             AX.X, ALU.max, apply_absolute_value=True))
                    step(v.tensor_scalar(peak[:, 0, :], peak[:, 0, :], floor, None, ALU.max))
                    step(v.reciprocal(peak[:, 1, :], peak[:, 0, :]))
                    v.tensor_scalar(peak[:, 2, :], peak[:, 0, :], wscale[:, n:n + 1], None, ALU.mult
                                    ).then_inc(sem("token_scales"), 1)
                    v.tensor_scalar(peak[:, 1, :], peak[:, 1, :], 127.0, None, ALU.mult
                                    ).then_inc(sem("token_scales"), 1)

                token_scales(0, 1e-5)
                for b in range(BATCH):
                    dve.wait_ge(sem("scale_rows"), b + 1)
                    step(v.tensor_tensor(xn[:, b, :], xn[:, b, :], bank[:, 4 + b, :], ALU.mult))
                    step(v.tensor_scalar(xn[:, b, :], xn[:, b, :], ROUND, ROUND + 127.0, ALU.add, ALU.min))
                    v.tensor_scalar(q1[:, b, :], xn[:, b, :], ROUND - 128.0, ROUND, ALU.max, ALU.subtract
                                    ).then_inc(sem("q1_ready"), 1)
                dve.wait_ge(sem("ffn_constants"), 3)
                dve.wait_ge(sem("unscale_ready"), 2)
                for n, j in enumerate(OF_TENSOR + OF_VECTOR):
                    for b in range(BATCH):
                        dve.wait_ge(sem("up_projected"), 2 * n + b + 1)
                        v.tensor_tensor(hidden[:, j, b, 1:SEQ + 1], bank[:, (2 * n + b) % 4, :],
                                        unscale[:, b, :], ALU.mult).then_inc(sem("hidden_ready"), 1)
                for n, j in enumerate(OF_VECTOR):
                    dve.wait_ge(sem("middle_tap"), n + 1)
                    for tap, at in ((0, 0), (2, 2)):
                        ins = v.scalar_tensor_tensor(conv[:, j, :, :], hidden[:, j, :, at:at + SEQ],
                                                     taps[:, j, tap:tap + 1], conv[:, j, :, :],
                                                     ALU.mult, ALU.add)
                        if tap == 0:
                            step(ins)
                    ins.then_inc(sem("convolved"), 1)
                for j in range(J):
                    dve.wait_ge(sem("tanh_ready"), j + 1)
                    v.scalar_tensor_tensor(conv[:, j, :, :], tanh[:, j, :, :], 1.0, conv[:, j, :, :],
                                           ALU.add, ALU.mult).then_inc(sem("silu_ready"), 1)
                largest = tanh[:, 0, :, :]
                for j in range(1, J):
                    dve.wait_ge(sem("silu_absolute"), j + 1)
                    v.tensor_tensor(largest, largest, tanh[:, j, :, :], ALU.max).then_inc(sem("largest"), 1)
                    dve.wait_ge(sem("largest"), j)
                token_scales(1, 2e-5)
                for b in range(BATCH):
                    dve.wait_ge(sem("scale_rows"), 2 + b + 1)
                    step(v.tensor_copy(scale[:, b, :], bank[:, 4 + b, :]))
                for j in range(J):
                    step(v.tensor_tensor(conv[:, j, :, :], conv[:, j, :, :], scale[:, :, :], ALU.mult))
                    step(v.tensor_scalar(conv[:, j, :, :], conv[:, j, :, :], ROUND, ROUND + 127.0, ALU.add, ALU.min))
                    v.tensor_scalar(q2[:, j, :, :], conv[:, j, :, :], ROUND - 128.0, ROUND, ALU.max, ALU.subtract
                                    ).then_inc(sem("q2_ready"), 1)
                for b in range(BATCH):
                    dve.wait_ge(sem("down_projected"), b + 1)
                    dve.wait_ge(sem("unscale_ready"), 2 + b + 1)
                    step(v.tensor_tensor(unscale[:, b, :], unscale[:, b, :], bank[:, b, :], ALU.mult))
                    step(v.tensor_tensor(s.x[:, b, :], s.x[:, b, :], unscale[:, b, :], ALU.add))

            @block.tensor
            def _(pe):
                mm = nc.tensor.matmul
                norm_mean(s, pe, k0, s.x[:, 0, :])
                norm_mean(s, pe, k0 + 1, s.x[:, 1, :])
                pe.wait_ge(sem("ffn_constants"), 1)
                pe.wait_ge(sem("mass_ready"), 2)
                mm(bank[:, 4, 0:2], share[:, :], mass[:, :], start=True, stop=True
                   ).then_inc(sem("mass_shared"), 1)
                for b in range(BATCH):
                    norm_variance(s, pe, k0 + b, SEQ)
                pe.wait_ge(sem("ternary_rows"), 2)
                for n, slot in enumerate((4, 5)):
                    for j in range(J):
                        ins = nc.tensor.transpose(bank[:, slot, j * 64:j * 64 + 64].bitcast(BF16),
                                                  ternary[:, n, j * P:(j + 1) * P], s.identity16[:, :])
                    ins.then_inc(sem("w_turned"), 1)
                for b in range(BATCH):
                    norm_rows(s, pe, k0 + b, SEQ)
                pe.wait_ge(sem("ternary_ready"), 1)

                def peaks(n, source):
                    for b in range(BATCH):
                        for q in range(4):
                            ins = nc.tensor.transpose(bank[:, 4 + b, q * P:(q + 1) * P],
                                                      source[:, b, q * P:(q + 1) * P], s.identity[:, :])
                        ins.then_inc(sem("peak_turned"), 1)

                def rows(n):
                    pe.wait_ge(sem("token_scales"), 2 * n + 2)
                    for kind, slot, name in ((1, 4, "scale_rows"), (2, 6, "unscale_rows")):
                        for b in range(BATCH):
                            for q in range(4):
                                column = peak[:, kind, 4 * b + q:4 * b + q + 1]
                                ins = mm(bank[:, slot + b, q * P:(q + 1) * P], column.to_broadcast([P, P]),
                                         s.identity[:, :], start=True, stop=True)
                            ins.then_inc(sem(name), 1)

                pe.wait_ge(sem("xn_ready"), xn0 + 2)
                peaks(0, xn)
                rows(0)
                for n, j in enumerate(OF_TENSOR + OF_VECTOR):
                    for b in range(BATCH):
                        if n == 0:
                            pe.wait_ge(sem("q1_ready"), b + 1)
                        if n >= 2:
                            pe.wait_ge(sem("hidden_ready"), 2 * n + b - 3)
                        mm(bank[:, (2 * n + b) % 4, :], w1_t16[:, j, :], q1[:, b, :], start=True, stop=True
                           ).then_inc(sem("up_projected"), 1)
                pe.wait_ge(sem("diagonals_ready"), 3 * len(OF_TENSOR))
                pe.wait_ge(sem("q1_ready"), BATCH)
                pe.wait_ge(sem("unscale_ready"), BATCH)
                for n, j in enumerate(OF_TENSOR):
                    for b in range(BATCH):
                        for tap in range(3):
                            ins = mm(bank[:, 4 + 2 * n + b, :], diagonals[:, n, tap, :],
                                     hidden[:, j, b, tap:tap + SEQ], start=tap == 0, stop=tap == 2)
                        ins.then_inc(sem("tensor_convolved"), 1)
                pe.wait_ge(sem("largest"), J - 1)
                pe.wait_ge(sem("bias_added"), len(OF_TENSOR))
                peaks(1, tanh[:, 0, :, :])
                rows(1)
                pe.wait_ge(sem("q2_ready"), J)
                for b in range(BATCH):
                    for j in range(J):
                        ins = mm(bank[:, b, :], w2_t16[:, j, :], q2[:, j, b, :], start=j == 0, stop=j == J - 1)
                    ins.then_inc(sem("down_projected"), 1)



def stage_delta_rule(s, i):
    nc = s.nc
    HEADS, DH = 16, 8
    CHUNK = 32
    CHUNKS = SEQ // CHUNK
    INST = BATCH * CHUNKS
    STEPS = 8
    TAPS = 4
    with ExitStack() as ctx:
        def sb(name, shape, dt=F32):
            return ctx.enter_context(nc.sbuf_tensor(name, shape, dt))

        w_rows, wb_rows, taps, gain = s.dr_w_rows, s.dr_wb_rows, s.dr_taps, s.dr_gain
        w_t = sb("dr_w_t", [P, 4, P])
        wb_t = sb("dr_wb_t", [P, HEADS, 1])
        wb_wide = sb("dr_wb_wide", [P, HEADS, DH])
        half = sb("dr_half", [P, 1])
        xn = sb("dr_xn", [P, BATCH, SEQ])
        spread_r = sb("spread_r", [P, DH, HEADS, DH], F32R)
        high = sb("dr_high", [P, 2, BATCH, SEQ], F32R)
        low = sb("dr_low", [P, 2, BATCH, SEQ], F32R)
        blocks = sb("blocks", [P, 1, HEADS, DH])
        head_sum = sb("head_sum", [P, HEADS])
        head_mean = sb("head_mean", [P, HEADS])
        eye8 = sb("eye8", [P, 1, DH])
        same_row = sb("same_row", [P, DH, 1, DH])
        padded = sb("dr_padded", [P, 3, BATCH, SEQ + TAPS - 1])
        mixed = sb("dr_mixed", [P, 3, BATCH, SEQ])
        tanh = sb("dr_tanh", [P, 3, BATCH, SEQ])
        diagonals = sb("dr_tap_diagonals", [P, TAPS, P])
        spread = tanh[:, 0, :, :].rearrange("p b n -> p (b n)").rearrange("p (e h d) -> p e h d", e=DH, h=HEADS)
        root_beta = sb("root_beta", [P, BATCH, SEQ])
        lengths = sb("lengths", [P, 2, TILES, HEADS, 1])
        wide = sb("wide_lengths", [P, 2, TILES, HEADS, DH])
        values = sb("dr_values", [P, INST, CHUNK, 2])
        keys8 = sb("keys8", [P, INST, CHUNK, DH])
        queries8 = sb("queries8", [P, INST, CHUNK, DH])
        S = sb("dr_state", [P, STEPS, INST, 2, DH])
        product, update = (xn[:, b, :].rearrange("p (i k d) -> p i k d", k=2, d=DH) for b in range(BATCH))
        seen = sb("dr_seen", [P, INST, 2])
        change = sb("dr_change", [P, INST, 2, 1])
        asked = sb("dr_asked", [P, STEPS, INST, 2, DH])
        starts = sb("dr_starts", [P, INST, 1, DH])
        keys_flat = keys8[:, :, :, :].rearrange("p i c d -> p (i c d)")
        queries_flat = queries8[:, :, :, :].rearrange("p i c d -> p (i c d)")
        BODY = STEPS * INST * 2
        sums = s.bank[:, 4:8, :].rearrange("p k n -> p (k n)")
        BEFORE = CHUNK - STEPS
        tokens = sums[:, 0:BEFORE * INST * 2].rearrange("p (s i k) -> p i s k", i=INST, k=2)
        block_m = keys_flat[:, 0:INST * P].rearrange("p (i h d) -> p i h d", i=INST, h=HEADS)
        row_sums = (high[:, 0, :, :].rearrange("p b n -> p (b n)")
                    .rearrange("p (d h m) -> p d h m", d=DH, h=HEADS))
        apart_n = (keys_flat[:, INST * (P + DH):INST * (P + DH + DH * DH)]
                   .rearrange("p (d i m) -> p d i m", d=DH, i=INST))
        turned_n = keys_flat[:, INST * P:INST * (P + DH)].rearrange("p (i m) -> p i m", i=INST)
        block_start = queries_flat[:, 0:INST * P].rearrange("p (i h d) -> p i h d", i=INST, h=HEADS)
        GROUP = 4
        CONSTANTS = 14
        bank, sem = s.bank, s.sem
        k0 = s.ln_count
        s.ln_count += 2
        xn0 = s.xn_count
        s.xn_count += 2
        with nc.Block() as block:
            @block.gpsimd
            def _(pool):
                g = nc.gpsimd
                n = 0

                def then(ins):
                    nonlocal n
                    n += 1
                    ins.then_inc(sem("dr_constants"), 1)
                    pool.wait_ge(sem("dr_constants"), n)

                then(g.memset(half[:, :], 0.5))
                then(g.memset(padded[:, :, :, 0:TAPS - 1], 0.0))
                then(g.memset(values[:, :, :, 1:2], 0.0))
                then(g.memset(S[:, 0, :, 0, :], 0.0))
                then(g.memset(spread[:, :, :, :], 0.0))
                then(g.affine_select(out=spread[:, :, :, :], in_=spread[:, :, :, :], compare_op=ALU.not_equal,
                                     fill=1.0, base=0, pattern=[[-1, DH], [-DH, HEADS], [0, DH]],
                                     channel_multiplier=1))
                then(g.tensor_copy(spread_r[:, :, :, :], spread[:, :, :, :]))
                then(g.memset(blocks[:, :, :, :], 1.0))
                then(g.affine_select(out=blocks[:, 0, :, :], in_=blocks[:, 0, :, :], compare_op=ALU.is_ge, fill=0.0,
                                     base=0, pattern=[[-DH, HEADS], [0, DH]], channel_multiplier=1))
                then(g.affine_select(out=blocks[:, 0, :, :], in_=blocks[:, 0, :, :], compare_op=ALU.is_ge, fill=0.0,
                                     base=DH - 1, pattern=[[DH, HEADS], [0, DH]], channel_multiplier=-1))
                then(g.tensor_copy(head_sum[:, :], blocks[:, 0, :, 0]))
                then(g.tensor_scalar(head_mean[:, :], head_sum[:, :], 1.0 / DH, None, ALU.mult))
                then(g.memset(same_row[:, :, :, :], 0.0))
                then(g.affine_select(out=same_row[:, :, 0, :], in_=same_row[:, :, 0, :], compare_op=ALU.not_equal,
                                     fill=1.0, base=0, pattern=[[1, DH], [-1, DH]], channel_multiplier=0))
                assert n == CONSTANTS

                def ask(token, st, first):
                    if st == 0 and not first:
                        pool.wait_ge(sem("asked_summed"), token)
                    pool.wait_ge(sem("state_step"), 10 * (token + st) + 10)
                    at = slice(st, st + 1) if first else bass.ds(token + st, 1)
                    g.tensor_tensor(asked[:, st, :, :, :], S[:, (st + 1) % STEPS, :, :, :],
                                    queries8[:, :, at, :].to_broadcast([P, INST, 2, DH]),
                                    ALU.mult).then_inc(sem("asked"), 1)

                pool.wait_ge(sem("queries_spread"), 16)
                shape = [P, DH, HEADS, DH]
                g.tensor_tensor(row_sums[:, :, :, :], blocks[:, :, :, :].to_broadcast(shape),
                                same_row[:, :, :, :].to_broadcast(shape), ALU.mult
                                ).then_inc(sem("row_sums_ready"), 1)
                for st in range(STEPS):
                    ask(0, st, True)
                with pool.Fori(1, CHUNK // STEPS) as body:
                    token = STEPS * body
                    for st in range(STEPS):
                        ask(token, st, False)

            @block.scalar
            def _(act):
                a = nc.scalar.activation
                act.wait_ge(sem("w_rows_turned"), 5)
                a(w_t[:, :, :], bank[:, 4, :].rearrange("p (j d) -> p j d", d=P), ACT.Copy
                  ).then_inc(sem("dr_weights"), 1)
                a(wb_t[:, :, :], bank[:, 5, 0:HEADS].rearrange("p (h o) -> p h o", o=1), ACT.Copy
                  ).then_inc(sem("dr_weights"), 1)
                act.wait_ge(sem("dr_weights"), 2)
                a(wb_wide[:, :, :], wb_t[:, :, :].to_broadcast([P, HEADS, DH]), ACT.Copy
                  ).then_inc(sem("dr_weights"), 1)
                act.wait_ge(sem("dr_loaded"), 16 * 8)
                for tap in range(TAPS):
                    a(diagonals[:, tap, :], s.identity[:, :], ACT.Copy, scale=taps[:, 2, tap:tap + 1]
                      ).then_inc(sem("dr_diagonals"), 1)
                norm_all_act(s, act, k0)
                act.wait_ge(sem("dr_constants"), CONSTANTS)
                order = (1, 0, 2)
                for n, j in enumerate(order):
                    for b in range(BATCH):
                        act.wait_ge(sem("dr_projected"), 2 * n + b + 1)
                        a(padded[:, j, b, TAPS - 1:], bank[:, (2 * n + b) % 4, :], ACT.Copy
                          ).then_inc(sem("dr_padded"), 1)
                    if j == 2:
                        continue
                    act.wait_ge(sem("dr_padded"), 2 * n + 2)
                    a(mixed[:, j, :, :], padded[:, j, :, TAPS - 1:], ACT.Copy, scale=taps[:, j, TAPS - 1:TAPS]
                      ).then_inc(sem("last_tap"), 1)
                for b in range(BATCH):
                    act.wait_ge(sem("dr_projected"), 6 + b + 1)
                    a(root_beta[:, b, :], bank[:, 6 + b, :], ACT.Tanh, scale=0.5).then_inc(sem("beta_tanh"), 1)
                for n, j in enumerate(order[:2]):
                    act.wait_ge(sem("dr_mixed"), n + 1)
                    a(tanh[:, j, :, :], mixed[:, j, :, :], ACT.Tanh, scale=0.5).then_inc(sem("dr_tanh"), 1)
                act.wait_ge(sem("values_convolved"), BATCH)
                a(tanh[:, 2, :, :], bank[:, 2:4, :], ACT.Tanh, scale=0.5).then_inc(sem("dr_tanh"), 1)
                act.wait_ge(sem("dr_silu"), 1)
                a(tanh[:, 1, :, :], mixed[:, 1, :, :], ACT.Square).then_inc(sem("dr_squared"), 1)
                act.wait_ge(sem("dr_silu"), 2)
                a(tanh[:, 0, :, :], mixed[:, 0, :, :], ACT.Square).then_inc(sem("dr_squared"), 1)
                act.wait_ge(sem("beta_tanh"), 2)
                a(root_beta[:, :, :], root_beta[:, :, :], ACT.Sqrt, scale=0.5, bias=half[:, :]
                  ).then_inc(sem("beta_ready"), 1)
                for n in range(2):
                    act.wait_ge(sem("lengths_summed"), n + 1)
                    a(lengths[:, n, :, :, :].rearrange("p t h o -> p (t h o)"), bank[:, 4 + n, 0:TILES * HEADS],
                      ACT.Sqrt).then_inc(sem("lengths_rooted"), 1)
                    act.wait_ge(sem("lengths_inverse"), n + 1)
                    a(wide[:, n, :, :, :].rearrange("p t h d -> p (t h) d"),
                      lengths[:, n, :, :, :].rearrange("p t h o -> p (t h) o").to_broadcast([P, TILES * HEADS, DH]),
                      ACT.Copy).then_inc(sem("lengths_wide"), 1)

                def keep_spread(n, b, d):
                    m = 16 * n + DH * b + d
                    act.wait_ge(sem("spread_done"), m + 1)
                    a((keys8, queries8)[n][:, b * CHUNKS:(b + 1) * CHUNKS, :, d],
                      bank[:, m % 4, :].rearrange("p (c s) -> p c s", s=CHUNK), ACT.Copy
                      ).then_inc(sem(("keys_spread", "queries_spread")[n]), 1)

                def high_part(n, j, b):
                    act.wait_ge(sem(("keys_scaled", "queries_scaled")[n]), b + 1)
                    a(high[:, j, b, :], mixed[:, j, b, :], ACT.Copy).then_inc(sem("dr_high"), 1)

                for n, j in enumerate((1, 0)):
                    for b in range(BATCH):
                        high_part(n, j, b)
                for b in range(BATCH):
                    for d in range(0, DH, 2):
                        keep_spread(0, b, d)
                for b in range(BATCH):
                    for d in range(DH):
                        keep_spread(1, b, d)

                act.wait_ge(sem("asked_summed"), CHUNK - STEPS)
                for kind in (1, 0):
                    for b in range(BATCH):
                        a(tanh[:, kind, b, :].rearrange("p (c s) -> p c s", s=CHUNK)[:, :, 0:BEFORE],
                          tokens[:, b * CHUNKS:(b + 1) * CHUNKS, :, kind], ACT.Copy
                          ).then_inc(sem("tokens_kept"), 1)
                for b in range(BATCH):
                    act.wait_ge(sem("o_ready"), b + 1)
                    a(tanh[:, 2, b, :], mixed[:, 0, b, :], ACT.Square).then_inc(sem("o_squared"), 1)
                for b in range(BATCH):
                    act.wait_ge(sem("o_mean"), b + 1)
                    a(lengths[:, 0, 4 * b:4 * b + 4, :, :].rearrange("p t h o -> p (t h o)"),
                      bank[:, 2 + b, 0:4 * HEADS], ACT.Sqrt, bias=s.rms_eps[:, :]).then_inc(sem("o_rooted"), 1)
                for b in range(BATCH):
                    act.wait_ge(sem("o_inverse"), b + 1)
                    a(wide[:, 0, 4 * b:4 * b + 4, :, :].rearrange("p t h d -> p (t h) d"),
                      lengths[:, 0, 4 * b:4 * b + 4, :, :].rearrange("p t h o -> p (t h) o"
                                                                    ).to_broadcast([P, 4 * HEADS, DH]),
                      ACT.Copy).then_inc(sem("o_wide"), 1)

            @block.vector
            def _(dve):
                v, step = nc.vector, s.dve
                norm_all_dve(s, dve, k0, xn)
                dve.wait_ge(sem("dr_constants"), CONSTANTS)
                v.tensor_reduce(eye8[:, :, :].rearrange("p o d -> p (o d)"), spread[:, :, :, 0],
                                AX.X, ALU.add).then_inc(sem("eye_ready"), 1)
                dve.wait_ge(sem("eye_ready"), 1)
                v.tensor_copy(S[:, 0, :, 1, :], eye8[:, :, :].to_broadcast([P, INST, DH])
                              ).then_inc(sem("eye_ready"), 1)
                for n, j in enumerate((1, 0)):
                    dve.wait_ge(sem("last_tap"), n + 1)
                    for tap in range(TAPS - 1):
                        ins = v.scalar_tensor_tensor(mixed[:, j, :, :], padded[:, j, :, tap:tap + SEQ],
                                                     taps[:, j, tap:tap + 1], mixed[:, j, :, :],
                                                     ALU.mult, ALU.add)
                        if tap < TAPS - 2:
                            step(ins)
                    ins.then_inc(sem("dr_mixed"), 1)
                for n, j in enumerate((1, 0, 2)):
                    dve.wait_ge(sem("dr_tanh"), n + 1)
                    convolved = bank[:, 2:4, :] if j == 2 else mixed[:, j, :, :]
                    v.scalar_tensor_tensor(mixed[:, j, :, :], tanh[:, j, :, :], 1.0, convolved,
                                           ALU.add, ALU.mult).then_inc(sem("dr_silu"), 1)
                for n in range(2):
                    dve.wait_ge(sem("lengths_rooted"), n + 1)
                    flat = lengths[:, n, :, :, :].rearrange("p t h o -> p (t h o)")
                    step(v.tensor_scalar(flat, flat, 2e-6, None, ALU.max))
                    v.reciprocal(flat, flat).then_inc(sem("lengths_inverse"), 1)
                    if n == 0:
                        dve.wait_ge(sem("beta_ready"), 1)
                        step(v.tensor_tensor(mixed[:, 1, :, :], mixed[:, 1, :, :], root_beta[:, :, :], ALU.mult))

                def low_part(j, b, count):
                    dve.wait_ge(sem("dr_high"), count)
                    v.tensor_tensor(low[:, j, b, :], mixed[:, j, b, :], high[:, j, b, :].bitcast(F32),
                                    ALU.subtract).then_inc(sem("dr_low"), 1)

                for b in range(BATCH):
                    dve.wait_ge(sem("length_rows"), b + 1)
                    v.tensor_tensor(mixed[:, 1, b, :], mixed[:, 1, b, :], bank[:, 6 + b, :], ALU.mult
                                    ).then_inc(sem("keys_scaled"), 1)
                for b in range(BATCH):
                    low_part(1, b, b + 1)
                dve.wait_ge(sem("dr_silu"), 3)
                v.scalar_tensor_tensor(values[:, :, :, 0],
                                       mixed[:, 2, :, :].rearrange("p b (c s) -> p (b c) s", s=CHUNK), 0.5,
                                       root_beta[:, :, :].rearrange("p b (c s) -> p (b c) s", s=CHUNK),
                                       ALU.mult, ALU.mult).then_inc(sem("eye_ready"), 1)
                for b in range(BATCH):
                    dve.wait_ge(sem("length_rows"), 2 + b + 1)
                    v.scalar_tensor_tensor(mixed[:, 0, b, :], mixed[:, 0, b, :], float(DH ** -0.5),
                                           bank[:, 4 + b, :], ALU.mult, ALU.mult).then_inc(sem("queries_scaled"), 1)
                for b in range(BATCH):
                    for d in range(1, DH, 2):
                        m = DH * b + d
                        dve.wait_ge(sem("spread_done"), m + 1)
                        v.tensor_copy(keys8[:, b * CHUNKS:(b + 1) * CHUNKS, :, d],
                                      bank[:, m % 4, :].rearrange("p (c s) -> p c s", s=CHUNK)
                                      ).then_inc(sem("odd_keys_spread"), 1)
                    low_part(0, b, 2 + b + 1)
                dve.wait_ge(sem("eye_ready"), 3)
                dve.wait_ge(sem("keys_spread"), DH)
                dve.wait_ge(sem("odd_keys_spread"), DH)

                def advance(token, st, first):
                    at = slice(st, st + 1) if first else bass.ds(token + st, 1)
                    n = 10 * (token + st)
                    halves = [slice(b * CHUNKS, (b + 1) * CHUNKS) for b in range(BATCH)]
                    shape = [P, CHUNKS, 2, DH]
                    done = sem("state_step")

                    def key(h):
                        return keys8[:, h, at, :].to_broadcast(shape)

                    for b, h in enumerate(halves):
                        if st or not first:
                            dve.wait_ge(done, n + b - 1)
                        v.tensor_tensor(product[:, h, :, :], S[:, st, h, :, :], key(h), ALU.mult).then_inc(done, 1)
                    for b, h in enumerate(halves):
                        dve.wait_ge(done, n + b + 1)
                        v.tensor_reduce(seen[:, h, :], product[:, h, :, :], AX.X, ALU.add).then_inc(done, 1)
                    for b, h in enumerate(halves):
                        dve.wait_ge(done, n + b + 3)
                        v.tensor_tensor(change[:, h, :, 0], values[:, h, at, :].rearrange("p i o k -> p i (o k)"),
                                        seen[:, h, :], ALU.subtract).then_inc(done, 1)
                    for b, h in enumerate(halves):
                        dve.wait_ge(done, n + b + 5)
                        v.tensor_tensor(update[:, h, :, :], change[:, h, :, :].to_broadcast(shape), key(h),
                                        ALU.mult).then_inc(done, 1)
                    if st == 0 and not first:
                        dve.wait_ge(sem("asked"), token - STEPS // 2)
                    if st == STEPS // 2 and not first:
                        dve.wait_ge(sem("asked"), token)
                    for b, h in enumerate(halves):
                        dve.wait_ge(done, n + b + 7)
                        v.tensor_tensor(S[:, (st + 1) % STEPS, h, :, :], S[:, st, h, :, :], update[:, h, :, :],
                                        ALU.add).then_inc(done, 1)

                for st in range(STEPS):
                    advance(0, st, True)
                with dve.Fori(1, CHUNK // STEPS) as body:
                    token = STEPS * body
                    for st in range(STEPS):
                        advance(token, st, False)

                dve.wait_ge(sem("state_step"), 10 * CHUNK)
                last = S[:, 0, :, :, :]

                def build_blocks(target, rows, group, b, semaphore):
                    low, high = max(1 if rows is starts else 0, group * GROUP), (group + 1) * GROUP
                    n = slice(b * CHUNKS + low, b * CHUNKS + high)
                    source = starts[:, n, :, :] if rows is starts else last[:, n, rows:rows + 1, :]
                    shape = [P, high - low, HEADS, DH]
                    v.tensor_tensor(target[:, n, :, :], source.to_broadcast(shape),
                                    blocks[:, :, :, :].to_broadcast(shape), ALU.mult).then_inc(sem(semaphore), 1)

                shape = [P, DH, INST, DH]
                v.tensor_tensor(apart_n[:, :, :, :],
                                last[:, :, 0, :].rearrange("p i d -> p d i")[:, :, :, None].to_broadcast(shape),
                                eye8[:, :, None, :].to_broadcast(shape), ALU.mult).then_inc(sem("n_apart"), 1)

                def build_m(group, b):
                    build_blocks(block_m, 1, group, b, "chunk_blocks")

                def last_tokens(kind, b):
                    dve.wait_ge(sem("asked"), CHUNK)
                    v.tensor_reduce(tanh[:, kind, b, :].rearrange("p (c s) -> p c s", s=CHUNK)[:, :, BEFORE:],
                                    asked[:, :, b * CHUNKS:(b + 1) * CHUNKS, kind, :].rearrange("p s i d -> p i s d"),
                                    AX.X, ALU.add).then_inc(sem(("own_outputs", "carried")[kind]), 1)

                def build_starts(group, b):
                    dve.wait_ge(sem("asked"), CHUNK)
                    dve.wait_ge(sem("start_ready"), BATCH * ((group + 1) * GROUP - 1))
                    build_blocks(block_start, starts, group, b, "start_blocks")

                for group in range(2):
                    for b in range(BATCH):
                        build_m(group, b)
                dve.wait_ge(sem("n_turned"), 1)
                v.tensor_copy(turned_n[:, 0:INST - 1, :].rearrange("p i m -> p (i m)"),
                              bank[:, 2, 0:(INST - 1) * DH]).then_inc(sem("turned_n_kept"), 1)
                dve.wait_ge(sem("turned_n_kept"), 1)
                for b in range(BATCH):
                    v.tensor_copy(starts[:, b * CHUNKS + 1, 0, :], turned_n[:, b * CHUNKS, :]
                                  ).then_inc(sem("start_ready"), 1)
                between = {2: (build_m, 2, 0), 3: (build_m, 2, 1), 4: (build_m, 3, 0), 5: (build_m, 3, 1),
                           6: (build_starts, 0, 0), 7: (build_starts, 0, 1), 8: (last_tokens, 1, 0),
                           9: (last_tokens, 1, 1), 10: (build_starts, 1, 0), 11: (build_starts, 1, 1),
                           12: (build_starts, 2, 0), 13: (build_starts, 2, 1)}
                for c in range(2, CHUNKS):
                    for b in range(BATCH):
                        n = b * CHUNKS + c
                        dve.wait_ge(sem("start_summed"), BATCH * (c - 2) + b + 1)
                        v.tensor_tensor(starts[:, n, 0, :], bank[:, b, c * DH:(c + 1) * DH], turned_n[:, n - 1, :],
                                        ALU.add).then_inc(sem("start_ready"), 1)
                    if c in between:
                        work, first, second = between[c]
                        work(first, second)
                build_starts(3, 0)
                build_starts(3, 1)
                last_tokens(0, 0)
                last_tokens(0, 1)
                dve.wait_ge(sem("tokens_kept"), 2 * BATCH)
                dve.wait_ge(sem("dr_gain_loaded"), 16 * HEADS)
                for b in range(BATCH):
                    dve.wait_ge(sem("own_outputs"), b + 1)
                    dve.wait_ge(sem("carried_out"), b + 1)
                    step(v.tensor_copy(mixed[:, 0, b, 0:CHUNK], tanh[:, 0, b, 0:CHUNK]))
                    v.tensor_tensor(mixed[:, 0, b, CHUNK:], tanh[:, 0, b, CHUNK:], bank[:, 2 + b, CHUNK:], ALU.add
                                    ).then_inc(sem("o_ready"), 1)
                for b in range(BATCH):
                    dve.wait_ge(sem("o_rooted"), b + 1)
                    flat = lengths[:, 0, 4 * b:4 * b + 4, :, :].rearrange("p t h o -> p (t h o)")
                    v.reciprocal(flat, flat).then_inc(sem("o_inverse"), 1)
                for b in range(BATCH):
                    dve.wait_ge(sem("o_rows"), b + 1)
                    v.scalar_tensor_tensor(mixed[:, 0, b, :], mixed[:, 0, b, :], gain[:, 0:1], bank[:, 2 + b, :],
                                           ALU.mult, ALU.mult).then_inc(sem("o_normed"), 1)
                for b in range(BATCH):
                    dve.wait_ge(sem("dr_out"), b + 1)
                    step(v.tensor_tensor(s.x[:, b, :], s.x[:, b, :], bank[:, b, :], ALU.add))

            @block.tensor
            def _(pe):
                mm = nc.tensor.matmul
                pe.wait_ge(sem("dr_loaded"), 16 * 8)
                for j in range(4):
                    nc.tensor.transpose(bank[:, 4, j * P:(j + 1) * P], w_rows[:, j, :], s.identity[:, :]
                                        ).then_inc(sem("w_rows_turned"), 1)
                nc.tensor.transpose(bank[:, 5, 0:HEADS], wb_rows[:, :], s.identity[0:HEADS, 0:HEADS]
                                    ).then_inc(sem("w_rows_turned"), 1)
                norm_all_pe(s, pe, k0)
                pe.wait_ge(sem("dr_weights"), 3)
                pe.wait_ge(sem("xn_ready"), xn0 + 2)
                for n, j in enumerate((1, 0, 2)):
                    for b in range(BATCH):
                        if n == 2:
                            pe.wait_ge(sem("dr_padded"), b + 1)
                        mm(bank[:, (2 * n + b) % 4, :], w_t[:, j, :], xn[:, b, :], start=True, stop=True
                           ).then_inc(sem("dr_projected"), 1)
                for b in range(BATCH):
                    mm(bank[:, 6 + b, :], wb_wide[:, :, :].rearrange("p h d -> p (h d)"), xn[:, b, :],
                       start=True, stop=True).then_inc(sem("dr_projected"), 1)
                pe.wait_ge(sem("dr_diagonals"), TAPS)
                pe.wait_ge(sem("dr_padded"), 6)
                for b in range(BATCH):
                    for tap in range(TAPS):
                        ins = mm(bank[:, 2 + b, :], diagonals[:, tap, :], padded[:, 2, b, tap:tap + SEQ],
                                 start=tap == 0, stop=tap == TAPS - 1)
                    ins.then_inc(sem("values_convolved"), 1)
                pe.wait_ge(sem("dr_constants"), CONSTANTS)
                for n, j in enumerate((1, 0)):
                    pe.wait_ge(sem("dr_squared"), n + 1)
                    for tile in range(TILES):
                        ins = mm(bank[:, 4 + n, tile * HEADS:(tile + 1) * HEADS],
                                 tanh[:, j, tile // 4, (tile % 4) * P:(tile % 4 + 1) * P], head_sum[:, :],
                                 start=True, stop=True)
                    ins.then_inc(sem("lengths_summed"), 1)
                pe.wait_ge(sem("beta_tanh"), 2)
                for n in range(2):
                    pe.wait_ge(sem("lengths_wide"), n + 1)
                    if n == 1:
                        pe.wait_ge(sem("lengths_rooted"), 2)
                    for b in range(BATCH):
                        for q in range(4):
                            tile = 4 * b + q
                            ins = mm(bank[:, (6 if n == 0 else 4) + b, q * P:(q + 1) * P],
                                     wide[:, n, tile, :, :].rearrange("p h d -> p (h d)"),
                                     s.identity[:, :], start=True, stop=True)
                        ins.then_inc(sem("length_rows"), 1)
                for n, j in enumerate((1, 0)):
                    for b in range(BATCH):
                        pe.wait_ge(sem("dr_low"), 2 * n + b + 1)
                        for d in range(DH):
                            m = 16 * n + DH * b + d
                            if m < 4:
                                pe.wait_ge(sem("dr_silu"), 3)
                            elif m < 20:
                                of_vector = (m - 4) % 2 == 1
                                pe.wait_ge(sem("odd_keys_spread" if of_vector else "keys_spread"), (m - 4) // 2 + 1)
                            else:
                                pe.wait_ge(sem("queries_spread"), m - 19)
                            rows = spread_r[:, d, :, :].rearrange("p h m -> p (h m)")
                            mm(bank[:, m % 4, :], rows, high[:, j, b, :], start=True, stop=False)
                            mm(bank[:, m % 4, :], rows, low[:, j, b, :], start=False, stop=True
                               ).then_inc(sem("spread_done"), 1)
                pe.wait_ge(sem("queries_scaled"), 2)

                def total(token):
                    pe.wait_ge(sem("asked"), token + STEPS)
                    width = INST * 2
                    at = (slice(token * width, token * width + BODY) if isinstance(token, int)
                          else bass.ds(token * width, BODY))
                    for d in range(DH):
                        rhs = asked[:, :, :, :, d].rearrange("p s i k -> p (s i k)")
                        ins = mm(sums[:, at], s.identity[:, :], rhs, start=d == 0, stop=d == DH - 1)
                    ins.then_inc(sem("asked_summed"), STEPS)

                total(0)
                with pe.Fori(1, CHUNK // STEPS - 1) as body:
                    token = STEPS * body
                    total(token)
                pe.wait_ge(sem("keys_spread"), DH)
                pe.wait_ge(sem("odd_keys_spread"), DH)
                pe.wait_ge(sem("queries_spread"), 16)

                pe.wait_ge(sem("row_sums_ready"), 1)
                pe.wait_ge(sem("n_apart"), 1)
                for d in range(DH):
                    ins = mm(bank[:, 2, 0:(INST - 1) * DH], row_sums[:, d, :, :].bitcast(F32).rearrange("p h m -> p (h m)"),
                             apart_n[:, d, 0:INST - 1, :].rearrange("p i m -> p (i m)"),
                             start=d == 0, stop=d == DH - 1)
                ins.then_inc(sem("n_turned"), 1)

                def follow(group):
                    chunks = range(max(1, group * GROUP), min((group + 1) * GROUP, CHUNKS - 1))
                    pe.wait_ge(sem("chunk_blocks"), BATCH * (group + 1))
                    for c in chunks:
                        for b in range(BATCH):
                            n = b * CHUNKS + c
                            pe.wait_ge(sem("start_ready"), BATCH * (c - 1) + b + 1)
                            mm(bank[:, b, (c + 1) * DH:(c + 2) * DH],
                               block_m[:, n, :, :].rearrange("p h d -> p (h d)"), starts[:, n, 0, :],
                               start=True, stop=True).then_inc(sem("start_summed"), 1)

                def carry(b, group):
                    pe.wait_ge(sem("start_blocks"), BATCH * group + b + 1)
                    for c in range(max(1, group * GROUP), (group + 1) * GROUP):
                        n = b * CHUNKS + c
                        ins = mm(bank[:, 2 + b, c * CHUNK:(c + 1) * CHUNK],
                                 block_start[:, n, :, :].rearrange("p h d -> p (h d)"),
                                 tanh[:, 1, b, c * CHUNK:(c + 1) * CHUNK], start=True, stop=True)
                    if group == CHUNKS // GROUP - 1:
                        ins.then_inc(sem("carried_out"), 1)

                for group in range(CHUNKS // GROUP):
                    follow(group)
                pe.wait_ge(sem("carried"), BATCH)
                pe.wait_ge(sem("tokens_kept"), BATCH)
                for b in range(BATCH):
                    for group in range(CHUNKS // GROUP):
                        carry(b, group)
                for b in range(BATCH):
                    pe.wait_ge(sem("o_squared"), b + 1)
                    for q in range(4):
                        ins = mm(bank[:, 2 + b, q * HEADS:(q + 1) * HEADS], tanh[:, 2, b, q * P:(q + 1) * P],
                                 head_mean[:, :], start=True, stop=True)
                    ins.then_inc(sem("o_mean"), 1)
                for b in range(BATCH):
                    pe.wait_ge(sem("o_wide"), b + 1)
                    for q in range(4):
                        ins = mm(bank[:, 2 + b, q * P:(q + 1) * P],
                                 wide[:, 0, 4 * b + q, :, :].rearrange("p h d -> p (h d)"), s.identity[:, :],
                                 start=True, stop=True)
                    ins.then_inc(sem("o_rows"), 1)
                for b in range(BATCH):
                    pe.wait_ge(sem("o_normed"), b + 1)
                    mm(bank[:, b, :], w_t[:, 3, :], mixed[:, 0, b, :], start=True, stop=True
                       ).then_inc(sem("dr_out"), 1)



def stage_cross_attention1(s, i):
    nc = s.nc
    QT = SEQ // P
    with ExitStack() as ctx:
        def sb(name, shape, dt=F32):
            return ctx.enter_context(nc.sbuf_tensor(name, shape, dt))

        w_rows, bias = s.x1_w_rows, s.x1_bias
        w_t = sb("x1_w_t", [P, 3, P])
        xn = sb("x1_xn", [P, BATCH, SEQ])
        queries = sb("x1_queries", [P, BATCH, SEQ])
        keys = sb("x1_keys", [P, BATCH * CTX])
        values = sb("x1_values", [CTX, BATCH, P])
        shift = sb("x1_shift", [P, TILES])
        sums = sb("x1_sums", [P, TILES, 1])
        probs = sb("x1_probs", [P, TILES, CTX])
        probs_t = sb("x1_probs_t", [CTX, BATCH, SEQ])
        bank, sem = s.bank, s.sem
        k0 = s.ln_count
        s.ln_count += 2
        xn0 = s.xn_count
        s.xn_count += 2
        with nc.Block() as block:
            @block.sync
            def _(sp):
                for kind, name in enumerate(("gate", "up")):
                    sp.dma_start(s.rt_raw[:, kind, :, :], i["L1_ffn_rt_" + name].rearrange("e h i -> h e i")
                                 ).then_inc(sem("routed_loaded"), 16)
                sp.dma_start(s.rt_down[:, :, :, :], i["L1_ffn_rt_down"].rearrange("e (j p) n -> p e j n", p=P)
                             ).then_inc(sem("routed_loaded"), 16)

            @block.scalar
            def _(act):
                a = nc.scalar.activation
                act.wait_ge(sem("x1_w_turned"), 1)
                a(w_t[:, :, :].rearrange("p j d -> p (j d)"), bank[:, 4, 0:3 * P], ACT.Copy
                  ).then_inc(sem("x1_weights"), 1)
                for b in range(BATCH):
                    norm_square(s, act, k0 + b, SEQ)
                act.wait_ge(sem("x1_loaded"), 96)
                act.wait_ge(sem("x1_kv"), 1)
                a(keys[:, :], bank[:, 5, 0:BATCH * CTX], ACT.Identity, bias=bias[:, 1:2]
                  ).then_inc(sem("x1_kv_ready"), 1)
                a(values[:, :, :], bank[0:CTX, 5, 256:512].rearrange("p (b d) -> p b d", b=BATCH), ACT.Copy
                  ).then_inc(sem("x1_kv_ready"), 1)
                for b in range(BATCH):
                    norm_deviation(s, act, k0 + b, SEQ, s.ln_eps[:, :])
                for b in range(BATCH):
                    act.wait_ge(sem("x1_projected"), b + 1)
                    a(queries[:, b, :], bank[:, b, :], ACT.Identity, bias=bias[:, 0:1]
                      ).then_inc(sem("x1_queries_ready"), 1)
                for b in range(BATCH):
                    act.wait_ge(sem("x1_shift"), b + 1)
                    for q in range(QT):
                        n = QT * b + q
                        a(probs[:, n, :], bank[:, 6 + b, q * CTX:(q + 1) * CTX], ACT.Exp,
                          bias=shift[:, n:n + 1], accum_out=sums[:, n, :]).then_inc(sem("x1_exp"), 1)
                for b in range(BATCH):
                    act.wait_ge(sem("x1_probs_turned"), b + 1)
                    a(probs_t[:, b, :], bank[0:CTX, 2 + b, :], ACT.Copy).then_inc(sem("x1_probs_ready"), 1)

            @block.vector
            def _(dve):
                v, step = nc.vector, s.dve
                norm_all_dve(s, dve, k0, xn)
                for b in range(BATCH):
                    dve.wait_ge(sem("x1_scored"), b + 1)
                    v.tensor_reduce(shift[:, QT * b:QT * b + QT],
                                    bank[:, 6 + b, 0:QT * CTX].rearrange("p (q k) -> p q k", k=CTX),
                                    AX.X, ALU.max, negate=True).then_inc(sem("x1_shift"), 1)
                for b in range(BATCH):
                    mine = slice(QT * b, QT * b + QT)
                    dve.wait_ge(sem("x1_exp"), QT * b + QT)
                    step(v.reciprocal(sums[:, mine, :], sums[:, mine, :]))
                    v.tensor_tensor(probs[:, mine, :], probs[:, mine, :],
                                    sums[:, mine, :].to_broadcast([P, QT, CTX]), ALU.mult
                                    ).then_inc(sem("x1_normalized"), 1)
                for b in range(BATCH):
                    dve.wait_ge(sem("x1_out"), b + 1)
                    v.scalar_tensor_tensor(s.x[:, b, :], bank[:, b, :], bias[:, 2:3], s.x[:, b, :],
                                           ALU.add, ALU.add).then_inc(sem("x1_done"), 1)

            @block.tensor
            def _(pe):
                mm = nc.tensor.matmul
                pe.wait_ge(sem("x1_loaded"), 96)
                for j in range(3):
                    ins = nc.tensor.transpose(bank[:, 4, j * P:(j + 1) * P], w_rows[:, j, :], s.identity[:, :])
                ins.then_inc(sem("x1_w_turned"), 1)
                for b in range(BATCH):
                    norm_mean(s, pe, k0 + b, s.x[:, b, :])
                pe.wait_ge(sem("x1_weights"), 1)
                mm(bank[:, 5, 0:BATCH * CTX], w_t[:, 1, :], s.ctx_t[:, :], start=True, stop=True)
                for b in range(BATCH):
                    ins = mm(bank[0:CTX, 5, 256 + b * P:256 + (b + 1) * P], s.ctx_t[:, b * CTX:(b + 1) * CTX],
                             w_t[:, 2, :], start=True, stop=True)
                ins.then_inc(sem("x1_kv"), 1)
                for b in range(BATCH):
                    norm_variance(s, pe, k0 + b, SEQ)
                for b in range(BATCH):
                    norm_rows(s, pe, k0 + b, SEQ)
                for b in range(BATCH):
                    pe.wait_ge(sem("xn_ready"), xn0 + b + 1)
                    mm(bank[:, b, :], w_t[:, 0, :], xn[:, b, :], start=True, stop=True
                       ).then_inc(sem("x1_projected"), 1)
                pe.wait_ge(sem("x1_kv_ready"), 2)
                for b in range(BATCH):
                    pe.wait_ge(sem("x1_queries_ready"), b + 1)
                    for q in range(QT):
                        ins = mm(bank[:, 6 + b, q * CTX:(q + 1) * CTX], queries[:, b, q * P:(q + 1) * P],
                                 keys[:, b * CTX:(b + 1) * CTX], start=True, stop=True)
                    ins.then_inc(sem("x1_scored"), 1)
                for b in range(BATCH):
                    pe.wait_ge(sem("x1_normalized"), b + 1)
                    for q in range(QT):
                        ins = nc.tensor.transpose(bank[0:CTX, 2 + b, q * P:(q + 1) * P],
                                                  probs[:, QT * b + q, :], s.identity[:, :])
                    ins.then_inc(sem("x1_probs_turned"), 1)
                for b in range(BATCH):
                    pe.wait_ge(sem("x1_probs_ready"), b + 1)
                    mm(bank[:, b, :], values[:, b, :], probs_t[:, b, :], start=True, stop=True
                       ).then_inc(sem("x1_out"), 1)



def stage_experts(s, i):
    nc = s.nc
    EXPERTS, INNER = 8, 256
    I = INNER // P
    SLOTS = 4
    with ExitStack() as ctx:
        def sb(name, shape, dt=F32):
            return ctx.enter_context(nc.sbuf_tensor(name, shape, dt))

        gate_w = sb("gate_w", [P, EXPERTS])
        sh_gate = sb("sh_gate", [P, INNER])
        sh_up = sb("sh_up", [P, INNER])
        sh_down = sb("sh_down", [P, I, P])
        rt_raw, rt_down = s.rt_raw, s.rt_down
        rt_high = sb("rt_high", [P, 2, EXPERTS, INNER], F32R)
        rt_low = sb("rt_low", [P, 2, EXPERTS, INNER], F32R)
        xn = sb("moe_xn", [P, BATCH, SEQ])
        logits = sb("logits", [P, TILES, EXPERTS])
        order = sb("order", [P, 1, EXPERTS])
        top = sb("top", [P, TILES, 1])
        score = sb("score", [P, TILES, 1])
        first = sb("first", [P, TILES, 1])
        chosen = sb("chosen", [P, TILES, EXPERTS])
        chosen16 = sb("chosen16", [P, TILES, EXPERTS], BF16)
        mask = sb("expert_mask", [P, EXPERTS, BATCH, SEQ], BF16)
        scored = sb("scored_x", [P, BATCH, SEQ])
        scored_high = sb("scored_high", [P, BATCH, SEQ], F32R)
        scored_low = sb("scored_low", [P, BATCH, SEQ], F32R)
        x_high = sb("routed_x_high", [P, SLOTS, SEQ], F32R)
        x_low = sb("routed_x_low", [P, SLOTS, SEQ], F32R)
        masked = sb("masked_inner", [P, I, EXPERTS, BATCH, SEQ])
        tanh = sb("moe_tanh", [P, 2, SEQ])
        inner = (sb("shared_inner", [P, I, BATCH, SEQ]),
                 rt_raw[:, 0, :, :].rearrange("p e i -> p (e i)").rearrange("p (j b n) -> p j b n", j=I, b=BATCH))
        bank, sem = s.bank, s.sem
        k0 = s.ln_count
        s.ln_count += 2
        xn0 = s.xn_count
        s.xn_count += 2

        def unit_bank(n):
            return (2, 0, 4, 6, 2, 0, 4, 6)[n]

        UNITS = [(kind, b, j) for kind in range(2) for b in range(BATCH) for j in range(I)]

        def wait_slot(engine, k):
            last = k - SLOTS
            if last < 0:
                return
            if last == EXPERTS - 1:
                engine.wait_ge(sem("up_done"), 6)
            else:
                engine.wait_ge(sem("expert_done"), last + 1 - last // EXPERTS)

        with nc.Block() as block:
            @block.sync
            def _(sp):
                sp.dma_start(gate_w[:, :], i["L1_ffn_gate_w"]).then_inc(sem("moe_gate_loaded"), 16)
                sp.dma_start(sh_gate[:, :], i["L1_ffn_sh_gate"]).then_inc(sem("moe_shared_loaded"), 16)
                sp.dma_start(sh_up[:, :], i["L1_ffn_sh_up"]).then_inc(sem("moe_shared_loaded"), 16)
                sp.dma_start(sh_down[:, :, :], i["L1_ffn_sh_down"].rearrange("(j p) n -> p j n", p=P)
                             ).then_inc(sem("moe_shared_loaded"), 16)

            @block.gpsimd
            def _(pool):
                for e in range(EXPERTS):
                    nc.gpsimd.memset(order[:, :, e:e + 1], float(e)).then_inc(sem("order_ready"), 1)
                    pool.wait_ge(sem("order_ready"), e + 1)
                for kind in range(2):
                    pool.wait_ge(sem("rt_high_ready"), kind + 1)
                    nc.gpsimd.tensor_tensor(rt_low[:, kind, :, :], rt_raw[:, kind, :, :],
                                            rt_high[:, kind, :, :].bitcast(F32), ALU.subtract
                                            ).then_inc(sem("rt_low_ready"), 1)
                for k in range(BATCH * EXPERTS):
                    b, e = k // EXPERTS, k % EXPERTS
                    pool.wait_ge(sem("scored_low_ready"), b + 1)
                    pool.wait_ge(sem("mask_ready"), 2 * e + b + 1)
                    wait_slot(pool, k)
                    nc.gpsimd.tensor_tensor(x_low[:, k % SLOTS, :], scored_low[:, b, :].bitcast(F32),
                                            mask[:, e, b, :], ALU.mult).then_inc(sem("x_low_ready"), 1)
                for b in range(BATCH):
                    pool.wait_ge(sem("inner_ready"), 4 + 2 * b + 2)
                    for e in range(EXPERTS):
                        nc.gpsimd.tensor_tensor(masked[:, 1, e, b, :], inner[1][:, 1, b, :], mask[:, e, b, :],
                                                ALU.mult).then_inc(sem("pool_masked"), 1)

            @block.scalar
            def _(act):
                a = nc.scalar.activation
                act.wait_ge(sem("routed_loaded"), 48)

                def high_weights(kind):
                    a(rt_high[:, kind, :, :], rt_raw[:, kind, :, :], ACT.Copy).then_inc(sem("rt_high_ready"), 1)

                high_weights(0)
                norm_all_act(s, act, k0)
                high_weights(1)
                act.wait_ge(sem("top_ready"), 1)
                a(score[:, :, :], top[:, :, :], ACT.Tanh, scale=0.5).then_inc(sem("score_tanh"), 1)
                for e in range(EXPERTS):
                    for b in range(BATCH):
                        n = 2 * e + b
                        act.wait_ge(sem("mask_spread"), n + 1)
                        a(mask[:, e, b, :], bank[:, 4 + n % 4, :], ACT.Copy).then_inc(sem("mask_ready"), 1)
                for n, (kind, b, j) in enumerate(UNITS):
                    act.wait_ge(sem("gate_done"), n + 1)
                    if n >= 2:
                        act.wait_ge(sem("inner_ready"), n - 1)
                    a(tanh[:, n % 2, :], bank[:, unit_bank(n), :], ACT.Tanh, scale=0.5
                      ).then_inc(sem("moe_tanh"), 1)

            @block.vector
            def _(dve):
                v, step = nc.vector, s.dve
                norm_all_dve(s, dve, k0, xn)
                dve.wait_ge(sem("routed_logits"), 1)
                step(v.tensor_copy(logits[:, :, :], bank[:, 6, 0:TILES * EXPERTS].rearrange(
                    "p (t e) -> p t e", e=EXPERTS)))
                v.tensor_reduce(top[:, :, :].rearrange("p t o -> p (t o)"), logits[:, :, :], AX.X, ALU.max
                                ).then_inc(sem("top_ready"), 1)
                dve.wait_ge(sem("top_ready"), 1)
                dve.wait_ge(sem("order_ready"), EXPERTS)
                step(v.tensor_tensor(chosen[:, :, :], logits[:, :, :], top[:, :, :].to_broadcast([P, TILES, EXPERTS]),
                                     ALU.is_equal))
                step(v.tensor_scalar(chosen[:, :, :], chosen[:, :, :], -float(EXPERTS), float(EXPERTS),
                                     ALU.mult, ALU.add))
                step(v.tensor_tensor(chosen[:, :, :], chosen[:, :, :],
                                     order[:, :, :].to_broadcast([P, TILES, EXPERTS]), ALU.add))
                step(v.tensor_reduce(first[:, :, :].rearrange("p t o -> p (t o)"), chosen[:, :, :], AX.X, ALU.min))
                v.tensor_tensor(chosen16[:, :, :], order[:, :, :].to_broadcast([P, TILES, EXPERTS]),
                                first[:, :, :].to_broadcast([P, TILES, EXPERTS]), ALU.is_equal
                                ).then_inc(sem("chosen_ready"), 1)
                dve.wait_ge(sem("score_tanh"), 1)
                v.tensor_scalar(score[:, :, :], score[:, :, :], 0.5, 0.5, ALU.mult, ALU.add
                                ).then_inc(sem("score_ready"), 1)
                for b in range(BATCH):
                    dve.wait_ge(sem("score_spread"), b + 1)
                    v.tensor_tensor(scored[:, b, :], xn[:, b, :], bank[:, b, :], ALU.mult
                                    ).then_inc(sem("scored_ready"), 1)
                    dve.wait_ge(sem("scored_ready"), b + 1)
                for b in range(BATCH):
                    step(v.tensor_copy(scored_high[:, b, :], scored[:, b, :]))
                    v.tensor_tensor(scored_low[:, b, :], scored[:, b, :], scored_high[:, b, :].bitcast(F32),
                                    ALU.subtract).then_inc(sem("scored_low_ready"), 1)

                def high_inputs(first, last):
                    for k in range(first, last):
                        b, e = k // EXPERTS, k % EXPERTS
                        dve.wait_ge(sem("mask_ready"), 2 * e + b + 1)
                        wait_slot(dve, k)
                        v.tensor_tensor(x_high[:, k % SLOTS, :], scored_high[:, b, :].bitcast(F32), mask[:, e, b, :],
                                        ALU.mult).then_inc(sem("x_high_ready"), 1)

                def activate(n):
                    kind, b, j = UNITS[n]
                    target = inner[kind][:, j, b, :]
                    dve.wait_ge(sem("moe_tanh"), n + 1)
                    step(v.scalar_tensor_tensor(target, tanh[:, n % 2, :], 1.0, bank[:, unit_bank(n), :],
                                                ALU.add, ALU.mult))
                    dve.wait_ge(sem("up_done"), n + 1)
                    v.scalar_tensor_tensor(target, target, 0.5, bank[:, unit_bank(n) + 1, :], ALU.mult, ALU.mult
                                           ).then_inc(sem("inner_ready"), 1)

                def mask_inner(b):
                    dve.wait_ge(sem("inner_ready"), 4 + 2 * b + 1)
                    for e in range(EXPERTS):
                        v.tensor_tensor(masked[:, 0, e, b, :], inner[1][:, 0, b, :], mask[:, e, b, :], ALU.mult
                                        ).then_inc(sem("dve_masked"), 1)

                high_inputs(0, SLOTS)
                for n in range(4):
                    activate(n)
                high_inputs(SLOTS, EXPERTS + SLOTS)
                activate(4)
                activate(5)
                high_inputs(EXPERTS + SLOTS, 2 * EXPERTS)
                mask_inner(0)
                activate(6)
                activate(7)
                mask_inner(1)
                for b in range(BATCH):
                    dve.wait_ge(sem("moe_out"), b + 1)
                    step(v.tensor_tensor(s.x[:, b, :], s.x[:, b, :], bank[:, b, :], ALU.add))

            @block.tensor
            def _(pe):
                mm = nc.tensor.matmul
                norm_all_pe(s, pe, k0)
                pe.wait_ge(sem("moe_gate_loaded"), 16)
                for b in range(BATCH):
                    pe.wait_ge(sem("xn_ready"), xn0 + b + 1)
                    for q in range(4):
                        n = 4 * b + q
                        ins = mm(bank[:, 6, n * EXPERTS:(n + 1) * EXPERTS], xn[:, b, q * P:(q + 1) * P],
                                 gate_w[:, :], start=True, stop=True)
                ins.then_inc(sem("routed_logits"), 1)

                def shared_unit(n):
                    _, b, j = UNITS[n]
                    for slot, name, weights in ((0, "gate_done", sh_gate), (1, "up_done", sh_up)):
                        mm(bank[:, unit_bank(n) + slot, :], weights[:, j * P:(j + 1) * P], xn[:, b, :],
                           start=True, stop=True).then_inc(sem(name), 1)

                pe.wait_ge(sem("moe_shared_loaded"), 48)
                shared_unit(0)
                pe.wait_ge(sem("chosen_ready"), 1)

                def spread_mask(n):
                    e, b = n // 2, n % 2
                    if n >= 4:
                        pe.wait_ge(sem("mask_ready"), n - 3)
                    for q in range(4):
                        column = chosen16[:, 4 * b + q, e:e + 1]
                        ins = mm(bank[:, 4 + n % 4, q * P:(q + 1) * P], column.to_broadcast([P, P]),
                                 s.identity16[:, :], start=True, stop=True)
                    ins.then_inc(sem("mask_spread"), 1)

                for n in range(4):
                    spread_mask(n)
                pe.wait_ge(sem("score_ready"), 1)
                for b in range(BATCH):
                    for q in range(4):
                        ins = mm(bank[:, b, q * P:(q + 1) * P], score[:, 4 * b + q, :].to_broadcast([P, P]),
                                 s.identity[:, :], start=True, stop=True)
                    ins.then_inc(sem("score_spread"), 1)
                for n in range(4, 10):
                    spread_mask(n)
                pe.wait_ge(sem("scored_ready"), 2)
                shared_unit(1)
                for n in range(10, 2 * EXPERTS):
                    spread_mask(n)
                pe.wait_ge(sem("mask_ready"), 2 * EXPERTS)

                def expert(b, e):
                    k = EXPERTS * b + e
                    pe.wait_ge(sem("x_high_ready"), k + 1)
                    pe.wait_ge(sem("x_low_ready"), k + 1)
                    high, low = x_high[:, k % SLOTS, :], x_low[:, k % SLOTS, :]
                    for j in range(I):
                        for kind, name in ((0, "gate_done"), (1, "up_done")):
                            out = bank[:, unit_bank(4 + 2 * b + j) + kind, :]
                            at = slice(j * P, (j + 1) * P)
                            mm(out, rt_high[:, kind, e, at], high, start=e == 0, stop=False)
                            mm(out, rt_low[:, kind, e, at], high, start=False, stop=False)
                            ins = mm(out, rt_high[:, kind, e, at], low, start=False, stop=e == EXPERTS - 1)
                            if e == EXPERTS - 1:
                                ins.then_inc(sem(name), 1)
                    if e < EXPERTS - 1:
                        ins.then_inc(sem("expert_done"), 1)

                for n in range(2, 4):
                    shared_unit(n)
                pe.wait_ge(sem("rt_low_ready"), 2)
                for b in range(BATCH):
                    pe.wait_ge(sem("inner_ready"), 2 + 2 * b)
                    for e in range(EXPERTS):
                        expert(b, e)
                pe.wait_ge(sem("inner_ready"), 6)
                for b in range(BATCH):
                    for j in range(I):
                        mm(bank[:, b, :], sh_down[:, j, :], inner[0][:, j, b, :], start=j == 0, stop=False)
                for b in range(BATCH):
                    for j in range(I):
                        for e in range(EXPERTS):
                            pe.wait_ge(sem(("dve_masked", "pool_masked")[j]), EXPERTS * b + e + 1)
                            ins = mm(bank[:, b, :], rt_down[:, e, j, :], masked[:, j, e, b, :], start=False,
                                     stop=j == I - 1 and e == EXPERTS - 1)
                    ins.then_inc(sem("moe_out"), 1)


def stage_output(s, out):
    nc = s.nc
    with ExitStack() as ctx:
        rows = ctx.enter_context(nc.sbuf_tensor("out_rows", [P, TILES, P], F32))
        with nc.Block() as block:
            @block.tensor
            def _(pe):
                for n in range(TILES):
                    nc.tensor.transpose(s.bank[:, n // 2, (n % 2) * P:(n % 2 + 1) * P],
                                        s.x[:, n // 4, (n % 4) * P:(n % 4 + 1) * P], s.identity[:, :]
                                        ).then_inc(s.sem("out_transposed"), 1)

            @block.scalar
            def _(act):
                for b in range(BATCH):
                    act.wait_ge(s.sem("out_transposed"), 4 * b + 4)
                    nc.scalar.activation(rows[:, 4 * b:4 * b + 4, :].rearrange("p (k n) d -> p k (n d)", n=2),
                                         s.bank[:, 2 * b:2 * b + 2, 0:2 * P], ACT.Copy
                                         ).then_inc(s.sem("out_rows_ready"), 1)

            @block.sync
            def _(sp):
                for b in range(BATCH):
                    sp.wait_ge(s.sem("out_rows_ready"), b + 1)
                    sp.dma_start(out[b].rearrange("(n p) d -> p n d", p=P), rows[:, 4 * b:4 * b + 4, :]
                                 ).then_inc(s.sem("stored"), 16)
                sp.wait_ge(s.sem("stored"), 32)


def build(nc, i, out):
    with ExitStack() as ctx:
        s = Shared(nc, ctx)

        def sb(name, shape, dt=F32):
            return ctx.enter_context(nc.sbuf_tensor(name, shape, dt))

        s.bank = ctx.enter_context(nc.psum_tensor("bank", [P, 8, 512], F32))
        s.x = sb("residual", [P, BATCH, SEQ])
        s.identity = sb("identity", [P, P])
        s.identity16 = sb("identity16", [P, P], BF16)
        s.mean_weights = sb("mean_weights", [P, P])
        s.ln_eps = sb("ln_eps", [P, 1])
        s.rms_eps = sb("rms_eps", [P, 1])
        s.centered = sb("centered", [P, 2, SEQ])
        s.squared = sb("squared", [P, 2, SEQ])
        s.deviation = sb("deviation", [P, 2, SEQ // P])
        s.ctx_t = sb("ctx_t", [P, BATCH * CTX])
        allocate_weights(s, sb)
        stage_recurrence(s, i)
        s.end_stage()
        stage_cross_attention0(s, i)
        s.end_stage()
        stage_ternary_ffn(s, i)
        s.end_stage()
        stage_delta_rule(s, i)
        s.rt_raw = sb("rt_raw", [P, 2, 8, 2 * P])
        s.rt_down = sb("rt_down", [P, 8, 2, P])
        stage_cross_attention1(s, i)
        stage_experts(s, i)
        stage_output(s, out)


def kernel(**inputs):
    import numpy as _np
    import concourse.bacc as _bacc
    from concourse import mybir as _mybir
    from concourse.bass_utils import run_bass_kernel_spmd as _run

    nc = _bacc.Bacc("TRN2", target_bir_lowering=False, num_devices=1)
    arrays, aps = {}, {}
    for name, value in inputs.items():
        a = _np.ascontiguousarray(value)
        arrays["in_" + name] = a
        aps[name] = nc.dram_tensor("in_" + name, a.shape, _mybir.dt.from_np(a.dtype), kind="ExternalInput").ap()
    out = nc.dram_tensor("out", (BATCH, SEQ, P), F32, kind="ExternalOutput").ap()
    build(nc, aps, out)
    result = _run(nc, [arrays], core_ids=[0])
    return result.results[0]["out"]
```
